# Optimizing a Trainium2 kernel written in Bass

```python
import numpy as np
import jax
import jax.numpy as jnp

def _softmax(x, axis=-1):
    return jax.nn.softmax(x, axis=axis)

def _gelu(x):
    return jax.nn.gelu(x, approximate=True)

def _silu(x):
    return jax.nn.silu(x)

def _sigmoid(x):
    return jax.nn.sigmoid(x)

def _layernorm(x, axis=-1, eps=1e-05):
    m = jnp.mean(x, axis=axis, keepdims=True)
    v = jnp.var(x, axis=axis, keepdims=True)
    return (x - m) / jnp.sqrt(v + eps)

def _scatter_add(tgt, idx, src, axis=0):
    return tgt.at[idx].add(src)

def _segment_sum(src, seg, n):
    return jax.ops.segment_sum(src, seg, n)
kernel_name = 'mk_xattn_seq_d2_seqx_r4_508bf0'

def setup_inputs(seed: int=0):
    np.random.seed(seed)
    _w = jnp.asarray

    def _rec_inputs():
        import jax
        import jax.numpy as jnp
        _rk = jax.random.key(seed)
        x = -0.0002928 + 1 * jax.random.normal(jax.random.fold_in(_rk, 1), (2, 512, 256), jnp.float32)
        _lenS = 512 - jax.random.randint(jax.random.fold_in(_rk, 7), (2,), 0, max(1, 512 // 4) + 1, jnp.int32)
        _lenS2 = 1024 - jax.random.randint(jax.random.fold_in(_rk, 8), (2,), 0, max(1, 1024 // 4) + 1, jnp.int32)
        _ctx_1024P = jax.random.normal(jax.random.fold_in(_rk, 11), (2, 16, 256), jnp.float32)
        _ctx_1024c = jax.random.dirichlet(jax.random.fold_in(_rk, 511), 0.3 * jnp.ones((16,), jnp.float32), (2, 1024))
        _ctx_1024t = jnp.einsum('bsk,bkd->bsd', _ctx_1024c, _ctx_1024P)
        _ctx_1024t = _ctx_1024t * jax.lax.rsqrt(jnp.mean(jnp.square(_ctx_1024t)) + 1e-12) * 0.953939
        ctx_1024 = -1.39393e-06 + 0.999914 * (_ctx_1024t + 0.3 * jax.random.normal(jax.random.fold_in(_rk, 611), (2, 1024, 256), jnp.float32))
        return (x, ctx_1024)
    x, ctx_1024 = _rec_inputs()

    def _L0_xattn_setup():
        import jax, jax.numpy as jnp
        import numpy as np
        B, S, SE, D, H, FF, E, K = (2, 512, 512, 256, 16, 1024, 8, 2)
        HD = D // H

        def _layernorm(x, g, b):
            m = x.mean(-1, keepdims=True)
            v = ((x - m) ** 2).mean(-1, keepdims=True)
            return (x - m) / jnp.sqrt(v + 1e-05) * g + b

        def _attn(q_in, k_in, v_in, wq, bq, wk, bk, wv, bv, wo, bo, causal):
            Bq, Sq, Dm = q_in.shape
            Sk = k_in.shape[1]
            Q = (q_in @ wq + bq).reshape(Bq, Sq, H, HD)
            Kp = (k_in @ wk + bk).reshape(Bq, Sk, H, HD)
            V = (v_in @ wv + bv).reshape(Bq, Sk, H, HD)
            scores = jnp.einsum('bqhd,bkhd->bhqk', Q, Kp) / jnp.sqrt(jnp.float32(HD))
            if causal:
                mask = jnp.tril(jnp.ones((Sq, Sk), bool))
                scores = jnp.where(mask, scores, -jnp.inf)
            a = jax.nn.softmax(scores, axis=-1)
            o = jnp.einsum('bhqk,bkhd->bqhd', a, V).reshape(Bq, Sq, Dm)
            return o @ wo + bo

        def _moe(x, rw, rb, w1, b1, w2, b2):
            T = x.shape[0] * x.shape[1]
            xf = x.reshape(T, D)
            router_weights = jax.nn.softmax(xf @ rw + rb, axis=-1)
            topw, topi = jax.lax.top_k(router_weights, K)
            topw = jax.nn.softmax(topw, axis=-1)
            combine = jnp.zeros((T, E), xf.dtype).at[jnp.arange(T)[:, None], topi].add(topw)
            h = jax.nn.gelu(jnp.einsum('td,edf->etf', xf, w1) + b1[:, None, :], approximate=False)
            eo = jnp.einsum('etf,efd->etd', h, w2) + b2[:, None, :]
            out = jnp.einsum('etd,te->td', eo, combine)
            return out.reshape(x.shape)
        key = jax.random.key(seed)
        ks = jax.random.split(key, 32)
        w = lambda k, shape: jax.random.normal(k, shape, jnp.float32) * 0.02
        inp = {'x': jax.random.normal(ks[0], (B, S, D), jnp.float32), 'encoder_output': jax.random.normal(ks[1], (B, SE, D), jnp.float32), 'sa_wq': w(ks[2], (D, D)), 'sa_bq': jnp.zeros((D,), jnp.float32), 'sa_wk': w(ks[3], (D, D)), 'sa_bk': jnp.zeros((D,), jnp.float32), 'sa_wv': w(ks[4], (D, D)), 'sa_bv': jnp.zeros((D,), jnp.float32), 'sa_wo': w(ks[5], (D, D)), 'sa_bo': jnp.zeros((D,), jnp.float32), 'ca_wq': w(ks[6], (D, D)), 'ca_bq': jnp.zeros((D,), jnp.float32), 'ca_wk': w(ks[7], (D, D)), 'ca_bk': jnp.zeros((D,), jnp.float32), 'ca_wv': w(ks[8], (D, D)), 'ca_bv': jnp.zeros((D,), jnp.float32), 'ca_wo': w(ks[9], (D, D)), 'ca_bo': jnp.zeros((D,), jnp.float32), 'ln1_g': jnp.ones((D,), jnp.float32), 'ln1_b': jnp.zeros((D,), jnp.float32), 'ln2_g': jnp.ones((D,), jnp.float32), 'ln2_b': jnp.zeros((D,), jnp.float32), 'ln3_g': jnp.ones((D,), jnp.float32), 'ln3_b': jnp.zeros((D,), jnp.float32), 'router_w': w(ks[10], (D, E)), 'router_b': jnp.zeros((E,), jnp.float32), 'e_w1': w(ks[11], (E, D, FF)), 'e_b1': jnp.zeros((E, FF), jnp.float32), 'e_w2': w(ks[12], (E, FF, D)), 'e_b2': jnp.zeros((E, D), jnp.float32)}
        return inp
    _L0_xattn_all = _L0_xattn_setup()
    _L0_xattn_in = {k: v for k, v in _L0_xattn_all.items() if k in ('sa_wq', 'sa_bq', 'sa_wk', 'sa_bk', 'sa_wv', 'sa_bv', 'sa_wo', 'sa_bo', 'ca_wq', 'ca_bq', 'ca_wk', 'ca_bk', 'ca_wv', 'ca_bv', 'ca_wo', 'ca_bo', 'ln1_g', 'ln1_b', 'ln2_g', 'ln2_b', 'ln3_g', 'ln3_b', 'router_w', 'router_b', 'e_w1', 'e_b1', 'e_w2', 'e_b2')}
    del _L0_xattn_all

    def _L1_xattn_setup():
        import jax, jax.numpy as jnp
        import numpy as np
        MODEL_DIM = 256
        HEAD_SIZE = 64
        N_HEADS = MODEL_DIM // HEAD_SIZE
        HIDDEN = 4 * MODEL_DIM
        B, S = (4, 512)

        def _mha(x, ctx, wq, wk, wv, wo):
            b, s, d = x.shape
            t = ctx.shape[1]
            q = (x @ wq).reshape(b, s, N_HEADS, HEAD_SIZE)
            k = (ctx @ wk).reshape(b, t, N_HEADS, HEAD_SIZE)
            v = (ctx @ wv).reshape(b, t, N_HEADS, HEAD_SIZE)
            scores = jnp.einsum('bqhd,bkhd->bhqk', q, k) / jnp.sqrt(jnp.float32(HEAD_SIZE)).astype(x.dtype)
            attn = jax.nn.softmax(scores, axis=-1)
            out = jnp.einsum('bhqk,bkhd->bqhd', attn, v).reshape(b, s, d)
            return out @ wo

        def _swiglu(x, wg, wu, wd):
            return jax.nn.silu(x @ wg) * (x @ wu) @ wd
        key = jax.random.key(seed)
        ks = jax.random.split(key, 20)
        sc = 0.02
        d, h = (MODEL_DIM, HIDDEN)
        return {'x': jax.random.normal(ks[0], (B, S, d), dtype=jnp.float32), 'y': jax.random.normal(ks[1], (B, S, d), dtype=jnp.float32), 'sa_wq': jax.random.normal(ks[2], (d, d), dtype=jnp.float32) * sc, 'sa_wk': jax.random.normal(ks[3], (d, d), dtype=jnp.float32) * sc, 'sa_wv': jax.random.normal(ks[4], (d, d), dtype=jnp.float32) * sc, 'sa_wo': jax.random.normal(ks[5], (d, d), dtype=jnp.float32) * sc, 'samlp_wg': jax.random.normal(ks[6], (d, h), dtype=jnp.float32) * sc, 'samlp_wu': jax.random.normal(ks[7], (d, h), dtype=jnp.float32) * sc, 'samlp_wd': jax.random.normal(ks[8], (h, d), dtype=jnp.float32) * sc, 'ca_wq': jax.random.normal(ks[9], (d, d), dtype=jnp.float32) * sc, 'ca_wk': jax.random.normal(ks[10], (d, d), dtype=jnp.float32) * sc, 'ca_wv': jax.random.normal(ks[11], (d, d), dtype=jnp.float32) * sc, 'ca_wo': jax.random.normal(ks[12], (d, d), dtype=jnp.float32) * sc, 'camlp_wg': jax.random.normal(ks[13], (d, h), dtype=jnp.float32) * sc, 'camlp_wu': jax.random.normal(ks[14], (d, h), dtype=jnp.float32) * sc, 'camlp_wd': jax.random.normal(ks[15], (h, d), dtype=jnp.float32) * sc}
    _L1_xattn_all = _L1_xattn_setup()
    _L1_xattn_in = {k: v for k, v in _L1_xattn_all.items() if k in ('sa_wq', 'sa_wk', 'sa_wv', 'sa_wo', 'samlp_wg', 'samlp_wu', 'samlp_wd', 'ca_wq', 'ca_wk', 'ca_wv', 'ca_wo', 'camlp_wg', 'camlp_wu', 'camlp_wd')}
    del _L1_xattn_all
    return {'x': x, 'ctx_1024': ctx_1024, 'L0_xattn_sa_wq': _L0_xattn_in['sa_wq'], 'L0_xattn_sa_bq': _L0_xattn_in['sa_bq'], 'L0_xattn_sa_wk': _L0_xattn_in['sa_wk'], 'L0_xattn_sa_bk': _L0_xattn_in['sa_bk'], 'L0_xattn_sa_wv': _L0_xattn_in['sa_wv'], 'L0_xattn_sa_bv': _L0_xattn_in['sa_bv'], 'L0_xattn_sa_wo': _L0_xattn_in['sa_wo'], 'L0_xattn_sa_bo': _L0_xattn_in['sa_bo'], 'L0_xattn_ca_wq': _L0_xattn_in['ca_wq'], 'L0_xattn_ca_bq': _L0_xattn_in['ca_bq'], 'L0_xattn_ca_wk': _L0_xattn_in['ca_wk'], 'L0_xattn_ca_bk': _L0_xattn_in['ca_bk'], 'L0_xattn_ca_wv': _L0_xattn_in['ca_wv'], 'L0_xattn_ca_bv': _L0_xattn_in['ca_bv'], 'L0_xattn_ca_wo': _L0_xattn_in['ca_wo'], 'L0_xattn_ca_bo': _L0_xattn_in['ca_bo'], 'L0_xattn_ln1_g': _L0_xattn_in['ln1_g'], 'L0_xattn_ln1_b': _L0_xattn_in['ln1_b'], 'L0_xattn_ln2_g': _L0_xattn_in['ln2_g'], 'L0_xattn_ln2_b': _L0_xattn_in['ln2_b'], 'L0_xattn_ln3_g': _L0_xattn_in['ln3_g'], 'L0_xattn_ln3_b': _L0_xattn_in['ln3_b'], 'L0_xattn_router_w': _L0_xattn_in['router_w'], 'L0_xattn_router_b': _L0_xattn_in['router_b'], 'L0_xattn_e_w1': _L0_xattn_in['e_w1'], 'L0_xattn_e_b1': _L0_xattn_in['e_b1'], 'L0_xattn_e_w2': _L0_xattn_in['e_w2'], 'L0_xattn_e_b2': _L0_xattn_in['e_b2'], 'L1_xattn_sa_wq': _L1_xattn_in['sa_wq'], 'L1_xattn_sa_wk': _L1_xattn_in['sa_wk'], 'L1_xattn_sa_wv': _L1_xattn_in['sa_wv'], 'L1_xattn_sa_wo': _L1_xattn_in['sa_wo'], 'L1_xattn_samlp_wg': _L1_xattn_in['samlp_wg'], 'L1_xattn_samlp_wu': _L1_xattn_in['samlp_wu'], 'L1_xattn_samlp_wd': _L1_xattn_in['samlp_wd'], 'L1_xattn_ca_wq': _L1_xattn_in['ca_wq'], 'L1_xattn_ca_wk': _L1_xattn_in['ca_wk'], 'L1_xattn_ca_wv': _L1_xattn_in['ca_wv'], 'L1_xattn_ca_wo': _L1_xattn_in['ca_wo'], 'L1_xattn_camlp_wg': _L1_xattn_in['camlp_wg'], 'L1_xattn_camlp_wu': _L1_xattn_in['camlp_wu'], 'L1_xattn_camlp_wd': _L1_xattn_in['camlp_wd']}

def reference(x, ctx_1024, L0_xattn_sa_wq, L0_xattn_sa_bq, L0_xattn_sa_wk, L0_xattn_sa_bk, L0_xattn_sa_wv, L0_xattn_sa_bv, L0_xattn_sa_wo, L0_xattn_sa_bo, L0_xattn_ca_wq, L0_xattn_ca_bq, L0_xattn_ca_wk, L0_xattn_ca_bk, L0_xattn_ca_wv, L0_xattn_ca_bv, L0_xattn_ca_wo, L0_xattn_ca_bo, L0_xattn_ln1_g, L0_xattn_ln1_b, L0_xattn_ln2_g, L0_xattn_ln2_b, L0_xattn_ln3_g, L0_xattn_ln3_b, L0_xattn_router_w, L0_xattn_router_b, L0_xattn_e_w1, L0_xattn_e_b1, L0_xattn_e_w2, L0_xattn_e_b2, L1_xattn_sa_wq, L1_xattn_sa_wk, L1_xattn_sa_wv, L1_xattn_sa_wo, L1_xattn_samlp_wg, L1_xattn_samlp_wu, L1_xattn_samlp_wd, L1_xattn_ca_wq, L1_xattn_ca_wk, L1_xattn_ca_wv, L1_xattn_ca_wo, L1_xattn_camlp_wg, L1_xattn_camlp_wu, L1_xattn_camlp_wd):
    import jax
    import jax.numpy as jnp

    def _L0_xattn_ref(x, encoder_output, sa_wq, sa_bq, sa_wk, sa_bk, sa_wv, sa_bv, sa_wo, sa_bo, ca_wq, ca_bq, ca_wk, ca_bk, ca_wv, ca_bv, ca_wo, ca_bo, ln1_g, ln1_b, ln2_g, ln2_b, ln3_g, ln3_b, router_w, router_b, e_w1, e_b1, e_w2, e_b2):
        import jax, jax.numpy as jnp
        import numpy as np
        B, S, SE, D, H, FF, E, K = (2, 512, 512, 256, 16, 1024, 8, 2)
        HD = D // H

        def _layernorm(x, g, b):
            m = x.mean(-1, keepdims=True)
            v = ((x - m) ** 2).mean(-1, keepdims=True)
            return (x - m) / jnp.sqrt(v + 1e-05) * g + b

        def _attn(q_in, k_in, v_in, wq, bq, wk, bk, wv, bv, wo, bo, causal):
            Bq, Sq, Dm = q_in.shape
            Sk = k_in.shape[1]
            Q = (q_in @ wq + bq).reshape(Bq, Sq, H, HD)
            Kp = (k_in @ wk + bk).reshape(Bq, Sk, H, HD)
            V = (v_in @ wv + bv).reshape(Bq, Sk, H, HD)
            scores = jnp.einsum('bqhd,bkhd->bhqk', Q, Kp) / jnp.sqrt(jnp.float32(HD))
            if causal:
                mask = jnp.tril(jnp.ones((Sq, Sk), bool))
                scores = jnp.where(mask, scores, -jnp.inf)
            a = jax.nn.softmax(scores, axis=-1)
            o = jnp.einsum('bhqk,bkhd->bqhd', a, V).reshape(Bq, Sq, Dm)
            return o @ wo + bo

        def _moe(x, rw, rb, w1, b1, w2, b2):
            T = x.shape[0] * x.shape[1]
            xf = x.reshape(T, D)
            router_weights = jax.nn.softmax(xf @ rw + rb, axis=-1)
            topw, topi = jax.lax.top_k(router_weights, K)
            topw = jax.nn.softmax(topw, axis=-1)
            combine = jnp.zeros((T, E), xf.dtype).at[jnp.arange(T)[:, None], topi].add(topw)
            h = jax.nn.gelu(jnp.einsum('td,edf->etf', xf, w1) + b1[:, None, :], approximate=False)
            eo = jnp.einsum('etf,efd->etd', h, w2) + b2[:, None, :]
            out = jnp.einsum('etd,te->td', eo, combine)
            return out.reshape(x.shape)
        x = _layernorm(x + _attn(x, x, x, sa_wq, sa_bq, sa_wk, sa_bk, sa_wv, sa_bv, sa_wo, sa_bo, True), ln1_g, ln1_b)
        x = _layernorm(x + _attn(x, encoder_output, encoder_output, ca_wq, ca_bq, ca_wk, ca_bk, ca_wv, ca_bv, ca_wo, ca_bo, False), ln2_g, ln2_b)
        x = _layernorm(x + _moe(x, router_w, router_b, e_w1, e_b1, e_w2, e_b2), ln3_g, ln3_b)
        return x

    def _L1_xattn_ref(x, y, sa_wq, sa_wk, sa_wv, sa_wo, samlp_wg, samlp_wu, samlp_wd, ca_wq, ca_wk, ca_wv, ca_wo, camlp_wg, camlp_wu, camlp_wd):
        import jax, jax.numpy as jnp
        import numpy as np
        MODEL_DIM = 256
        HEAD_SIZE = 64
        N_HEADS = MODEL_DIM // HEAD_SIZE
        HIDDEN = 4 * MODEL_DIM
        B, S = (4, 512)

        def _mha(x, ctx, wq, wk, wv, wo):
            b, s, d = x.shape
            t = ctx.shape[1]
            q = (x @ wq).reshape(b, s, N_HEADS, HEAD_SIZE)
            k = (ctx @ wk).reshape(b, t, N_HEADS, HEAD_SIZE)
            v = (ctx @ wv).reshape(b, t, N_HEADS, HEAD_SIZE)
            scores = jnp.einsum('bqhd,bkhd->bhqk', q, k) / jnp.sqrt(jnp.float32(HEAD_SIZE)).astype(x.dtype)
            attn = jax.nn.softmax(scores, axis=-1)
            out = jnp.einsum('bhqk,bkhd->bqhd', attn, v).reshape(b, s, d)
            return out @ wo

        def _swiglu(x, wg, wu, wd):
            return jax.nn.silu(x @ wg) * (x @ wu) @ wd
        x = x + _mha(x, x, sa_wq, sa_wk, sa_wv, sa_wo)
        x = x + _swiglu(x, samlp_wg, samlp_wu, samlp_wd)
        x = x + _mha(x, y, ca_wq, ca_wk, ca_wv, ca_wo)
        x = x + _swiglu(x, camlp_wg, camlp_wu, camlp_wd)
        return x
    x = _L0_xattn_ref(x, ctx_1024, L0_xattn_sa_wq, L0_xattn_sa_bq, L0_xattn_sa_wk, L0_xattn_sa_bk, L0_xattn_sa_wv, L0_xattn_sa_bv, L0_xattn_sa_wo, L0_xattn_sa_bo, L0_xattn_ca_wq, L0_xattn_ca_bq, L0_xattn_ca_wk, L0_xattn_ca_bk, L0_xattn_ca_wv, L0_xattn_ca_bv, L0_xattn_ca_wo, L0_xattn_ca_bo, L0_xattn_ln1_g, L0_xattn_ln1_b, L0_xattn_ln2_g, L0_xattn_ln2_b, L0_xattn_ln3_g, L0_xattn_ln3_b, L0_xattn_router_w, L0_xattn_router_b, L0_xattn_e_w1, L0_xattn_e_b1, L0_xattn_e_w2, L0_xattn_e_b2)
    x = _L1_xattn_ref(x, ctx_1024, L1_xattn_sa_wq, L1_xattn_sa_wk, L1_xattn_sa_wv, L1_xattn_sa_wo, L1_xattn_samlp_wg, L1_xattn_samlp_wu, L1_xattn_samlp_wd, L1_xattn_ca_wq, L1_xattn_ca_wk, L1_xattn_ca_wv, L1_xattn_ca_wo, L1_xattn_camlp_wg, L1_xattn_camlp_wu, L1_xattn_camlp_wd)
    return x

_drawn_inputs = setup_inputs


def setup_inputs(seed=0):
    import zlib

    import numpy as np

    out = dict(_drawn_inputs(seed))
    spreads = {'L0_xattn_sa_bq': (0.0, 0.8),
     'L0_xattn_sa_bk': (0.0, 0.8),
     'L0_xattn_sa_bv': (0.0, 0.1),
     'L0_xattn_sa_bo': (0.0, 0.1),
     'L0_xattn_ca_bq': (0.0, 0.8),
     'L0_xattn_ca_bk': (0.0, 0.8),
     'L0_xattn_ca_bv': (0.0, 0.1),
     'L0_xattn_ca_bo': (0.0, 0.1),
     'L0_xattn_ln1_g': (1.0, 0.2),
     'L0_xattn_ln1_b': (0.0, 0.1),
     'L0_xattn_ln2_g': (1.0, 0.2),
     'L0_xattn_ln2_b': (0.0, 0.1),
     'L0_xattn_ln3_g': (1.0, 0.2),
     'L0_xattn_ln3_b': (0.0, 0.1),
     'L0_xattn_router_b': (0.0, 0.1),
     'L0_xattn_e_b1': (0.0, 0.339),
     'L0_xattn_e_b2': (0.0, 0.1)}
    factors = {'L0_xattn_sa_wq': 8.0,
     'L0_xattn_sa_wk': 8.0,
     'L0_xattn_sa_wv': 3.991,
     'L0_xattn_ca_wq': 8.0,
     'L0_xattn_ca_wk': 8.0,
     'L1_xattn_sa_wq': 8.0,
     'L1_xattn_sa_wk': 8.0,
     'L1_xattn_sa_wv': 2.692,
     'L1_xattn_sa_wo': 2.715,
     'L1_xattn_ca_wq': 8.0,
     'L1_xattn_ca_wk': 8.0}
    for name, (base, spread) in spreads.items():
        noise = np.random.default_rng([zlib.crc32(name.encode()), seed]).standard_normal(out[name].shape)
        drawn = base * np.exp(spread * noise) if base else spread * noise
        out[name] = jnp.asarray(drawn.astype(out[name].dtype))
    for name, factor in factors.items():
        out[name] = (out[name] * factor).astype(out[name].dtype)
    return out
```

```python
from contextlib import ExitStack

import numpy as np
from concourse import mybir

F32 = mybir.dt.float32
BF16 = mybir.dt.bfloat16
U32 = mybir.dt.uint32
ALU = mybir.AluOpType
ACT = mybir.ActivationFunctionType
AX = mybir.AxisListType

P = 128
B, S, D = 2, 512, 256
SE = 1024
T = B * S
DC = D // P
TB = S // P
NT = T // P
FF = 1024
FC = FF // P
E = 8
NEG = -1.0e30
EPS = 1e-5


class Signal:

    def __init__(self, sem, known):
        self.sem, self.known, self.count, self.seen = sem, known, 0, {}

    def next(self, label=None, by=1):
        self.count += by
        if label is not None:
            self.seen[label] = self.count
        return self.sem, by

    def when(self, label):
        return self.sem, (self.known[label] if self.known is not None else 1)

    def now(self):
        return self.sem, self.count


class Attention:

    def __init__(self, name, heads, nk, causal, group, split_rows, layer, lead):
        self.name, self.H, self.nk, self.causal, self.G = name, heads, nk, causal, group
        self.HD = D // heads
        self.scale = 1.0 / float(np.sqrt(self.HD))
        self.KT = nk // P
        self.layer = layer
        self.groups = [(b, g) for b in range(B) for g in range(heads // group)]
        self.heads = {(b, g): [g * group + j for j in range(group)] for b, g in self.groups}
        self.lead = lead

    def queries_from(self, kt):
        return kt * P if self.causal else 0

    def keys_to(self, qt):
        return (qt + 1) * P if self.causal else self.nk

    def steps(self):
        first = []
        for b, g in self.groups:
            first += [("max", b, h, qt) for h in self.heads[b, g] for qt in range(TB)]
            first.append(("shift", b, g))
        units = []
        for b, g in self.groups:
            units += [("unit", b, g, kt, j) for kt in range(self.KT) for j in range(self.G)]
        per_group = self.KT * self.G
        jobs = self.G * TB + 1
        out, at, held = [], 0, []
        for n, u in enumerate(units):
            want = min(len(first), int(np.ceil((n + 1) * jobs / per_group)) + jobs + self.lead)
            while at < want:
                out.append(first[at])
                at += 1
            out.append(u + (n,))
            due = sorted((x for x in held if x[0] <= n), key=lambda x: x[1][0] != "evict")
            held = [x for x in held if x[0] > n]
            out += [x[1] for x in due]
            if (n + 1) % per_group == 0:
                b, g = u[1], u[2]
                held.append((n + 2, ("evict", b, g)))
                held.append((n + 4, ("norm", b, g)))
                if g == self.H // self.G - 1:
                    held.append((n + 8, ("heads", b)))
                    held.append((n + 11, ("proj", b)))
                    if self.layer == 0:
                        held.append((n + 14, ("ln", b)))
                        held.append((n + 26, ("turn", b)))
        out += first[at:]
        out += [x[1] for x in held]
        return out


ATTENTIONS = {
    "sa0": Attention("sa0", 16, S, True, 4, 96, 0, 4),
    "ca0": Attention("ca0", 16, SE, False, 4, 96, 0, 4),
    "sa1": Attention("sa1", 4, S, False, 2, 128, 1, 4),
    "ca1": Attention("ca1", 4, SE, False, 2, 128, 1, 4),
}
QUERY_PARTS = (0, 0, 1, 1, 0, 2)
KEY_PARTS = (0, 1, 0, 1, 2, 0)


def program(nc, io, known):
    ctx = ExitStack()
    signals = {}

    with ctx:
        def sb(name, shape, dt=F32):
            return ctx.enter_context(nc.sbuf_tensor(name, shape, dt))

        def signal(name):
            s = Signal(ctx.enter_context(nc.semaphore(name)), None if known is None else known[name])
            signals[name] = s
            return s

        ident = sb("ident", [P, P])
        identb = sb("identb", [P, P], BF16)
        mask_q = sb("mask_q", [P, P], BF16)
        mask_k = sb("mask_k", [P, P], BF16)
        onesb = sb("onesb", [P, P], BF16)
        onesf = sb("onesf", [P, 32])
        minus_half = sb("minus_half", [P, TB])
        expert_no = sb("expert_no", [P, E])
        xT = sb("xT", [P, DC, T])
        xtok = sb("xtok", [P, NT, D])
        ctxT = sb("ctxT", [P, DC, B * SE])
        wset = [sb(f"wset{i}", [P, 4, DC, D]) for i in range(2)]
        arena = sb("arena", [P, 49152], BF16)
        vx = sb("vx", [P, 16 * 272 + 16])
        exact = sb("exact", [P, DC, S])
        parts = sb("parts", [P, 2, DC, 3, S], BF16)
        probs = parts[:, :, :, :, :].rearrange("p i c r t -> p (i c r t)")[:, 0:4 * 2 * S].bitcast(F32)\
            .rearrange("p (i t) -> p i t", i=4)
        sums = sb("sums", [P, 2, S])
        dens = sb("dens", [64, S])
        otok = sb("otok", [P, TB, D])
        oT = exact
        negmax = sb("negmax", [P, 2, TB, 4])
        shift = sb("shift", [4, S])
        shiftb = sb("shiftb", [4, 3, S], BF16)
        rden = sb("rden", [P, TB, 4])
        biasT = {n: sb(f"biasT_{n}", [P, DC]) for n in ("sa_bq", "sa_bk", "ca_bq", "ca_bk")}
        row = {n: sb(f"row_{n}", [P, D]) for n in
               ("sa_bv", "sa_bo", "ca_bv", "ca_bo", "ln1_g", "ln1_b", "ln2_g", "ln2_b", "ln3_g", "ln3_b")}
        stats = sb("stats", [P, TB, 6])
        mv = sb("mv", [P, TB, 2])
        var = sb("var", [P, TB])
        rstd = sb("rstd", [P, TB])
        rw = sb("rw", [P, DC, E])
        rb = sb("rb", [P, E])
        b1T = sb("b1T", [P, E, FC])
        b2 = sb("b2", [E, D])
        lg = sb("lg", [P, NT, E])
        best = sb("best", [P, NT, 8])
        besti = sb("besti", [P, NT, 8], U32)
        bestf = sb("bestf", [P, NT, 8])
        small = sb("small", [P, 6, NT])
        comb = sb("comb", [P, NT, E])
        comb2 = sb("comb2", [P, NT, E])
        combT = otok[0:E, :, :].rearrange("e t d -> e (t d)")

        a_bank = [ctx.enter_context(nc.psum_tensor(f"a_bank{i}", [P, 2 * 512], F32)) for i in range(2)]
        b_bank = [ctx.enter_context(nc.psum_tensor(f"b_bank{i}", [P, 512], F32)) for i in range(2)]
        o_bank = [ctx.enter_context(nc.psum_tensor(f"o_bank{i}", [P, 512], F32)) for i in range(2)]

        arena_f = arena[:, :].bitcast(F32)
        ctx_in = arena_f[:, 0:16 * D].rearrange("p (t d) -> p t d", t=16)
        w1 = [arena_f[:, 2048 * i:2048 * (i + 1)].rearrange("p (c f) -> p c f", c=DC) for i in range(2)]
        w2 = [arena_f[:, 4096 + 2048 * i:4096 + 2048 * (i + 1)].rearrange("p (c n) -> p c n", c=FC)
              for i in range(2)]
        hT = [arena_f[:, 8192 + 4096 * i:8192 + 4096 * (i + 1)].rearrange("p (c t) -> p c t", c=FC)
              for i in range(2)]
        mlp_w = [arena_f[:, 16384 + 2048 * i:16384 + 2048 * (i + 1)] for i in range(3)]
        gate = arena_f[:, 22528:22528 + 1024].rearrange("p (i t) -> p i t", i=2)

        def q_stack(a, b, i=0):
            n = a.H * S
            base = (b * 3 + i) * n if a.layer else b * n
            return arena[:, base:base + n].rearrange("p (h t) -> p h t", h=a.H)

        def k_stack(a, b, i=0):
            n = a.H * a.nk
            base = 12288 + (b * 2 + i) * n if a.layer else 16384 + b * n
            return arena[:, base:base + n].rearrange("p (h t) -> p h t", h=a.H)

        def m_rows(b):
            return arena[:, 28672 + b * 2048:28672 + (b + 1) * 2048].rearrange("p (h t) -> p h t", h=4)

        def v_head(a, tile, h):
            if a.layer:
                return vx[:, tile * D + h * 64:tile * D + h * 64 + 64]
            return vx[:, tile * 272 + h * 17:tile * 272 + h * 17 + 32]

        scratch_q = nc.dram_tensor("scratch_q", (4, 3, D, T), BF16, kind="Internal").ap()
        scratch_k = nc.dram_tensor("scratch_k", (4, 3, D, B * SE), BF16, kind="Internal").ap()

        a_full = signal("a_full")
        b_full = signal("b_full")
        pv_done = signal("pv_done")
        pe_past = signal("pe_past")
        a_free = signal("a_free")
        vec = signal("vec")
        b_free = signal("b_free")
        act_done = signal("act_done")
        pool_done = signal("pool_done")
        load = {n: signal("load_" + n) for n in
                ("x", "ctx", "wsa0", "wca0", "wsa1", "wca1", "rows", "mlp_sa1", "mlp_ca1")}
        w_load = [signal(f"load_w{i}") for i in range(2)]
        part_out = [signal(f"part_out{i}") for i in range(2)]
        stack_in = [signal(f"stack_in{i}") for i in range(4)]
        shift_in = [signal(f"shift_in{i}") for i in range(2)]
        stored = signal("stored")

        att_index = {n: i for i, n in enumerate(ATTENTIONS)}
        split_jobs = []
        for n, a in ATTENTIONS.items():
            split_jobs += [(n, "k", u) for u in range(B * a.nk // S)]
            split_jobs += [(n, "q", u) for u in range(B)]
        split_no = {j: i for i, j in enumerate(split_jobs)}

        a_keys, b_keys = [], []
        a_turn = {} if known is None else known["_a_turn"]
        b_turn = {} if known is None else known["_b_turn"]

        def a_slot(key):
            return a_bank[a_turn.get(key, 0)]

        def b_slot(key):
            return b_bank[b_turn.get(key, 0)]

        block = ctx.enter_context(nc.Block())

        @block.tensor
        def _(pe):
            def take_a(key):
                if len(a_keys) >= 2:
                    pe.wait_ge(*a_free.when(a_keys[-2]))
                a_keys.append(key)
                return a_bank[(len(a_keys) - 1) % 2]

            def take_b(key):
                if len(b_keys) >= 2:
                    pe.wait_ge(*b_free.when(b_keys[-2]))
                b_keys.append(key)
                return b_bank[(len(b_keys) - 1) % 2]

            def turn(key, tiles):
                pair = take_a(key)
                for t, tile in enumerate(tiles):
                    for c in range(DC):
                        mm = pe.transpose(pair[:, c * S + t * P:c * S + (t + 1) * P],
                                          tile[:, c * P:(c + 1) * P], ident[:, :])
                mm.then_inc(*a_full.next(key))

            def project_T(key, w, src, at):
                pair = take_a(key)
                for dc in range(DC):
                    for c in range(DC):
                        mm = pe.matmul(pair[:, dc * S:(dc + 1) * S], w[:, c, dc * P:(dc + 1) * P],
                                       src[:, c, at:at + S], start=(c == 0), stop=(c == DC - 1))
                mm.then_inc(*a_full.next(key))

            def project_tok(key, w, src, at):
                pair = take_a(key)
                for t in range(TB):
                    for c in range(DC):
                        mm = pe.matmul(pair[:, t * D:(t + 1) * D], src[:, c, at + t * P:at + (t + 1) * P],
                                       w[:, c, :], start=(c == 0), stop=(c == DC - 1))
                mm.then_inc(*a_full.next(key))

            def projections(a, w):
                kv = xT if a.nk == S else ctxT
                for u in range(B * a.nk // S):
                    project_T(("split", a.name, "k", u), w[:, 1], kv, u * S)
                    project_tok(("v", a.name, u), w[:, 2], kv, u * S)
                for u in range(B):
                    project_T(("split", a.name, "q", u), w[:, 0], xT, u * S)

            def score_passes(a, b, h, queries, keys, with_shift):
                out = []
                if not a.layer:
                    rows = 99 if with_shift else 96
                    out.append((q_stack(a, b)[0:rows, h, queries], k_stack(a, b)[0:rows, h, keys]))
                else:
                    for qi, ki in ((0, 0), (1, 0), (2, 1)):
                        out.append((q_stack(a, b, qi)[:, h, queries], k_stack(a, b, ki)[:, h, keys]))
                    if with_shift:
                        out.append((m_rows(b)[:, h, queries], onesb[:, 0:P]))
                return out

            def attention(a):
                pending = []

                def product(item):
                    b, g, kt, j, n = item
                    h = g * a.G + j
                    q0 = a.queries_from(kt)
                    gi = a.groups.index((b, g))
                    tile = b * a.KT + kt
                    pe.wait_ge(*b_free.when(("unit", a.name, n)))
                    first = kt == 0 and j == 0
                    if first:
                        if a.layer == 0 and gi >= 2:
                            pe.wait_ge(*vec.when(("evict", a.name, gi - 2)))
                        if a.layer == 1 and gi >= 1:
                            pe.wait_ge(*vec.when(("evict", a.name, gi - 1)))
                        if gi == 0:
                            pe.wait_ge(*a_free.when(("v", a.name, B * a.nk // S - 1)))
                    p = probs[:, n % 4, 0:S - q0]
                    if a.layer == 0:
                        bank = o_bank[gi % 2]
                        mm = pe.matmul(bank[32 * j:32 * j + 32, q0:S], v_head(a, tile, h), p,
                                       start=(kt == 0), stop=(kt == a.KT - 1), tile_position=(0, 32 * j))
                    else:
                        pe.matmul(o_bank[0][64 * j:64 * j + 64, :], v_head(a, tile, h), p,
                                  start=(kt == 0), stop=(kt == a.KT - 1), tile_position=(0, 64 * j))
                        mm = pe.matmul(o_bank[1][32 * j:32 * j + 32, :], onesf[:, :], p,
                                       start=(kt == 0), stop=(kt == a.KT - 1), tile_position=(0, 32 * j))
                    mm.then_inc(*pv_done.next((a.name, n)))

                stacks_waited = set()
                for step in a.steps():
                    kind, b = step[0], step[1]
                    if step == ("evict",) + a.groups[-1]:
                        while pending:
                            product(pending.pop(0))
                    if kind == "max":
                        _, b, h, qt = step
                        if not stacks_waited:
                            stacks_waited.add(b)
                            pe.wait_ge(*stack_in[att_index[a.name]].when("all"))
                        pair = take_a(step + (a.name,))
                        nk = a.keys_to(qt)
                        for k0 in range(0, nk, 512):
                            n = min(512, nk - k0)
                            ps = score_passes(a, b, h, slice(qt * P, (qt + 1) * P), slice(k0, k0 + n), False)
                            for i, (q, k) in enumerate(ps):
                                mm = pe.matmul(pair[:, k0:k0 + n], q, k, start=(i == 0),
                                               stop=(i == len(ps) - 1 and not a.causal))
                        if a.causal:
                            mm = pe.matmul(pair[:, qt * P:(qt + 1) * P], identb[:, :], mask_q[:, :],
                                           start=False, stop=True)
                        mm.then_inc(*a_full.next(step + (a.name,)))
                    elif kind == "shift":
                        _, b, g = step
                        gi = a.groups.index((b, g))
                        pair = take_a(step + (a.name,))
                        for h in a.heads[b, g]:
                            for qt in range(TB):
                                last = ("max", b, h, qt, a.name)
                        pe.wait_ge(*a_free.when(last))
                        for qt in range(TB):
                            mm = pe.transpose(pair[0:a.G, qt * P:(qt + 1) * P],
                                              negmax[:, gi % 2, qt, 0:a.G], ident[:, :])
                        mm.then_inc(*a_full.next(step + (a.name,)))
                    elif kind == "unit":
                        _, b, g, kt, j, n = step
                        h = g * a.G + j
                        q0 = a.queries_from(kt)
                        key = ("unit", a.name, n)
                        if kt == 0 and j == 0:
                            gi = a.groups.index((b, g))
                            pe.wait_ge(*shift_in[gi % 2].when((a.name, gi)))
                        bank = take_b(key)
                        ps = score_passes(a, b, h, slice(q0, S), slice(kt * P, (kt + 1) * P), True)
                        for i, (q, k) in enumerate(ps):
                            mm = pe.matmul(bank[:, 0:S - q0], k, q, start=(i == 0),
                                           stop=(i == len(ps) - 1 and not a.causal))
                        if a.causal:
                            mm = pe.matmul(bank[:, 0:P], identb[:, :], mask_k[:, :], start=False, stop=True)
                        mm.then_inc(*b_full.next(key))
                        pending.append(step[1:])
                        if len(pending) > 2:
                            product(pending.pop(0))
                    elif kind == "norm":
                        _, b, g = step
                        gi = a.groups.index((b, g))
                        pe.wait_ge(*vec.when(("evict", a.name, gi)))
                        pair = take_a(step + (a.name,))
                        src = sums[:, gi % 2, :]
                        for qt in range(TB):
                            mm = pe.transpose(pair[:, qt * P:(qt + 1) * P], src[:, qt * P:(qt + 1) * P],
                                              ident[:, :])
                        if a.layer:
                            for qt in range(TB):
                                mm = pe.transpose(pair[:, 512 + qt * 64:512 + (qt + 1) * 64],
                                                  dens[:, qt * P:(qt + 1) * P], ident[0:64, 0:64])
                        mm.then_inc(*a_full.next(step + (a.name,)))
                    elif kind == "heads":
                        pe.wait_ge(*a_free.when(("norm", b, a.H // a.G - 1, a.name)))
                        turn(step + (a.name,), [otok[:, t, :] for t in range(TB)])
                    elif kind == "proj":
                        pe.wait_ge(*a_free.when(("heads", b, a.name)))
                        w = wset[att_index[a.name] % 2][:, 3]
                        if a.layer:
                            project_T(step + (a.name,), w, oT, 0)
                        else:
                            project_tok(step + (a.name,), w, oT, 0)
                    elif kind == "turn":
                        pe.wait_ge(*pool_done.when(("ln", a.name, b)))
                        turn(step + (a.name,), [xtok[:, b * TB + t, :] for t in range(TB)])
                while pending:
                    product(pending.pop(0))

            pe.wait_ge(*pool_done.when("constants"))
            pe.wait_ge(*load["x"].when("all"))
            for b in range(B):
                turn(("x", b), [xtok[:, b * TB + t, :] for t in range(TB)])
            pe.wait_ge(*load["ctx"].when("all"))
            for u in range(B * SE // S):
                turn(("ctx", u), [ctx_in[:, u * TB + t, :] for t in range(TB)])

            def attend(name):
                a = ATTENTIONS[name]
                pe.wait_ge(*load["w" + name].when("all"))
                projections(a, wset[att_index[name] % 2])
                attention(a)
                pe.wait_ge(*a_free.when(a_keys[-1]))

            pe.wait_ge(*a_free.when(("ctx", B * SE // S - 1)))
            attend("sa0")
            attend("ca0")

            key = ("router",)
            pair = take_a(key)
            pe.wait_ge(*load["rows"].when("all"))
            for t in range(NT):
                for c in range(DC):
                    mm = pe.matmul(pair[:, t * E:(t + 1) * E], xT[:, c, t * P:(t + 1) * P], rw[:, c, :],
                                   start=(c == 0), stop=(c == DC - 1))
            mm.then_inc(*a_full.next(key))

            def expert_hidden(e, hf):
                if hf == 0:
                    pe.wait_ge(*w_load[e % 2].when(e))
                for f in range(FC):
                    bank = take_b(("h", e, hf, f))
                    for c in range(DC):
                        mm = pe.matmul(bank[:, :], w1[e % 2][:, c, f * P:(f + 1) * P],
                                       xT[:, c, hf * S:(hf + 1) * S], start=(c == 0), stop=(c == DC - 1))
                    mm.then_inc(*b_full.next(("h", e, hf, f)))

            def expert_out(e, hf):
                pair = take_a(("eo", e, hf))
                pe.wait_ge(*b_free.when(("h", e, hf, FC - 1)))
                for t in range(TB):
                    for f in range(FC):
                        mm = pe.matmul(pair[:, t * D:(t + 1) * D], hT[hf][:, f, t * P:(t + 1) * P],
                                       w2[e % 2][:, f, :], start=(f == 0), stop=(f == FC - 1))
                mm.then_inc(*a_full.next(("eo", e, hf)))

            expert_hidden(0, 0)
            pair = take_a(("combT",))
            pe.wait_ge(*vec.when("comb"))
            for t in range(NT):
                mm = pe.transpose(pair[0:E, t * P:(t + 1) * P], comb[:, t, :], ident[:, :])
            mm.then_inc(*a_full.next(("combT",)))
            pe.wait_ge(*a_free.when(("combT",)))
            for b in range(B):
                pair = take_a(("b2", b))
                for t in range(TB):
                    at = (b * TB + t) * P
                    mm = pe.matmul(pair[:, t * D:(t + 1) * D], combT[:, at:at + P], b2[:, :],
                                   start=True, stop=True)
                mm.then_inc(*a_full.next(("b2", b)))
            order = [(e, hf) for e in range(E) for hf in range(B)]
            for i, (e, hf) in enumerate(order):
                if i + 1 < len(order):
                    expert_hidden(*order[i + 1])
                expert_out(e, hf)
            for b in range(B):
                pe.wait_ge(*pool_done.when(("ln", "moe", b)))
                turn(("turn", b, "moe"), [xtok[:, b * TB + t, :] for t in range(TB)])
            pe.wait_ge(*a_free.when(a_keys[-1]))

            def mlp(name):
                wg = mlp_w[0].rearrange("p (c f) -> p c f", c=DC)
                wu = mlp_w[1].rearrange("p (c f) -> p c f", c=DC)
                wd = mlp_w[2].rearrange("p (c n) -> p c n", c=FC)
                pe.wait_ge(*load["mlp_" + name].when("all"))
                for hf in range(B):
                    for f in range(FC):
                        bank = take_b(("g", name, hf, f))
                        for c in range(DC):
                            mm = pe.matmul(bank[:, :], wg[:, c, f * P:(f + 1) * P], xT[:, c, hf * S:(hf + 1) * S],
                                           start=(c == 0), stop=(c == DC - 1))
                        mm.then_inc(*b_full.next(("g", name, hf, f)))
                        pair = take_a(("u", name, hf, f))
                        for c in range(DC):
                            mm = pe.matmul(pair[:, 0:S], wu[:, c, f * P:(f + 1) * P], xT[:, c, hf * S:(hf + 1) * S],
                                           start=(c == 0), stop=(c == DC - 1))
                        mm.then_inc(*a_full.next(("u", name, hf, f)))
                for hf in range(B):
                    pair = take_a(("down", name, hf))
                    pe.wait_ge(*a_free.when(("u", name, hf, FC - 1)))
                    for dc in range(DC):
                        for f in range(FC):
                            mm = pe.matmul(pair[:, dc * S:(dc + 1) * S], wd[:, f, dc * P:(dc + 1) * P],
                                           hT[hf][:, f, :], start=(f == 0), stop=(f == FC - 1))
                    mm.then_inc(*a_full.next(("down", name, hf)))
                pe.wait_ge(*a_free.when(a_keys[-1]))

            attend("sa1")
            mlp("sa1")
            attend("ca1")
            mlp("ca1")
            for b in range(B):
                pair = take_a(("out", b))
                for t in range(TB):
                    for c in range(DC):
                        at = (b * TB + t) * P
                        mm = pe.transpose(pair[:, t * D + c * P:t * D + (c + 1) * P], xT[:, c, at:at + P],
                                          ident[:, :])
                mm.then_inc(*a_full.next(("out", b)))

        @block.vector
        def _(dve):
            def copy_T(key, dst):
                dve.wait_ge(*a_full.when(key))
                dve.tensor_copy(dst, a_slot(key)[:, :].rearrange("p (c t) -> p c t", c=DC))\
                   .then_inc(*a_free.next(key))

            def split(name, which, u):
                a = ATTENTIONS[name]
                key = ("split", name, which, u)
                i = split_no[name, which, u]
                dve.wait_ge(*a_full.when(key))
                pair = a_slot(key)
                if a.layer == 0:
                    bias = biasT[name[:2] + "_b" + which]
                    dve.tensor_scalar(exact[:, 0, :], pair[:, 0:S], bias[:, 0:1], None, ALU.add)\
                       .then_inc(*vec.next())
                    dve.tensor_scalar(exact[:, 1, :], pair[:, S:2 * S], bias[:, 1:2], None, ALU.add)\
                       .then_inc(*a_free.next(key))
                else:
                    dve.tensor_copy(exact[:, :, :], pair[:, :].rearrange("p (c t) -> p c t", c=DC))\
                       .then_inc(*a_free.next(key))
                part = parts[:, i % 2]
                if i >= 2:
                    dve.wait_ge(*part_out[i % 2].when(i - 2))
                dve.wait_ge(*vec.now()) if a.layer == 0 else None
                dve.wait_ge(*a_free.now())
                dve.tensor_copy(part[:, :, 0, :], exact[:, :, :]).then_inc(*vec.next())
                dve.wait_ge(*vec.now())
                dve.tensor_tensor(exact[:, :, :], exact[:, :, :], part[:, :, 0, :], ALU.subtract)\
                   .then_inc(*vec.next())
                dve.wait_ge(*vec.now())
                dve.tensor_copy(part[:, :, 1, :], exact[:, :, :]).then_inc(*vec.next())
                dve.wait_ge(*vec.now())
                dve.tensor_tensor(part[:, :, 2, :], exact[:, :, :], part[:, :, 1, :], ALU.subtract)\
                   .then_inc(*vec.next(("split", i)))
                dve.wait_ge(*vec.now())

            def values(name, u):
                a = ATTENTIONS[name]
                key = ("v", name, u)
                dve.wait_ge(*a_full.when(key))
                pair = a_slot(key)
                if a.layer == 0:
                    for t in range(TB):
                        tile = u * TB + t
                        dst = vx[:, tile * 272:tile * 272 + 272].rearrange("p (h d) -> p h d", d=17)[:, :, 0:16]
                        ins = dve.tensor_tensor(dst, pair[:, t * D:(t + 1) * D].rearrange("p (h d) -> p h d", d=16),
                                                row[name[:2] + "_bv"][:, :].rearrange("p (h d) -> p h d", d=16),
                                                ALU.add)
                        ins.then_inc(*(a_free.next(key) if t == TB - 1 else vec.next()))
                else:
                    at = u * TB * D
                    dve.tensor_copy(vx[:, at:at + TB * D], pair[:, :]).then_inc(*a_free.next(key))

            def normalise_rows(b, name):
                for t in range(TB):
                    dve.bn_stats(stats[:, t, :], xtok[:, b * TB + t, :]).then_inc(*vec.next())
                dve.wait_ge(*vec.now())
                for t in range(TB):
                    dve.bn_aggr(mv[:, t, :], stats[:, t, :]).then_inc(*vec.next())
                dve.wait_ge(*vec.now())
                dve.tensor_scalar(var[:, :], mv[:, :, 1], EPS, None, ALU.add)\
                   .then_inc(*vec.next(("var", name, b)))
                dve.wait_ge(*pool_done.when(("rstd", name, b)))
                for t in range(TB):
                    x = xtok[:, b * TB + t, :]
                    dve.tensor_scalar(x, x, mv[:, t, 0:1], rstd[:, t:t + 1], ALU.subtract, ALU.mult)\
                       .then_inc(*vec.next(("centred", name, b)))

            def attention(a):
                for step in a.steps():
                    kind, b = step[0], step[1]
                    key = step + (a.name,)
                    if kind == "max":
                        _, b, h, qt = step
                        g, j = h // a.G, h % a.G
                        gi = a.groups.index((b, g))
                        dve.wait_ge(*a_full.when(key))
                        dve.tensor_reduce(negmax[:, gi % 2, qt, j:j + 1], a_slot(key)[:, 0:a.keys_to(qt)],
                                          AX.X, ALU.max, negate=True).then_inc(*a_free.next(key))
                    elif kind == "shift":
                        _, b, g = step
                        gi = a.groups.index((b, g))
                        sh, out = shift[0:a.G, :], shiftb[0:a.G]
                        dve.wait_ge(*a_full.when(key))
                        dve.tensor_copy(sh, a_slot(key)[0:a.G, 0:S]).then_inc(*a_free.next(key))
                        if gi >= 1:
                            dve.wait_ge(*shift_in[(gi - 1) % 2].when((a.name, gi - 1)))
                        dve.wait_ge(*a_free.now())
                        dve.tensor_copy(out[:, 0, :], sh).then_inc(*vec.next())
                        dve.wait_ge(*vec.now())
                        dve.tensor_tensor(sh, sh, out[:, 0, :], ALU.subtract).then_inc(*vec.next())
                        dve.wait_ge(*vec.now())
                        dve.tensor_copy(out[:, 1, :], sh).then_inc(*vec.next())
                        dve.wait_ge(*vec.now())
                        dve.tensor_tensor(out[:, 2, :], sh, out[:, 1, :], ALU.subtract)\
                           .then_inc(*vec.next(("shift", a.name, gi)))
                        dve.wait_ge(*vec.now())
                    elif kind == "evict":
                        _, b, g = step
                        gi = a.groups.index((b, g))
                        last = (gi + 1) * a.KT * a.G - 1
                        dve.wait_ge(*pv_done.when((a.name, last)))
                        if a.layer:
                            dve.tensor_copy(dens[:, :], o_bank[1][0:64, :]).then_inc(*vec.next())
                            dve.tensor_copy(sums[:, gi % 2, :], o_bank[0][:, :])\
                               .then_inc(*vec.next(("evict", a.name, gi)))
                        else:
                            dve.tensor_copy(sums[:, gi % 2, :], o_bank[gi % 2][:, :])\
                               .then_inc(*vec.next(("evict", a.name, gi)))
                    elif kind == "norm":
                        _, b, g = step
                        dve.wait_ge(*a_full.when(key))
                        pair = a_slot(key)
                        if a.layer:
                            o = pair[:, 0:512].rearrange("p (t h d) -> p t h d", t=TB, h=2)
                            den = pair[:, 512:768].rearrange("p (t h d) -> p t h d", t=TB, h=2)[:, :, :, 0]
                        else:
                            o = pair[:, 0:512].rearrange("p (t h d) -> p t h d", t=TB, h=4)
                            den = o[:, :, :, 16]
                            o = o[:, :, :, 0:16]
                        dve.reciprocal(rden[:, :, 0:a.G], den).then_inc(*vec.next())
                        dve.wait_ge(*vec.now())
                        w = a.G * a.HD
                        dst = otok[:, :, g * w:(g + 1) * w].rearrange("p t (h d) -> p t h d", d=a.HD)
                        for t in range(TB):
                            r = rden[:, t, 0:a.G].unsqueeze(2).to_broadcast([P, a.G, a.HD])
                            ins = dve.tensor_tensor(dst[:, t], o[:, t], r, ALU.mult)
                            ins.then_inc(*(a_free.next(key) if t == TB - 1 else vec.next()))
                    elif kind == "heads":
                        copy_T(key, oT[:, :, :])
                    elif kind == "proj":
                        dve.wait_ge(*a_full.when(key))
                        if a.layer:
                            x = xT[:, :, b * S:(b + 1) * S]
                            dve.tensor_tensor(x, a_slot(key)[:, :].rearrange("p (c t) -> p c t", c=DC), x, ALU.add)\
                               .then_inc(*a_free.next(key))
                        else:
                            dve.wait_ge(*pool_done.when(("bo", a.name)))
                            x = xtok[:, b * TB:(b + 1) * TB, :]
                            dve.tensor_tensor(x, a_slot(key)[:, :].rearrange("p (t d) -> p t d", t=TB), x, ALU.add)\
                               .then_inc(*a_free.next(key))
                            dve.wait_ge(*a_free.now())
                    elif kind == "ln":
                        normalise_rows(b, a.name)
                    elif kind == "turn":
                        copy_T(key, xT[:, :, b * S:(b + 1) * S])

            def projections(name):
                a = ATTENTIONS[name]
                for u in range(B * a.nk // S):
                    split(name, "k", u)
                    values(name, u)
                for u in range(B):
                    split(name, "q", u)

            dve.wait_ge(*pool_done.when("constants"))
            for b in range(B):
                copy_T(("x", b), xT[:, :, b * S:(b + 1) * S])
            for u in range(B * SE // S):
                copy_T(("ctx", u), ctxT[:, :, u * S:(u + 1) * S])
            dve.wait_ge(*load["rows"].when("all"))
            for name in ("sa0", "ca0"):
                projections(name)
                attention(ATTENTIONS[name])

            def link(ins):
                ins.then_inc(*vec.next())
                dve.wait_ge(*vec.now())

            key = ("router",)
            dve.wait_ge(*a_full.when(key))
            dve.tensor_tensor(lg[:, :, :], a_slot(key)[:, 0:NT * E].rearrange("p (t e) -> p t e", e=E),
                              rb[:, :].unsqueeze(1).to_broadcast([P, NT, E]), ALU.add)\
               .then_inc(*a_free.next(key))
            dve.wait_ge(*a_free.now())
            link(dve.tensor_reduce(small[:, 0, :], lg[:, :, :], AX.X, ALU.max))
            dve.tensor_tensor(lg[:, :, :], lg[:, :, :], small[:, 0, :].unsqueeze(2).to_broadcast([P, NT, E]),
                              ALU.subtract).then_inc(*vec.next("logits"))
            dve.wait_ge(*act_done.when("router_exp"))
            link(dve.tensor_reduce(small[:, 1, :], lg[:, :, :], AX.X, ALU.add))
            link(dve.reciprocal(small[:, 2, :], small[:, 1, :]))
            link(dve.tensor_tensor(lg[:, :, :], lg[:, :, :], small[:, 2, :].unsqueeze(2).to_broadcast([P, NT, E]),
                                   ALU.mult))
            for t in range(NT):
                dve.max(best[:, t, :], lg[:, t, :]).then_inc(*vec.next())
            dve.wait_ge(*vec.now())
            dve.tensor_tensor(small[:, 3, :], best[:, :, 1], best[:, :, 0], ALU.subtract)\
               .then_inc(*vec.next("gap"))
            for t in range(NT):
                dve.max_index(besti[:, t, :], best[:, t, :], lg[:, t, :]).then_inc(*vec.next())
            dve.wait_ge(*vec.now())
            link(dve.tensor_copy(bestf[:, :, :], besti[:, :, :]))
            dve.wait_ge(*act_done.when("gap_exp"))
            link(dve.tensor_scalar(small[:, 4, :], small[:, 3, :], 1.0, None, ALU.add))
            link(dve.reciprocal(small[:, 4, :], small[:, 4, :]))
            link(dve.tensor_tensor(small[:, 5, :], small[:, 3, :], small[:, 4, :], ALU.mult))
            for t in range(NT):
                dve.tensor_scalar(comb[:, t, :], expert_no[:, :], bestf[:, t, 0:1], small[:, 4, t:t + 1],
                                  ALU.is_equal, ALU.mult).then_inc(*vec.next())
                dve.tensor_scalar(comb2[:, t, :], expert_no[:, :], bestf[:, t, 1:2], small[:, 5, t:t + 1],
                                  ALU.is_equal, ALU.mult).then_inc(*vec.next())
            dve.wait_ge(*vec.now())
            dve.tensor_tensor(comb[:, :, :], comb[:, :, :], comb2[:, :, :], ALU.add).then_inc(*vec.next("comb"))
            dve.wait_ge(*a_full.when(("combT",)))
            dve.tensor_copy(combT[:, :], a_slot(("combT",))[0:E, :]).then_inc(*a_free.next(("combT",)))
            for b in range(B):
                key = ("b2", b)
                dve.wait_ge(*a_full.when(key))
                x = xtok[:, b * TB:(b + 1) * TB, :]
                dve.tensor_tensor(x, a_slot(key)[:, :].rearrange("p (t d) -> p t d", t=TB), x, ALU.add)\
                   .then_inc(*a_free.next(key))
            dve.wait_ge(*a_free.now())
            for e in range(E):
                for hf in range(B):
                    key = ("eo", e, hf)
                    dve.wait_ge(*a_full.when(key))
                    if e:
                        dve.wait_ge(*a_free.when(("eo", e - 1, hf)))
                    for t in range(TB):
                        x = xtok[:, hf * TB + t, :]
                        ins = dve.scalar_tensor_tensor(out=x, in0=a_slot(key)[:, t * D:(t + 1) * D],
                                                       scalar=comb[:, hf * TB + t, e:e + 1], in1=x,
                                                       op0=ALU.mult, op1=ALU.add)
                        ins.then_inc(*(a_free.next(key) if t == TB - 1 else vec.next()))
            dve.wait_ge(*a_free.now())
            for b in range(B):
                normalise_rows(b, "moe")
                if b == 0:
                    continue
            for b in range(B):
                copy_T(("turn", b, "moe"), xT[:, :, b * S:(b + 1) * S])

            def mlp(name):
                for hf in range(B):
                    for f in range(FC):
                        key = ("u", name, hf, f)
                        dve.wait_ge(*a_full.when(key))
                        dve.wait_ge(*b_free.when(("g", name, hf, f)))
                        dve.tensor_tensor(hT[hf][:, f, :], a_slot(key)[:, 0:S], gate[:, f % 2, :], ALU.mult)\
                           .then_inc(*a_free.next(key))
                for hf in range(B):
                    key = ("down", name, hf)
                    dve.wait_ge(*a_full.when(key))
                    x = xT[:, :, hf * S:(hf + 1) * S]
                    dve.tensor_tensor(x, a_slot(key)[:, :].rearrange("p (c t) -> p c t", c=DC), x, ALU.add)\
                       .then_inc(*a_free.next(key))
                dve.wait_ge(*a_free.now())

            for name in ("sa1", "ca1"):
                projections(name)
                attention(ATTENTIONS[name])
                dve.wait_ge(*a_free.now())
                mlp(name)
            for b in range(B):
                key = ("out", b)
                dve.wait_ge(*a_full.when(key))
                dve.tensor_copy(xtok[:, b * TB:(b + 1) * TB, :],
                                a_slot(key)[:, :].rearrange("p (t d) -> p t d", t=TB))\
                   .then_inc(*a_free.next(key))

        @block.scalar
        def _(act):
            def exps(a):
                for step in a.steps():
                    if step[0] != "unit":
                        continue
                    _, b, g, kt, j, n = step
                    key = ("unit", a.name, n)
                    w = S - a.queries_from(kt)
                    act.wait_ge(*b_full.when(key))
                    if n >= 4:
                        act.wait_ge(*pv_done.when((a.name, n - 4)))
                    act.activation(probs[:, n % 4, 0:w], b_slot(key)[:, 0:w], ACT.Exp, scale=a.scale)\
                       .then_inc(*b_free.next(key))

            exps(ATTENTIONS["sa0"])
            exps(ATTENTIONS["ca0"])
            act.wait_ge(*vec.when("logits"))
            act.activation(lg[:, :, :], lg[:, :, :], ACT.Exp).then_inc(*act_done.next("router_exp"))
            act.wait_ge(*vec.when("gap"))
            act.activation(small[:, 3, :], small[:, 3, :], ACT.Exp).then_inc(*act_done.next("gap_exp"))
            for e in range(E):
                for hf in range(B):
                    for f in range(FC):
                        key = ("h", e, hf, f)
                        act.wait_ge(*b_full.when(key))
                        if f == 0 and e:
                            act.wait_ge(*a_full.when(("eo", e - 1, hf)))
                        act.activation(hT[hf][:, f, :], b_slot(key)[:, :], ACT.Gelu, bias=b1T[:, e, f:f + 1])\
                           .then_inc(*b_free.next(key))

            def silus(name):
                for hf in range(B):
                    for f in range(FC):
                        key = ("g", name, hf, f)
                        act.wait_ge(*b_full.when(key))
                        n = hf * FC + f
                        if n >= 2:
                            act.wait_ge(*a_free.when(("u", name, (n - 2) // FC, (n - 2) % FC)))
                        act.activation(gate[:, f % 2, :], b_slot(key)[:, :], ACT.Silu).then_inc(*b_free.next(key))

            exps(ATTENTIONS["sa1"])
            silus("sa1")
            exps(ATTENTIONS["ca1"])
            silus("ca1")

        @block.gpsimd
        def _(pool):
            for t, v in ((ident, 0.0), (identb, 0.0), (mask_q, 0.0), (mask_k, 0.0)):
                pool.memset(t[:, :], v).then_inc(*pool_done.next())
            pool.memset(onesb[:, :], 1.0).then_inc(*pool_done.next())
            pool.memset(onesf[:, :], 1.0).then_inc(*pool_done.next())
            pool.memset(minus_half[:, :], -0.5).then_inc(*pool_done.next())
            pool.iota(expert_no[:, :], pattern=[[1, E]], base=0, channel_multiplier=0,
                      allow_small_or_imprecise_dtypes=True).then_inc(*pool_done.next())
            pool.wait_ge(*pool_done.now())
            for m in (ident, identb):
                pool.affine_select(out=m[:, :], in_=m[:, :], compare_op=ALU.not_equal, fill=1.0, base=0,
                                   pattern=[[-1, P]], channel_multiplier=1).then_inc(*pool_done.next())
            pool.affine_select(out=mask_q[:, :], in_=mask_q[:, :], compare_op=ALU.is_ge, fill=NEG, base=0,
                               pattern=[[-1, P]], channel_multiplier=1).then_inc(*pool_done.next())
            pool.affine_select(out=mask_k[:, :], in_=mask_k[:, :], compare_op=ALU.is_ge, fill=NEG, base=0,
                               pattern=[[1, P]], channel_multiplier=-1).then_inc(*pool_done.next())
            pool.memset(vx[:, :], 1.0).then_inc(*pool_done.next("constants"))
            pool.wait_ge(*a_full.when(("ctx", B * SE // S - 1)))
            pool.memset(arena[96:99, 16384:49152], 1.0).then_inc(*pool_done.next("shift_ones"))

            def add_bo(name):
                if name == "sa0":
                    pool.wait_ge(*load["rows"].when("all"))
                    pool.wait_ge(*a_full.when(("x", B - 1)))
                else:
                    pool.wait_ge(*a_full.when(("turn", B - 1, "sa0")))
                pool.wait_ge(*pool_done.now())
                r = row[name[:2] + "_bo"][:, :].unsqueeze(1).to_broadcast([P, NT, D])
                pool.tensor_tensor(xtok[:, :, :], xtok[:, :, :], r, ALU.add).then_inc(*pool_done.next(("bo", name)))

            def layernorm(name, ln, b):
                pool.wait_ge(*vec.when(("var", name, b)))
                pool.tensor_tensor(rstd[:, :], var[:, :], minus_half[:, :], ALU.pow)\
                    .then_inc(*pool_done.next(("rstd", name, b)))
                pool.wait_ge(*vec.when(("centred", name, b)))
                x = xtok[:, b * TB:(b + 1) * TB, :]
                pool.tensor_tensor(x, x, row[ln + "_g"][:, :].unsqueeze(1).to_broadcast([P, TB, D]), ALU.mult)\
                    .then_inc(*pool_done.next())
                pool.wait_ge(*pool_done.now())
                pool.tensor_tensor(x, x, row[ln + "_b"][:, :].unsqueeze(1).to_broadcast([P, TB, D]), ALU.add)\
                    .then_inc(*pool_done.next(("ln", name, b)))

            for name, ln in (("sa0", "ln1"), ("ca0", "ln2")):
                add_bo(name)
                for b in range(B):
                    layernorm(name, ln, b)
            for b in range(B):
                layernorm("moe", "ln3", b)
            for b in range(B):
                pool.wait_ge(*a_full.when(("eo", E - 1, B - 1)))
                pool.memset(m_rows(b), 0.0).then_inc(*pool_done.next(("m_zero", "sa1")))
            pool.wait_ge(*a_full.when(("down", "sa1", B - 1)))
            for b in range(B):
                pool.memset(m_rows(b), 0.0).then_inc(*pool_done.next(("m_zero", "ca1")))

        @block.sync
        def _(sp):
            def loads(name, pairs):
                for dst, src in pairs:
                    sp.dma_start(dst, src).then_inc(*load[name].next("all", 16))

            def weights(name):
                pre = "L%s_xattn_%s_w" % (name[2], name[:2])
                i = att_index[name]
                return [(wset[i % 2][:, n], io[pre + c].rearrange("(c p) n -> p c n", p=P))
                        for n, c in enumerate("qkvo")]

            loads("x", [(xtok[:, b * TB:(b + 1) * TB, :], io["x"][b].rearrange("(t p) d -> p t d", p=P))
                        for b in range(B)])
            loads("wsa0", weights("sa0"))
            loads("ctx", [(ctx_in[:, b * 8:(b + 1) * 8, :], io["ctx_1024"][b].rearrange("(t p) d -> p t d", p=P))
                          for b in range(B)])
            L0 = "L0_xattn_"
            with nc.allow_non_contiguous_dma(reason="biases onto the partitions, a few kilobytes"):
                loads("rows", [(biasT[n][:, :], io[L0 + n].rearrange("(c p) -> p c", p=P)) for n in biasT]
                      + [(b1T[:, :, :], io[L0 + "e_b1"].rearrange("e (f p) -> p e f", p=P))])
            loads("rows", [(row[n][:, :], io[L0 + n].partition_broadcast(P)) for n in row]
                  + [(rb[:, :], io[L0 + "router_b"].partition_broadcast(P)),
                     (b2[:, :], io[L0 + "e_b2"]),
                     (rw[:, :, :], io[L0 + "router_w"].rearrange("(c p) n -> p c n", p=P))])
            loads("wca0", weights("ca0"))

            def stack(name):
                a = ATTENTIONS[name]
                ai = att_index[name]
                jobs = [j for j in split_jobs if j[0] == name]
                if name == "ca0":
                    sp.wait_ge(*a_free.when(("heads", B - 1, "sa0")))
                if name == "ca1":
                    sp.wait_ge(*a_full.when(("down", "sa1", B - 1)))
                for _, which, u in jobs:
                    i = split_no[name, which, u]
                    scr = (scratch_q if which == "q" else scratch_k)[ai]
                    sp.wait_ge(*vec.when(("split", i)))
                    for c in range(DC):
                        sp.dma_start(scr[:, c * P:(c + 1) * P, u * S:(u + 1) * S].rearrange("r p t -> p r t"),
                                     parts[:, i % 2, c]).then_inc(*part_out[i % 2].next(i, 16))
                    sp.wait_ge(*part_out[i % 2].now())
                    per = a.nk // S if which == "k" else 1
                    b, t0 = u // per, (u % per) * S
                    if name == "sa0" and i == 0:
                        sp.wait_ge(*a_full.when(("ctx", B * SE // S - 1)))
                    if name == "sa1":
                        sp.wait_ge(*a_full.when(("eo", E - 1, B - 1)))
                    order = QUERY_PARTS if which == "q" else KEY_PARTS
                    for r, part in enumerate(order):
                        src = scr[part, :, u * S:(u + 1) * S].rearrange("(h d) t -> d h t", d=a.HD)
                        if a.layer == 0:
                            st = (q_stack if which == "q" else k_stack)(a, b)
                            dst = st[r * 16:(r + 1) * 16, :, t0:t0 + S]
                        elif which == "q":
                            dst = q_stack(a, b, r // 2)[(r % 2) * 64:(r % 2) * 64 + 64, :, t0:t0 + S]
                        else:
                            if r in (2, 3):
                                continue
                            dst = k_stack(a, b, 0 if r < 2 else 1)[(r % 2) * 64:(r % 2) * 64 + 64, :, t0:t0 + S]
                        sp.dma_start(dst, src).then_inc(*stack_in[ai].next("all", 16))

            def shifts(name):
                a = ATTENTIONS[name]
                for gi, (b, g) in enumerate(a.groups):
                    sp.wait_ge(*vec.when(("shift", name, gi)))
                    if gi == 0:
                        sp.wait_ge(*pool_done.when(("m_zero", name) if a.layer else "shift_ones"))
                    for r in range(3):
                        rows = m_rows(b) if a.layer else q_stack(a, b)
                        at = r if a.layer else 96 + r
                        dst = rows[at:at + 1, g * a.G:(g + 1) * a.G, :]
                        sp.dma_start(dst, shiftb[0:a.G, r, :])\
                          .then_inc(*shift_in[gi % 2].next((name, gi), 16))

            stack("sa0")
            shifts("sa0")
            stack("ca0")
            sp.wait_ge(*a_free.when(("proj", B - 1, "sa0")))
            loads("wsa1", weights("sa1"))
            shifts("ca0")
            sp.wait_ge(*a_free.when(("proj", B - 1, "ca0")))
            loads("wca1", weights("ca1"))
            for e in range(E):
                if e >= 2:
                    sp.wait_ge(*a_full.when(("eo", e - 2, B - 1)))
                sp.dma_start(w1[e % 2], io[L0 + "e_w1"][e].rearrange("(c p) f -> p c f", p=P))\
                  .then_inc(*w_load[e % 2].next(e, 16))
                sp.dma_start(w2[e % 2], io[L0 + "e_w2"][e].rearrange("(f p) n -> p f n", p=P))\
                  .then_inc(*w_load[e % 2].next(e, 16))

            def mlp_weights(name):
                pre = "L1_xattn_" + name[:2] + "mlp_w"
                loads("mlp_" + name, [
                    (mlp_w[0].rearrange("p (c f) -> p c f", c=DC), io[pre + "g"].rearrange("(c p) f -> p c f", p=P)),
                    (mlp_w[1].rearrange("p (c f) -> p c f", c=DC), io[pre + "u"].rearrange("(c p) f -> p c f", p=P)),
                    (mlp_w[2].rearrange("p (c n) -> p c n", c=FC), io[pre + "d"].rearrange("(f p) n -> p f n", p=P))])

            stack("sa1")
            shifts("sa1")
            sp.wait_ge(*a_free.when(("heads", B - 1, "sa1")))
            mlp_weights("sa1")
            stack("ca1")
            shifts("ca1")
            sp.wait_ge(*a_free.when(("down", "sa1", B - 1)))
            mlp_weights("ca1")
            for b in range(B):
                sp.wait_ge(*a_free.when(("out", b)))
                sp.dma_start(io["out"][b].rearrange("(t p) d -> p t d", p=P), xtok[:, b * TB:(b + 1) * TB, :])\
                  .then_inc(*stored.next("out", 16))
            sp.wait_ge(*stored.now())

    seen = {n: s.seen for n, s in signals.items()}
    seen["_a_turn"] = {k: i % 2 for i, k in enumerate(a_keys)}
    seen["_b_turn"] = {k: i % 2 for i, k in enumerate(b_keys)}
    return seen


def kernel(**inputs):
    import numpy as _np
    import concourse.bacc as _bacc
    from concourse import mybir as _mybir
    from concourse.bass_utils import run_bass_kernel_spmd as _run

    arrays = {f"in_{name}": _np.ascontiguousarray(a) for name, a in inputs.items()}

    def build(known):
        nc = _bacc.Bacc("TRN2", target_bir_lowering=False, num_devices=1)
        io = {name[3:]: nc.dram_tensor(name, a.shape, _mybir.dt.from_np(a.dtype), kind="ExternalInput").ap()
              for name, a in arrays.items()}
        io["out"] = nc.dram_tensor("out", (B, S, D), F32, kind="ExternalOutput").ap()
        return nc, program(nc, io, known)

    _, known = build(None)
    nc, _ = build(known)
    r = _run(nc, [arrays], core_ids=[0])
    return r.results[0]["out"]
```

```python
from contextlib import ExitStack

import numpy as np
from concourse import mybir
from concourse.bass import DynSlice, IndirectOffsetOnAxis

F32 = mybir.dt.float32
BF16 = mybir.dt.bfloat16
U32 = mybir.dt.uint32
ALU = mybir.AluOpType
ACT = mybir.ActivationFunctionType
AX = mybir.AxisListType

P = 128
B, S, D = 2, 512, 256
SE = 1024
T = B * S
DC = D // P
TB = S // P
NT = T // P
FF = 1024
FC = FF // P
E = 8
NEG = -1.0e30
EPS = 1e-5
TOP = 2
SLOT = 256
SLOTS = (TOP * T + E * (SLOT - 1)) // SLOT
ST = SLOT // P


class Signal:

    def __init__(self, sem, known):
        self.sem, self.known, self.count, self.seen = sem, known, 0, {}

    def next(self, label=None, by=1):
        self.count += by
        if label is not None:
            self.seen[label] = self.count
        return self.sem, by

    def when(self, label):
        return self.sem, (self.known[label] if self.known is not None else 1)

    def now(self):
        return self.sem, self.count


class Attention:

    def __init__(self, name, heads, nk, causal, group, split_rows, layer, lead):
        self.name, self.H, self.nk, self.causal, self.G = name, heads, nk, causal, group
        self.HD = D // heads
        self.scale = 1.0 / float(np.sqrt(self.HD))
        self.KT = nk // P
        self.layer = layer
        self.groups = [(b, g) for b in range(B) for g in range(heads // group)]
        self.heads = {(b, g): [g * group + j for j in range(group)] for b, g in self.groups}
        self.lead = lead
        self.per_job = 2 if nk == S else 1
        self.early = None

    def queries_from(self, kt):
        return kt * P if self.causal else 0

    def keys_to(self, qt):
        return (qt + 1) * P if self.causal else self.nk

    def steps(self):
        first = []
        for b, g in self.groups:
            first += [("max", b, h, qt) for h in self.heads[b, g][::self.per_job] for qt in range(TB)]
            first.append(("shift", b, g))
        units = []
        for b, g in self.groups:
            units += [("unit", b, g, kt, j) for kt in range(self.KT) for j in range(self.G)]
        per_group = self.KT * self.G
        jobs = self.G // self.per_job * TB + 1
        out, at, held = [], 0, []
        early = [(u, c) for u in range(B * SE // S) for c in range(DC)]
        for n, u in enumerate(units):
            want = min(len(first), int(np.ceil((n + 1) * jobs / per_group)) + jobs + self.lead)
            while at < want:
                out.append(first[at])
                at += 1
            out.append(u + (n,))
            if self.early and n % 8 == 6 and early:
                if n not in (70, 78, 86):
                    out.append(("early", 0) + early.pop(0))
            due = sorted((x for x in held if x[0] <= n), key=lambda x: x[1][0] != "evict")
            held = [x for x in held if x[0] > n]
            out += [x[1] for x in due]
            if (n + 1) % per_group == 0:
                b, g = u[1], u[2]
                held.append((n + 2, ("evict", b, g)))
                held.append((n + 4, ("norm", b, g)))
                if g == self.H // self.G - 1:
                    held.append((n + 8, ("heads", b)))
                    held.append((n + 11, ("proj", b)))
                    if self.layer == 0:
                        held.append((n + 14, ("ln", b)))
                        held.append((n + 26, ("turn", b)))
        out += first[at:]
        out += [x[1] for x in held]
        return out


ATTENTIONS = {
    "sa0": Attention("sa0", 16, S, True, 4, 96, 0, 4),
    "ca0": Attention("ca0", 16, SE, False, 4, 96, 0, 4),
    "sa1": Attention("sa1", 4, S, False, 2, 128, 1, 4),
    "ca1": Attention("ca1", 4, SE, False, 2, 128, 1, 4),
}
QUERY_PARTS = (0, 0, 1, 1, 0, 2)
KEY_PARTS = (0, 1, 0, 1, 2, 0)
ATTENTIONS["sa0"].early = "ca0"


def split_order():
    def of(name, which, us):
        return [(name, which, u, c) for u in us for c in range(DC)]

    out = []
    for u in range(B):
        out += of("sa0", "k", [u]) + of("sa0", "q", [u])
    out += of("ca0", "k", range(B * SE // S)) + of("ca0", "q", range(B)) + of("ca1", "k", range(B * SE // S))
    for u in range(B):
        out += of("sa1", "k", [u]) + of("sa1", "q", [u])
    return out + of("ca1", "q", range(B))


def program(nc, io, known):
    ctx = ExitStack()
    signals = {}

    with ctx:
        def sb(name, shape, dt=F32):
            return ctx.enter_context(nc.sbuf_tensor(name, shape, dt))

        def signal(name):
            s = Signal(ctx.enter_context(nc.semaphore(name)), None if known is None else known[name])
            signals[name] = s
            return s

        ident = sb("ident", [P, P])
        identb = sb("identb", [P, P], BF16)
        mask_q = sb("mask_q", [P, P], BF16)
        mask_k = sb("mask_k", [P, P], BF16)
        onesb = sb("onesb", [P, P], BF16)
        onesf = sb("onesf", [P, 32])
        minus_half = sb("minus_half", [P, TB])
        expert_no = sb("expert_no", [P, E])
        xT = sb("xT", [P, DC, T])
        xtok = sb("xtok", [P, NT, D])
        ctxT = sb("ctxT", [P, DC, B * SE])
        wset = [sb(f"wset{i}", [P, 4, DC, D]) for i in range(2)]
        arena = sb("arena", [P, 49152], BF16)
        vx = sb("vx", [P, 16 * 272 + 16])
        exact = sb("exact", [P, DC, S])
        parts = sb("parts", [P, 2, 3, S], BF16)
        probs = sb("probs", [P, 4, S])
        sums = sb("sums", [P, 2, S])
        dens = sb("dens", [64, S])
        otok = sb("otok", [P, TB, D])
        oT = exact
        negmax = sb("negmax", [P, 2, TB, 4])
        shift = sb("shift", [4, S])
        shiftb = sb("shiftb", [4, 3, S], BF16)
        rden = sb("rden", [P, TB, 4])
        biasT = {n: sb(f"biasT_{n}", [P, DC]) for n in ("sa_bq", "sa_bk", "ca_bq", "ca_bk")}
        row = {n: sb(f"row_{n}", [P, D]) for n in
               ("sa_bv", "sa_bo", "ca_bv", "ca_bo", "ln1_g", "ln1_b", "ln2_g", "ln2_b", "ln3_g", "ln3_b")}
        stats = sb("stats", [P, TB, 6])
        mv = sb("mv", [P, TB, 2])
        var = sb("var", [P, TB])
        rstd = sb("rstd", [P, TB])
        rw = sb("rw", [P, DC, E])
        rb = sb("rb", [P, E])
        b1T = sb("b1T", [P, E, FC])
        b2 = dens[0:E, 0:D]
        small = sb("small", [P, 6, NT])
        below = sb("below", [P, P], BF16)
        placed = sb("placed", [P, TOP, NT])
        place_no = sb("place_no", [P, TOP, NT], U32)
        slot_no = sb("slot_no", [1, SLOTS])
        slot_ef = sb("slot_ef", [1, SLOTS])
        slot_e = sb("slot_e", [1, SLOTS], U32)
        def table(n, *shape, at=[0]):
            view = vx[:, at[0]:at[0] + n]
            at[0] += n
            names = "abc"[:len(shape)]
            return view.rearrange("p (%s) -> p %s" % (" ".join(names), " ".join(names)), **dict(zip(names, shape)))

        lg = table(NT * E, NT, E)
        best = table(NT * 8, NT, 8)
        besti = table(NT * 8, NT, 8).bitcast(U32)
        bestf = table(NT * 8, NT, 8)
        comb = table(NT * E, NT, E)
        chosen = table(TOP * NT * E, TOP, NT, E)
        chosenb = table(NT * E // 2, NT * E // 2).bitcast(BF16).rearrange("p (t e) -> p t e", e=E)
        rank = table((NT + 1) * E, NT + 1, E)
        ends = table(4 * (4 + E), 4, 4 + E)
        place = table(NT * E, NT, E)
        past = table(SLOTS * E, SLOTS, E)[0:1]
        combT = otok[0:E, :, :].rearrange("e t d -> e (t d)")

        a_bank = [ctx.enter_context(nc.psum_tensor(f"a_bank{i}", [P, 2 * 512], F32)) for i in range(2)]
        b_bank = [ctx.enter_context(nc.psum_tensor(f"b_bank{i}", [P, 512], F32)) for i in range(2)]
        o_bank = [ctx.enter_context(nc.psum_tensor(f"o_bank{i}", [P, 512], F32)) for i in range(2)]

        arena_f = arena[:, :].bitcast(F32)
        ctx_in = arena_f[:, 8192:8192 + 16 * D].rearrange("p (t d) -> p t d", t=16)
        w1 = [arena_f[:, 2048 * i:2048 * (i + 1)].rearrange("p (c f) -> p c f", c=DC) for i in range(2)]
        w2 = [arena_f[:, 4096 + 2048 * i:4096 + 2048 * (i + 1)].rearrange("p (c n) -> p c n", c=FC)
              for i in range(2)]
        hT = [arena_f[:, 8192 + 4096 * i:8192 + 4096 * (i + 1)].rearrange("p (c t) -> p c t", c=FC)
              for i in range(2)]
        hS = [arena_f[:, 8192 + 2048 * i:8192 + 2048 * (i + 1)].rearrange("p (c t) -> p c t", c=FC)
              for i in range(2)]
        xS = [arena_f[:, 16384 + 512 * i:16384 + 512 * (i + 1)].rearrange("p (t d) -> p t d", t=ST)
              for i in range(2)]
        yS = [arena_f[:, 17408 + 512 * i:17408 + 512 * (i + 1)].rearrange("p (t d) -> p t d", t=ST)
              for i in range(2)]
        xST = [arena_f[:, 18432 + 512 * i:18432 + 512 * (i + 1)].rearrange("p (c t) -> p c t", c=DC)
               for i in range(2)]
        back = arena_f[:, 19456:19456 + TOP * NT * D].rearrange("p (k t d) -> p k t d", k=TOP, t=NT)
        b1S = [arena_f[:, 23552 + 8 * i:23552 + 8 * (i + 1)] for i in range(2)]
        zeros = arena_f[:, 12288:12288 + ST * D].rearrange("p (t d) -> p t d", t=ST)
        mlp_w = [arena_f[:, 16384 + 2048 * i:16384 + 2048 * (i + 1)] for i in range(3)]
        gate = arena_f[:, 22528:22528 + 1024].rearrange("p (i t) -> p i t", i=2)

        def q_stack(a, b, i=0):
            n = a.H * S
            base = (b * 3 + i) * n if a.layer else b * n
            return arena[:, base:base + n].rearrange("p (h t) -> p h t", h=a.H)

        def k_stack(a, b, i=0):
            n = a.H * a.nk
            if a.layer:
                base = 12288 + (b * 2 + i) * n
            else:
                base = (32768 if a.causal else 16384) + b * n
            return arena[:, base:base + n].rearrange("p (h t) -> p h t", h=a.H)

        def m_rows(b):
            return arena[:, 28672 + b * 2048:28672 + (b + 1) * 2048].rearrange("p (h t) -> p h t", h=4)

        def v_head(a, tile, h):
            if a.layer:
                return vx[:, tile * D + h * 64:tile * D + h * 64 + 64]
            return vx[:, tile * 272 + h * 17:tile * 272 + h * 17 + 32]

        scratch_q = nc.dram_tensor("scratch_q", (4, 3, D, T), BF16, kind="Internal").ap()
        sent = nc.dram_tensor("sent", (SLOTS * SLOT, D), F32, kind="Internal").ap()
        computed = nc.dram_tensor("computed", (SLOTS * SLOT, D), F32, kind="Internal").ap()
        scratch_k = nc.dram_tensor("scratch_k", (4, 3, D, B * SE), BF16, kind="Internal").ap()

        a_full = signal("a_full")
        b_full = signal("b_full")
        pv_done = signal("pv_done")
        pe_past = signal("pe_past")
        a_free = signal("a_free")
        vec = signal("vec")
        b_free = signal("b_free")
        act_done = signal("act_done")
        pool_done = signal("pool_done")
        load = {n: signal("load_" + n) for n in
                ("x", "ctx", "wsa0", "wca0", "wsa1", "wca1", "rows", "mlp_sa1", "mlp_ca1")}
        w1_load = [signal(f"load_w1_{i}") for i in range(2)]
        w2_load = [signal(f"load_w2_{i}") for i in range(2)]
        part_out = [signal(f"part_out{i}") for i in range(2)]
        stack_in = {(n, b): signal(f"stack_in_{n}_{b}") for n in ATTENTIONS for b in range(B)}
        shift_in = [signal(f"shift_in{i}") for i in range(2)]
        stored = signal("stored")
        zeroed = signal("zeroed")
        sent_out = signal("sent_out")
        b1_load = [signal(f"b1_load{i}") for i in range(2)]
        slot_in = [signal(f"slot_in{i}") for i in range(2)]
        slot_out = [signal(f"slot_out{i}") for i in range(2)]
        back_in = [signal(f"back_in{i}") for i in range(B)]

        att_index = {n: i for i, n in enumerate(ATTENTIONS)}
        split_no = {j: i for i, j in enumerate(split_order())}

        a_keys, b_keys = [], []
        a_turn = {} if known is None else known["_a_turn"]
        b_turn = {} if known is None else known["_b_turn"]

        def a_slot(key):
            return a_bank[a_turn.get(key, 0)]

        def b_slot(key):
            return b_bank[b_turn.get(key, 0)]

        block = ctx.enter_context(nc.Block())

        @block.tensor
        def _(pe):
            def take_a(key):
                if len(a_keys) >= 2:
                    pe.wait_ge(*a_free.when(a_keys[-2]))
                a_keys.append(key)
                return a_bank[(len(a_keys) - 1) % 2]

            def take_b(key):
                if len(b_keys) >= 2:
                    pe.wait_ge(*b_free.when(b_keys[-2]))
                b_keys.append(key)
                return b_bank[(len(b_keys) - 1) % 2]

            def turn(key, tiles):
                pair = take_a(key)
                for t, tile in enumerate(tiles):
                    for c in range(DC):
                        mm = pe.transpose(pair[:, c * S + t * P:c * S + (t + 1) * P],
                                          tile[:, c * P:(c + 1) * P], ident[:, :])
                mm.then_inc(*a_full.next(key))

            def project_T(key, w, src, at):
                pair = take_a(key)
                for dc in range(DC):
                    for c in range(DC):
                        mm = pe.matmul(pair[:, dc * S:(dc + 1) * S], w[:, c, dc * P:(dc + 1) * P],
                                       src[:, c, at:at + S], start=(c == 0), stop=(c == DC - 1))
                mm.then_inc(*a_full.next(key))

            def project_chunk(name, which, u, c):
                a = ATTENTIONS[name]
                w = wset[att_index[name] % 2][:, "qk".index(which)]
                src = xT if which == "q" or a.nk == S else ctxT
                pair = take_a(("split", name, which, u, c))
                for k in range(DC):
                    mm = pe.matmul(pair[:, 0:S], w[:, k, c * P:(c + 1) * P], src[:, k, u * S:(u + 1) * S],
                                   start=(k == 0), stop=(k == DC - 1))
                mm.then_inc(*a_full.next(("split", name, which, u, c)))

            def project_tok(key, w, src, at):
                pair = take_a(key)
                for t in range(TB):
                    for c in range(DC):
                        mm = pe.matmul(pair[:, t * D:(t + 1) * D], src[:, c, at + t * P:at + (t + 1) * P],
                                       w[:, c, :], start=(c == 0), stop=(c == DC - 1))
                mm.then_inc(*a_full.next(key))

            def projections(a, w):
                for job in split_order():
                    if job[0] == a.name and not (job[1] == "k" and a.nk == SE):
                        project_chunk(*job)
                if a.name == "sa0":
                    context()
                kv = xT if a.nk == S else ctxT
                for u in range(B * a.nk // S):
                    project_tok(("v", a.name, u), w[:, 2], kv, u * S)

            def context():
                pe.wait_ge(*load["ctx"].when("all"))
                for u in range(B * SE // S):
                    turn(("ctx", u), [ctx_in[:, u * TB + t, :] for t in range(TB)])

            def score_passes(a, b, h, queries, keys, with_shift):
                out = []
                if not a.layer:
                    rows = 99 if with_shift else 96
                    out.append((q_stack(a, b)[0:rows, h, queries], k_stack(a, b)[0:rows, h, keys]))
                else:
                    for qi, ki in ((0, 0), (1, 0), (2, 1)):
                        out.append((q_stack(a, b, qi)[:, h, queries], k_stack(a, b, ki)[:, h, keys]))
                    if with_shift:
                        out.append((m_rows(b)[:, h, queries], onesb[:, 0:P]))
                return out

            def attention(a):
                pending = []

                def product(item):
                    b, g, kt, j, n = item
                    h = g * a.G + j
                    q0 = a.queries_from(kt)
                    gi = a.groups.index((b, g))
                    tile = b * a.KT + kt
                    pe.wait_ge(*b_free.when(("unit", a.name, n)))
                    first = kt == 0 and j == 0
                    if first:
                        if a.layer == 0 and gi >= 2:
                            pe.wait_ge(*vec.when(("evict", a.name, gi - 2)))
                        if a.layer == 1 and gi >= 1:
                            pe.wait_ge(*vec.when(("evict", a.name, gi - 1)))
                        if gi == 0:
                            pe.wait_ge(*a_free.when(("v", a.name, B * a.nk // S - 1)))
                    p = probs[:, n % 4, 0:S - q0]
                    if a.layer == 0:
                        bank = o_bank[gi % 2]
                        mm = pe.matmul(bank[32 * j:32 * j + 32, q0:S], v_head(a, tile, h), p,
                                       start=(kt == 0), stop=(kt == a.KT - 1), tile_position=(0, 32 * j))
                    else:
                        pe.matmul(o_bank[0][64 * j:64 * j + 64, :], v_head(a, tile, h), p,
                                  start=(kt == 0), stop=(kt == a.KT - 1), tile_position=(0, 64 * j))
                        mm = pe.matmul(o_bank[1][32 * j:32 * j + 32, :], onesf[:, :], p,
                                       start=(kt == 0), stop=(kt == a.KT - 1), tile_position=(0, 32 * j))
                    mm.then_inc(*pv_done.next((a.name, n)))

                stacks_waited = set()
                for step in a.steps():
                    kind, b = step[0], step[1]
                    if step == ("evict",) + a.groups[-1]:
                        while pending:
                            product(pending.pop(0))
                    if kind == "max":
                        _, b, h, qt = step
                        if b not in stacks_waited:
                            stacks_waited.add(b)
                            pe.wait_ge(*stack_in[a.name, b].when("all"))
                        pair = take_a(step + (a.name,))
                        nk = a.keys_to(qt)
                        for hh in range(a.per_job):
                            for k0 in range(0, nk, 512):
                                n = min(512, nk - k0)
                                at = hh * S + k0
                                ps = score_passes(a, b, h + hh, slice(qt * P, (qt + 1) * P), slice(k0, k0 + n),
                                                  False)
                                for i, (q, k) in enumerate(ps):
                                    mm = pe.matmul(pair[:, at:at + n], q, k, start=(i == 0),
                                                   stop=(i == len(ps) - 1 and not a.causal))
                            if a.causal:
                                at = hh * S + qt * P
                                mm = pe.matmul(pair[:, at:at + P], identb[:, :], mask_q[:, :],
                                               start=False, stop=True)
                        mm.then_inc(*a_full.next(step + (a.name,)))
                    elif kind == "shift":
                        _, b, g = step
                        gi = a.groups.index((b, g))
                        pair = take_a(step + (a.name,))
                        for h in a.heads[b, g][::a.per_job]:
                            for qt in range(TB):
                                last = ("max", b, h, qt, a.name)
                        pe.wait_ge(*a_free.when(last))
                        for qt in range(TB):
                            mm = pe.transpose(pair[0:a.G, qt * P:(qt + 1) * P],
                                              negmax[:, gi % 2, qt, 0:a.G], ident[:, :])
                        mm.then_inc(*a_full.next(step + (a.name,)))
                    elif kind == "unit":
                        _, b, g, kt, j, n = step
                        h = g * a.G + j
                        q0 = a.queries_from(kt)
                        key = ("unit", a.name, n)
                        if kt == 0 and j == 0:
                            gi = a.groups.index((b, g))
                            pe.wait_ge(*shift_in[gi % 2].when((a.name, gi)))
                        bank = take_b(key)
                        ps = score_passes(a, b, h, slice(q0, S), slice(kt * P, (kt + 1) * P), True)
                        for i, (q, k) in enumerate(ps):
                            mm = pe.matmul(bank[:, 0:S - q0], k, q, start=(i == 0),
                                           stop=(i == len(ps) - 1 and not a.causal))
                        if a.causal:
                            mm = pe.matmul(bank[:, 0:P], identb[:, :], mask_k[:, :], start=False, stop=True)
                        mm.then_inc(*b_full.next(key))
                        pending.append(step[1:])
                        if len(pending) > 2:
                            product(pending.pop(0))
                    elif kind == "early":
                        if step[2:] == (0, 0):
                            pe.wait_ge(*load["w" + a.early].when("all"))
                        project_chunk(a.early, "k", *step[2:])
                    elif kind == "norm":
                        _, b, g = step
                        gi = a.groups.index((b, g))
                        pe.wait_ge(*vec.when(("evict", a.name, gi)))
                        pair = take_a(step + (a.name,))
                        src = sums[:, gi % 2, :]
                        for qt in range(TB):
                            mm = pe.transpose(pair[:, qt * P:(qt + 1) * P], src[:, qt * P:(qt + 1) * P],
                                              ident[:, :])
                        if a.layer:
                            for qt in range(TB):
                                mm = pe.transpose(pair[:, 512 + qt * 64:512 + (qt + 1) * 64],
                                                  dens[:, qt * P:(qt + 1) * P], ident[0:64, 0:64])
                        mm.then_inc(*a_full.next(step + (a.name,)))
                    elif kind == "heads":
                        pe.wait_ge(*a_free.when(("norm", b, a.H // a.G - 1, a.name)))
                        turn(step + (a.name,), [otok[:, t, :] for t in range(TB)])
                    elif kind == "proj":
                        pe.wait_ge(*a_free.when(("heads", b, a.name)))
                        w = wset[att_index[a.name] % 2][:, 3]
                        if a.layer:
                            project_T(step + (a.name,), w, oT, 0)
                        else:
                            project_tok(step + (a.name,), w, oT, 0)
                    elif kind == "turn":
                        pe.wait_ge(*pool_done.when(("ln", a.name, b)))
                        turn(step + (a.name,), [xtok[:, b * TB + t, :] for t in range(TB)])
                while pending:
                    product(pending.pop(0))

            pe.wait_ge(*pool_done.when("constants"))
            pe.wait_ge(*load["x"].when("all"))
            for b in range(B):
                turn(("x", b), [xtok[:, b * TB + t, :] for t in range(TB)])
            pe.wait_ge(*a_free.when(("x", B - 1)))

            def attend(name):
                a = ATTENTIONS[name]
                pe.wait_ge(*load["w" + name].when("all"))
                projections(a, wset[att_index[name] % 2])
                attention(a)
                pe.wait_ge(*a_free.when(a_keys[-1]))

            attend("sa0")
            attend("ca0")

            key = ("router",)
            pair = take_a(key)
            pe.wait_ge(*load["rows"].when("all"))
            for t in range(NT):
                for c in range(DC):
                    mm = pe.matmul(pair[:, t * E:(t + 1) * E], xT[:, c, t * P:(t + 1) * P], rw[:, c, :],
                                   start=(c == 0), stop=(c == DC - 1))
            mm.then_inc(*a_full.next(key))

            def slot_turn(s):
                pair = take_a(("xs", s))
                pe.wait_ge(*slot_in[s % 2].when(s))
                for t in range(ST):
                    for c in range(DC):
                        mm = pe.transpose(pair[:, c * SLOT + t * P:c * SLOT + (t + 1) * P],
                                          xS[s % 2][:, t, c * P:(c + 1) * P], ident[:, :])
                mm.then_inc(*a_full.next(("xs", s)))

            def slot_hidden(s):
                pe.wait_ge(*w1_load[s % 2].when(s))
                pe.wait_ge(*a_free.when(("xs", s)))
                for f in range(FC):
                    bank = take_b(("h", s, f))
                    for c in range(DC):
                        mm = pe.matmul(bank[:, 0:SLOT], w1[s % 2][:, c, f * P:(f + 1) * P],
                                       xST[s % 2][:, c, :], start=(c == 0), stop=(c == DC - 1))
                    mm.then_inc(*b_full.next(("h", s, f)))

            def slot_result(s):
                pair = take_a(("eo", s))
                pe.wait_ge(*b_free.when(("h", s, FC - 1)))
                pe.wait_ge(*w2_load[s % 2].when(s))
                for t in range(ST):
                    for f in range(FC):
                        mm = pe.matmul(pair[:, t * D:(t + 1) * D], hS[s % 2][:, f, t * P:(t + 1) * P],
                                       w2[s % 2][:, f, :], start=(f == 0), stop=(f == FC - 1))
                mm.then_inc(*a_full.next(("eo", s)))

            def ranks():
                pair = take_a(("rank",))
                pe.wait_ge(*vec.when("chosen"))
                for t in range(NT):
                    pe.matmul(pair[:, (t + 1) * E:(NT + 1) * E], onesb[:, :],
                              chosenb[:, t, :].unsqueeze(1).to_broadcast([P, NT - t, E]),
                              start=(t == 0), stop=False, skip_group_check=True)
                pe.matmul(pair[:, 0:NT * E], below[:, :], chosenb[:, :, :].rearrange("p t e -> p (t e)"),
                          start=False, stop=True, skip_group_check=True).then_inc(*a_full.next(("rank",)))

            def share_of_b2():
                pair = take_a(("combT",))
                pe.wait_ge(*vec.when("comb"))
                for t in range(NT):
                    mm = pe.transpose(pair[0:E, t * P:(t + 1) * P], comb[:, t, :], ident[:, :])
                mm.then_inc(*a_full.next(("combT",)))
                pe.wait_ge(*a_free.when(("combT",)))
                for b in range(B):
                    pair = take_a(("b2", b))
                    for t in range(TB):
                        at = (b * TB + t) * P
                        mm = pe.matmul(pair[:, t * D:(t + 1) * D], combT[:, at:at + P], b2[:, :],
                                       start=True, stop=True)
                    mm.then_inc(*a_full.next(("b2", b)))

            pe.wait_ge(*load["wca1"].when("all"))
            for u in range(B * SE // S):
                for c in range(DC):
                    project_chunk("ca1", "k", u, c)
                    if u == 1 and c == 1:
                        ranks()
            share_of_b2()

            slot_turn(0)
            slot_hidden(0)
            for s in range(SLOTS):
                if s + 1 < SLOTS:
                    slot_turn(s + 1)
                    slot_hidden(s + 1)
                slot_result(s)
            for b in range(B):
                pe.wait_ge(*pool_done.when(("ln", "moe", b)))
                turn(("turn", b, "moe"), [xtok[:, b * TB + t, :] for t in range(TB)])
            pe.wait_ge(*a_free.when(a_keys[-1]))

            def mlp(name):
                wg = mlp_w[0].rearrange("p (c f) -> p c f", c=DC)
                wu = mlp_w[1].rearrange("p (c f) -> p c f", c=DC)
                wd = mlp_w[2].rearrange("p (c n) -> p c n", c=FC)
                pe.wait_ge(*load["mlp_" + name].when("all"))
                for hf in range(B):
                    for f in range(FC):
                        bank = take_b(("g", name, hf, f))
                        for c in range(DC):
                            mm = pe.matmul(bank[:, :], wg[:, c, f * P:(f + 1) * P], xT[:, c, hf * S:(hf + 1) * S],
                                           start=(c == 0), stop=(c == DC - 1))
                        mm.then_inc(*b_full.next(("g", name, hf, f)))
                        pair = take_a(("u", name, hf, f))
                        for c in range(DC):
                            mm = pe.matmul(pair[:, 0:S], wu[:, c, f * P:(f + 1) * P], xT[:, c, hf * S:(hf + 1) * S],
                                           start=(c == 0), stop=(c == DC - 1))
                        mm.then_inc(*a_full.next(("u", name, hf, f)))
                for hf in range(B):
                    pair = take_a(("down", name, hf))
                    pe.wait_ge(*a_free.when(("u", name, hf, FC - 1)))
                    for dc in range(DC):
                        for f in range(FC):
                            mm = pe.matmul(pair[:, dc * S:(dc + 1) * S], wd[:, f, dc * P:(dc + 1) * P],
                                           hT[hf][:, f, :], start=(f == 0), stop=(f == FC - 1))
                    mm.then_inc(*a_full.next(("down", name, hf)))
                pe.wait_ge(*a_free.when(a_keys[-1]))

            attend("sa1")
            mlp("sa1")
            attend("ca1")
            mlp("ca1")
            for b in range(B):
                pair = take_a(("out", b))
                for t in range(TB):
                    for c in range(DC):
                        at = (b * TB + t) * P
                        mm = pe.transpose(pair[:, t * D + c * P:t * D + (c + 1) * P], xT[:, c, at:at + P],
                                          ident[:, :])
                mm.then_inc(*a_full.next(("out", b)))

        @block.vector
        def _(dve):
            def copy_T(key, dst):
                dve.wait_ge(*a_full.when(key))
                dve.tensor_copy(dst, a_slot(key)[:, :].rearrange("p (c t) -> p c t", c=DC))\
                   .then_inc(*a_free.next(key))

            def split(name, which, u, c):
                a = ATTENTIONS[name]
                key = ("split", name, which, u, c)
                i = split_no[name, which, u, c]
                x, part = exact[:, c, :], parts[:, i % 2]
                dve.wait_ge(*a_full.when(key))
                if a.layer == 0:
                    bias = biasT[name[:2] + "_b" + which]
                    dve.tensor_scalar(x, a_slot(key)[:, 0:S], bias[:, c:c + 1], None, ALU.add)\
                       .then_inc(*a_free.next(key))
                else:
                    dve.tensor_copy(x, a_slot(key)[:, 0:S]).then_inc(*a_free.next(key))
                if i >= 2:
                    dve.wait_ge(*part_out[i % 2].when(i - 2))
                dve.wait_ge(*a_free.now())
                dve.tensor_copy(part[:, 0, :], x).then_inc(*vec.next())
                dve.wait_ge(*vec.now())
                dve.tensor_tensor(x, x, part[:, 0, :], ALU.subtract).then_inc(*vec.next())
                dve.wait_ge(*vec.now())
                dve.tensor_copy(part[:, 1, :], x).then_inc(*vec.next())
                dve.wait_ge(*vec.now())
                dve.tensor_tensor(part[:, 2, :], x, part[:, 1, :], ALU.subtract)\
                   .then_inc(*vec.next(("split", i)))
                dve.wait_ge(*vec.now())

            def values(name, u):
                a = ATTENTIONS[name]
                key = ("v", name, u)
                dve.wait_ge(*a_full.when(key))
                pair = a_slot(key)
                if a.layer == 0:
                    for t in range(TB):
                        tile = u * TB + t
                        dst = vx[:, tile * 272:tile * 272 + 272].rearrange("p (h d) -> p h d", d=17)[:, :, 0:16]
                        ins = dve.tensor_tensor(dst, pair[:, t * D:(t + 1) * D].rearrange("p (h d) -> p h d", d=16),
                                                row[name[:2] + "_bv"][:, :].rearrange("p (h d) -> p h d", d=16),
                                                ALU.add)
                        ins.then_inc(*(a_free.next(key) if t == TB - 1 else vec.next()))
                else:
                    at = u * TB * D
                    dve.tensor_copy(vx[:, at:at + TB * D], pair[:, :]).then_inc(*a_free.next(key))

            def normalise_rows(b, name):
                for t in range(TB):
                    dve.bn_stats(stats[:, t, :], xtok[:, b * TB + t, :]).then_inc(*vec.next())
                dve.wait_ge(*vec.now())
                for t in range(TB):
                    dve.bn_aggr(mv[:, t, :], stats[:, t, :]).then_inc(*vec.next())
                dve.wait_ge(*vec.now())
                dve.tensor_scalar(var[:, :], mv[:, :, 1], EPS, None, ALU.add)\
                   .then_inc(*vec.next(("var", name, b)))
                dve.wait_ge(*pool_done.when(("rstd", name, b)))
                for t in range(TB):
                    x = xtok[:, b * TB + t, :]
                    dve.tensor_scalar(x, x, mv[:, t, 0:1], rstd[:, t:t + 1], ALU.subtract, ALU.mult)\
                       .then_inc(*vec.next(("centred", name, b)))

            def attention(a):
                for step in a.steps():
                    kind, b = step[0], step[1]
                    key = step + (a.name,)
                    if kind == "max":
                        _, b, h, qt = step
                        g, j = h // a.G, h % a.G
                        gi = a.groups.index((b, g))
                        dve.wait_ge(*a_full.when(key))
                        if a.per_job == 1:
                            scores = a_slot(key)[:, 0:a.keys_to(qt)]
                        else:
                            scores = a_slot(key)[:, :].rearrange("p (h k) -> p h k", h=2)[:, :, 0:a.keys_to(qt)]
                        dve.tensor_reduce(negmax[:, gi % 2, qt, j:j + a.per_job], scores,
                                          AX.X, ALU.max, negate=True).then_inc(*a_free.next(key))
                    elif kind == "shift":
                        _, b, g = step
                        gi = a.groups.index((b, g))
                        sh, out = shift[0:a.G, :], shiftb[0:a.G]
                        dve.wait_ge(*a_full.when(key))
                        dve.tensor_copy(sh, a_slot(key)[0:a.G, 0:S]).then_inc(*a_free.next(key))
                        if gi >= 1:
                            dve.wait_ge(*shift_in[(gi - 1) % 2].when((a.name, gi - 1)))
                        dve.wait_ge(*a_free.now())
                        dve.tensor_copy(out[:, 0, :], sh).then_inc(*vec.next())
                        dve.wait_ge(*vec.now())
                        dve.tensor_tensor(sh, sh, out[:, 0, :], ALU.subtract).then_inc(*vec.next())
                        dve.wait_ge(*vec.now())
                        dve.tensor_copy(out[:, 1, :], sh).then_inc(*vec.next())
                        dve.wait_ge(*vec.now())
                        dve.tensor_tensor(out[:, 2, :], sh, out[:, 1, :], ALU.subtract)\
                           .then_inc(*vec.next(("shift", a.name, gi)))
                        dve.wait_ge(*vec.now())
                    elif kind == "evict":
                        _, b, g = step
                        gi = a.groups.index((b, g))
                        last = (gi + 1) * a.KT * a.G - 1
                        dve.wait_ge(*pv_done.when((a.name, last)))
                        if a.layer:
                            dve.tensor_copy(dens[:, :], o_bank[1][0:64, :]).then_inc(*vec.next())
                            dve.tensor_copy(sums[:, gi % 2, :], o_bank[0][:, :])\
                               .then_inc(*vec.next(("evict", a.name, gi)))
                        else:
                            dve.tensor_copy(sums[:, gi % 2, :], o_bank[gi % 2][:, :])\
                               .then_inc(*vec.next(("evict", a.name, gi)))
                    elif kind == "norm":
                        _, b, g = step
                        dve.wait_ge(*a_full.when(key))
                        pair = a_slot(key)
                        if a.layer:
                            o = pair[:, 0:512].rearrange("p (t h d) -> p t h d", t=TB, h=2)
                            den = pair[:, 512:768].rearrange("p (t h d) -> p t h d", t=TB, h=2)[:, :, :, 0]
                        else:
                            o = pair[:, 0:512].rearrange("p (t h d) -> p t h d", t=TB, h=4)
                            den = o[:, :, :, 16]
                            o = o[:, :, :, 0:16]
                        dve.reciprocal(rden[:, :, 0:a.G], den).then_inc(*vec.next())
                        dve.wait_ge(*vec.now())
                        w = a.G * a.HD
                        dst = otok[:, :, g * w:(g + 1) * w].rearrange("p t (h d) -> p t h d", d=a.HD)
                        for t in range(TB):
                            r = rden[:, t, 0:a.G].unsqueeze(2).to_broadcast([P, a.G, a.HD])
                            ins = dve.tensor_tensor(dst[:, t], o[:, t], r, ALU.mult)
                            ins.then_inc(*(a_free.next(key) if t == TB - 1 else vec.next()))
                    elif kind == "heads":
                        copy_T(key, oT[:, :, :])
                    elif kind == "proj":
                        dve.wait_ge(*a_full.when(key))
                        if a.layer:
                            x = xT[:, :, b * S:(b + 1) * S]
                            dve.tensor_tensor(x, a_slot(key)[:, :].rearrange("p (c t) -> p c t", c=DC), x, ALU.add)\
                               .then_inc(*a_free.next(key))
                        else:
                            dve.wait_ge(*pool_done.when(("bo", a.name)))
                            x = xtok[:, b * TB:(b + 1) * TB, :]
                            dve.tensor_tensor(x, a_slot(key)[:, :].rearrange("p (t d) -> p t d", t=TB), x, ALU.add)\
                               .then_inc(*a_free.next(key))
                            dve.wait_ge(*a_free.now())
                    elif kind == "early":
                        split(a.early, "k", *step[2:])
                    elif kind == "ln":
                        normalise_rows(b, a.name)
                    elif kind == "turn":
                        copy_T(key, xT[:, :, b * S:(b + 1) * S])

            def projections(name):
                a = ATTENTIONS[name]
                for job in split_order():
                    if job[0] == name and not (job[1] == "k" and a.nk == SE):
                        split(*job)
                if name == "sa0":
                    for u in range(B * SE // S):
                        copy_T(("ctx", u), ctxT[:, :, u * S:(u + 1) * S])
                for u in range(B * a.nk // S):
                    values(name, u)

            dve.wait_ge(*pool_done.when("constants"))
            for b in range(B):
                copy_T(("x", b), xT[:, :, b * S:(b + 1) * S])
            dve.wait_ge(*load["rows"].when("all"))
            for name in ("sa0", "ca0"):
                projections(name)
                attention(ATTENTIONS[name])

            def link(ins):
                ins.then_inc(*vec.next())
                dve.wait_ge(*vec.now())

            key = ("router",)
            dve.wait_ge(*a_full.when(key))
            dve.tensor_tensor(lg[:, :, :], a_slot(key)[:, 0:NT * E].rearrange("p (t e) -> p t e", e=E),
                              rb[:, :].unsqueeze(1).to_broadcast([P, NT, E]), ALU.add)\
               .then_inc(*a_free.next(key))
            dve.wait_ge(*a_free.now())
            dve.wait_ge(*pool_done.when("router_constants"))
            link(dve.tensor_reduce(small[:, 0, :], lg[:, :, :], AX.X, ALU.max))
            dve.tensor_tensor(lg[:, :, :], lg[:, :, :], small[:, 0, :].unsqueeze(2).to_broadcast([P, NT, E]),
                              ALU.subtract).then_inc(*vec.next("logits"))
            dve.wait_ge(*act_done.when("router_exp"))
            link(dve.tensor_reduce(small[:, 1, :], lg[:, :, :], AX.X, ALU.add))
            link(dve.reciprocal(small[:, 2, :], small[:, 1, :]))
            link(dve.tensor_tensor(lg[:, :, :], lg[:, :, :], small[:, 2, :].unsqueeze(2).to_broadcast([P, NT, E]),
                                   ALU.mult))
            for t in range(NT):
                dve.max(best[:, t, :], lg[:, t, :]).then_inc(*vec.next())
            dve.wait_ge(*vec.now())
            dve.tensor_tensor(small[:, 3, :], best[:, :, 1], best[:, :, 0], ALU.subtract)\
               .then_inc(*vec.next("gap"))
            for t in range(NT):
                dve.max_index(besti[:, t, :], best[:, t, :], lg[:, t, :]).then_inc(*vec.next())
            dve.wait_ge(*vec.now())
            link(dve.tensor_copy(bestf[:, :, :], besti[:, :, :]))
            dve.wait_ge(*act_done.when("gap_exp"))
            link(dve.tensor_scalar(small[:, 4, :], small[:, 3, :], 1.0, None, ALU.add))
            link(dve.reciprocal(small[:, 4, :], small[:, 4, :]))
            link(dve.tensor_tensor(small[:, 5, :], small[:, 3, :], small[:, 4, :], ALU.mult))
            for k in range(TOP):
                dve.tensor_tensor(chosen[:, k], expert_no[:, :].unsqueeze(1).to_broadcast([P, NT, E]),
                                  bestf[:, :, k].unsqueeze(2).to_broadcast([P, NT, E]), ALU.is_equal)\
                   .then_inc(*vec.next())
            dve.wait_ge(*vec.now())
            dve.tensor_tensor(chosenb[:, :, :], chosen[:, 0], chosen[:, 1], ALU.add).then_inc(*vec.next("chosen"))
            for u in range(2):
                for c in range(DC):
                    split("ca1", "k", u, c)
            link(dve.tensor_tensor(comb[:, :, :], chosen[:, 0], small[:, 4, :].unsqueeze(2).to_broadcast([P, NT, E]),
                                   ALU.mult))
            link(dve.tensor_tensor(place[:, :, :], chosen[:, 1], small[:, 5, :].unsqueeze(2).to_broadcast([P, NT, E]),
                                   ALU.mult))
            dve.tensor_tensor(comb[:, :, :], comb[:, :, :], place[:, :, :], ALU.add).then_inc(*vec.next("comb"))
            dve.memset(ends[:, :, :], 0.0).then_inc(*vec.next())
            dve.wait_ge(*a_full.when(("rank",)))
            dve.tensor_copy(rank[:, :, :], a_slot(("rank",))[:, 0:(NT + 1) * E].rearrange("p (t e) -> p t e", e=E))\
               .then_inc(*a_free.next(("rank",)))
            dve.wait_ge(*a_free.now())
            dve.wait_ge(*vec.now())
            need = ends[:, 0, 4:4 + E]
            link(dve.tensor_scalar(need, rank[:, NT, :], 0.0, None, ALU.is_gt))
            for k in range(1, T // SLOT):
                link(dve.scalar_tensor_tensor(out=need, in0=rank[:, NT, :], scalar=float(k * SLOT), in1=need,
                                              op0=ALU.is_gt, op1=ALU.add))
            for i, by in enumerate((1, 2, 4)):
                link(dve.tensor_tensor(ends[:, i + 1, 4:4 + E], ends[:, i, 4:4 + E],
                                       ends[:, i, 4 - by:4 - by + E], ALU.add))
            link(dve.tensor_tensor(past[:, :, :], ends[0:1, 3, 4:4 + E].unsqueeze(1).to_broadcast([1, SLOTS, E]),
                                   slot_no[:, :].unsqueeze(2).to_broadcast([1, SLOTS, E]), ALU.is_le))
            link(dve.tensor_reduce(slot_ef[:, :], past[:, :, :], AX.X, ALU.add))
            link(dve.tensor_scalar(slot_ef[:, :], slot_ef[:, :], float(E - 1), None, ALU.min))
            dve.tensor_copy(slot_e[:, :], slot_ef[:, :]).then_inc(*vec.next("slot_e"))
            dve.wait_ge(*vec.now())
            link(dve.scalar_tensor_tensor(out=rank[:, 0:NT, :], in0=ends[:, 3, 3:3 + E].unsqueeze(1).to_broadcast([P, NT, E]),
                                          scalar=float(SLOT), in1=rank[:, 0:NT, :], op0=ALU.mult, op1=ALU.add))
            for k in range(TOP):
                link(dve.tensor_tensor(place[:, :, :], chosen[:, k], rank[:, 0:NT, :], ALU.mult))
                link(dve.tensor_reduce(placed[:, k, :], place[:, :, :], AX.X, ALU.add))
            dve.tensor_copy(place_no[:, :, :], placed[:, :, :]).then_inc(*vec.next("places"))
            for u in range(2, 4):
                for c in range(DC):
                    split("ca1", "k", u, c)
            dve.wait_ge(*a_full.when(("combT",)))
            dve.tensor_copy(combT[:, :], a_slot(("combT",))[0:E, :]).then_inc(*a_free.next(("combT",)))
            for b in range(B):
                key = ("b2", b)
                dve.wait_ge(*a_full.when(key))
                if b == 0:
                    dve.wait_ge(*sent_out.when("all"))
                x = xtok[:, b * TB:(b + 1) * TB, :]
                dve.tensor_tensor(x, a_slot(key)[:, :].rearrange("p (t d) -> p t d", t=TB), x, ALU.add)\
                   .then_inc(*a_free.next(key))

            def slot_turned(s):
                dve.wait_ge(*a_full.when(("xs", s)))
                dve.tensor_copy(xST[s % 2], a_slot(("xs", s))[:, 0:DC * SLOT].rearrange("p (c t) -> p c t", c=DC))\
                   .then_inc(*a_free.next(("xs", s)))

            slot_turned(0)
            for s in range(SLOTS):
                if s + 1 < SLOTS:
                    slot_turned(s + 1)
                key = ("eo", s)
                dve.wait_ge(*a_full.when(key))
                if s >= 2:
                    dve.wait_ge(*slot_out[s % 2].when(s - 2))
                dve.tensor_copy(yS[s % 2], a_slot(key)[:, 0:ST * D].rearrange("p (t d) -> p t d", t=ST))\
                   .then_inc(*a_free.next(key))
            for b in range(B):
                dve.wait_ge(*back_in[b].when("all"))
                for k in range(TOP):
                    for t in range(b * TB, (b + 1) * TB):
                        x = xtok[:, t, :]
                        dve.scalar_tensor_tensor(out=x, in0=back[:, k, t, :], scalar=small[:, 4 + k, t:t + 1], in1=x,
                                                 op0=ALU.mult, op1=ALU.add).then_inc(*vec.next())
                    dve.wait_ge(*vec.now())
                normalise_rows(b, "moe")
            for b in range(B):
                copy_T(("turn", b, "moe"), xT[:, :, b * S:(b + 1) * S])

            def mlp(name):
                for hf in range(B):
                    for f in range(FC):
                        key = ("u", name, hf, f)
                        dve.wait_ge(*a_full.when(key))
                        dve.wait_ge(*b_free.when(("g", name, hf, f)))
                        dve.tensor_tensor(hT[hf][:, f, :], a_slot(key)[:, 0:S], gate[:, f % 2, :], ALU.mult)\
                           .then_inc(*a_free.next(key))
                for hf in range(B):
                    key = ("down", name, hf)
                    dve.wait_ge(*a_full.when(key))
                    x = xT[:, :, hf * S:(hf + 1) * S]
                    dve.tensor_tensor(x, a_slot(key)[:, :].rearrange("p (c t) -> p c t", c=DC), x, ALU.add)\
                       .then_inc(*a_free.next(key))
                dve.wait_ge(*a_free.now())

            for name in ("sa1", "ca1"):
                projections(name)
                attention(ATTENTIONS[name])
                dve.wait_ge(*a_free.now())
                mlp(name)
            for b in range(B):
                key = ("out", b)
                dve.wait_ge(*a_full.when(key))
                dve.tensor_copy(xtok[:, b * TB:(b + 1) * TB, :],
                                a_slot(key)[:, :].rearrange("p (t d) -> p t d", t=TB))\
                   .then_inc(*a_free.next(key))

        @block.scalar
        def _(act):
            def exps(a):
                for step in a.steps():
                    if step[0] != "unit":
                        continue
                    _, b, g, kt, j, n = step
                    key = ("unit", a.name, n)
                    w = S - a.queries_from(kt)
                    act.wait_ge(*b_full.when(key))
                    if n >= 4:
                        act.wait_ge(*pv_done.when((a.name, n - 4)))
                    act.activation(probs[:, n % 4, 0:w], b_slot(key)[:, 0:w], ACT.Exp, scale=a.scale)\
                       .then_inc(*b_free.next(key))

            exps(ATTENTIONS["sa0"])
            exps(ATTENTIONS["ca0"])
            act.wait_ge(*vec.when("logits"))
            act.activation(lg[:, :, :], lg[:, :, :], ACT.Exp).then_inc(*act_done.next("router_exp"))
            act.wait_ge(*vec.when("gap"))
            act.activation(small[:, 3, :], small[:, 3, :], ACT.Exp).then_inc(*act_done.next("gap_exp"))
            for s in range(SLOTS):
                act.wait_ge(*b1_load[s % 2].when(s))
                for f in range(FC):
                    key = ("h", s, f)
                    act.wait_ge(*b_full.when(key))
                    if f == 0 and s >= 2:
                        act.wait_ge(*a_full.when(("eo", s - 2)))
                    act.activation(hS[s % 2][:, f, :], b_slot(key)[:, 0:SLOT], ACT.Gelu, bias=b1S[s % 2][:, f:f + 1])\
                       .then_inc(*b_free.next(key))

            def silus(name):
                for hf in range(B):
                    for f in range(FC):
                        key = ("g", name, hf, f)
                        act.wait_ge(*b_full.when(key))
                        n = hf * FC + f
                        if n >= 2:
                            act.wait_ge(*a_free.when(("u", name, (n - 2) // FC, (n - 2) % FC)))
                        act.activation(gate[:, f % 2, :], b_slot(key)[:, :], ACT.Silu).then_inc(*b_free.next(key))

            exps(ATTENTIONS["sa1"])
            silus("sa1")
            exps(ATTENTIONS["ca1"])
            silus("ca1")

        @block.gpsimd
        def _(pool):
            for t, v in ((ident, 0.0), (identb, 0.0), (mask_q, 0.0), (mask_k, 0.0)):
                pool.memset(t[:, :], v).then_inc(*pool_done.next())
            pool.memset(onesb[:, :], 1.0).then_inc(*pool_done.next())
            pool.memset(onesf[:, :], 1.0).then_inc(*pool_done.next())
            pool.memset(minus_half[:, :], -0.5).then_inc(*pool_done.next())
            pool.iota(expert_no[:, :], pattern=[[1, E]], base=0, channel_multiplier=0,
                      allow_small_or_imprecise_dtypes=True).then_inc(*pool_done.next())
            pool.wait_ge(*pool_done.now())
            for m in (ident, identb):
                pool.affine_select(out=m[:, :], in_=m[:, :], compare_op=ALU.not_equal, fill=1.0, base=0,
                                   pattern=[[-1, P]], channel_multiplier=1).then_inc(*pool_done.next())
            pool.affine_select(out=mask_q[:, :], in_=mask_q[:, :], compare_op=ALU.is_ge, fill=NEG, base=0,
                               pattern=[[-1, P]], channel_multiplier=1).then_inc(*pool_done.next())
            pool.affine_select(out=mask_k[:, :], in_=mask_k[:, :], compare_op=ALU.is_ge, fill=NEG, base=0,
                               pattern=[[1, P]], channel_multiplier=-1).then_inc(*pool_done.next())
            pool.memset(vx[:, :], 1.0).then_inc(*pool_done.next("constants"))
            pool.memset(zeros, 0.0).then_inc(*pool_done.next("zeros"))
            pool.memset(below[:, :], 1.0).then_inc(*pool_done.next())
            pool.wait_ge(*pool_done.now())
            pool.affine_select(out=below[:, :], in_=below[:, :], compare_op=ALU.is_ge, fill=0.0, base=-1,
                               pattern=[[1, P]], channel_multiplier=-1).then_inc(*pool_done.next())
            pool.iota(slot_no[:, :], pattern=[[1, SLOTS]], base=0, channel_multiplier=0,
                      allow_small_or_imprecise_dtypes=True).then_inc(*pool_done.next("router_constants"))
            pool.wait_ge(*pool_done.now())
            pool.memset(arena[96:99, 32768:49152], 1.0).then_inc(*pool_done.next(("shift_ones", "sa0")))
            pool.wait_ge(*a_full.when(("ctx", B * SE // S - 1)))
            pool.wait_ge(*zeroed.when("all"))
            pool.wait_ge(*pool_done.now())
            pool.memset(arena[96:99, 16384:32768], 1.0).then_inc(*pool_done.next(("shift_ones", "ca0")))

            def add_bo(name):
                if name == "sa0":
                    pool.wait_ge(*load["rows"].when("all"))
                    pool.wait_ge(*a_full.when(("x", B - 1)))
                else:
                    pool.wait_ge(*a_full.when(("turn", B - 1, "sa0")))
                pool.wait_ge(*pool_done.now())
                r = row[name[:2] + "_bo"][:, :].unsqueeze(1).to_broadcast([P, NT, D])
                pool.tensor_tensor(xtok[:, :, :], xtok[:, :, :], r, ALU.add).then_inc(*pool_done.next(("bo", name)))

            def layernorm(name, ln, b):
                pool.wait_ge(*vec.when(("var", name, b)))
                pool.tensor_tensor(rstd[:, :], var[:, :], minus_half[:, :], ALU.pow)\
                    .then_inc(*pool_done.next(("rstd", name, b)))
                pool.wait_ge(*vec.when(("centred", name, b)))
                x = xtok[:, b * TB:(b + 1) * TB, :]
                pool.tensor_tensor(x, x, row[ln + "_g"][:, :].unsqueeze(1).to_broadcast([P, TB, D]), ALU.mult)\
                    .then_inc(*pool_done.next())
                pool.wait_ge(*pool_done.now())
                pool.tensor_tensor(x, x, row[ln + "_b"][:, :].unsqueeze(1).to_broadcast([P, TB, D]), ALU.add)\
                    .then_inc(*pool_done.next(("ln", name, b)))

            for name, ln in (("sa0", "ln1"), ("ca0", "ln2")):
                add_bo(name)
                for b in range(B):
                    layernorm(name, ln, b)
            pool.wait_ge(*vec.when("places"))
            pool.wait_ge(*zeroed.when("all"))
            for t in range(NT):
                for k in range(TOP):
                    pool.indirect_dma_start(sent, IndirectOffsetOnAxis(ap=place_no[:, k, t:t + 1], axis=0),
                                            xtok[:, t, :], None).then_inc(*sent_out.next("all", 16))
            for s in range(SLOTS - 2, SLOTS):
                pool.wait_ge(*slot_out[s % 2].when(s))
            for t in range(NT):
                for k in range(TOP):
                    pool.indirect_dma_start(back[:, k, t, :], None, computed,
                                            IndirectOffsetOnAxis(ap=place_no[:, k, t:t + 1], axis=0))\
                        .then_inc(*back_in[t // TB].next("all", 16))
            for b in range(B):
                layernorm("moe", "ln3", b)
            for b in range(B):
                pool.wait_ge(*a_full.when(("eo", SLOTS - 1)))
                pool.memset(m_rows(b), 0.0).then_inc(*pool_done.next(("m_zero", "sa1")))
            pool.wait_ge(*a_full.when(("down", "sa1", B - 1)))
            for b in range(B):
                pool.memset(m_rows(b), 0.0).then_inc(*pool_done.next(("m_zero", "ca1")))

        @block.sync
        def _(sp):
            def loads(name, pairs):
                for dst, src in pairs:
                    sp.dma_start(dst, src).then_inc(*load[name].next("all", 16))

            def weights(name):
                pre = "L%s_xattn_%s_w" % (name[2], name[:2])
                i = att_index[name]
                return [(wset[i % 2][:, n], io[pre + c].rearrange("(c p) n -> p c n", p=P))
                        for n, c in enumerate("qkvo")]

            loads("x", [(xtok[:, b * TB:(b + 1) * TB, :], io["x"][b].rearrange("(t p) d -> p t d", p=P))
                        for b in range(B)])
            loads("wsa0", weights("sa0"))
            loads("ctx", [(ctx_in[:, b * 8:(b + 1) * 8, :], io["ctx_1024"][b].rearrange("(t p) d -> p t d", p=P))
                          for b in range(B)])
            L0 = "L0_xattn_"
            with nc.allow_non_contiguous_dma(reason="biases onto the partitions, a few kilobytes"):
                loads("rows", [(biasT[n][:, :], io[L0 + n].rearrange("(c p) -> p c", p=P)) for n in biasT]
                      + [(b1T[:, :, :], io[L0 + "e_b1"].rearrange("e (f p) -> p e f", p=P))])
            loads("rows", [(row[n][:, :], io[L0 + n].partition_broadcast(P)) for n in row]
                  + [(rb[:, :], io[L0 + "router_b"].partition_broadcast(P)),
                     (b2[:, :], io[L0 + "e_b2"]),
                     (rw[:, :, :], io[L0 + "router_w"].rearrange("(c p) n -> p c n", p=P))])
            loads("wca0", weights("ca0"))
            sp.wait_ge(*pool_done.when("zeros"))
            for s in range(SLOTS):
                sp.dma_start(sent[s * SLOT:(s + 1) * SLOT, :].rearrange("(t p) d -> p t d", p=P), zeros)\
                  .then_inc(*zeroed.next("all", 16))

            def store_parts(name, which, u, c):
                i = split_no[name, which, u, c]
                scr = (scratch_q if which == "q" else scratch_k)[att_index[name]]
                sp.wait_ge(*vec.when(("split", i)))
                sp.dma_start(scr[:, c * P:(c + 1) * P, u * S:(u + 1) * S].rearrange("r p t -> p r t"),
                             parts[:, i % 2]).then_inc(*part_out[i % 2].next(i, 16))

            def stack(name, which, u):
                a = ATTENTIONS[name]
                scr = (scratch_q if which == "q" else scratch_k)[att_index[name]]
                for c in range(DC):
                    i = split_no[name, which, u, c]
                    sp.wait_ge(*part_out[i % 2].when(i))
                per = a.nk // S if which == "k" else 1
                b, t0 = u // per, (u % per) * S
                for r, part in enumerate(QUERY_PARTS if which == "q" else KEY_PARTS):
                    src = scr[part, :, u * S:(u + 1) * S].rearrange("(h d) t -> d h t", d=a.HD)
                    if a.layer == 0:
                        st = (q_stack if which == "q" else k_stack)(a, b)
                        dst = st[r * 16:(r + 1) * 16, :, t0:t0 + S]
                    elif which == "q":
                        dst = q_stack(a, b, r // 2)[(r % 2) * 64:(r % 2) * 64 + 64, :, t0:t0 + S]
                    else:
                        if r in (2, 3):
                            continue
                        dst = k_stack(a, b, 0 if r < 2 else 1)[(r % 2) * 64:(r % 2) * 64 + 64, :, t0:t0 + S]
                    sp.dma_start(dst, src).then_inc(*stack_in[name, b].next("all", 16))

            def last_unit(a, b):
                return b_full.when(("unit", a.name, (b + 1) * len(a.groups) // B * a.KT * a.G - 1))

            def shifts(name):
                a = ATTENTIONS[name]
                for step in a.steps():
                    if step[0] == "early":
                        store_parts(a.early, "k", *step[2:])
                        u, c = step[2:]
                        if c == DC - 1 and u == 0:
                            sp.wait_ge(*pool_done.when(("shift_ones", "ca0")))
                        if c == DC - 1 and u < 2:
                            stack(a.early, "k", u)
                    if step[0] != "shift":
                        continue
                    _, b, g = step
                    gi = a.groups.index((b, g))
                    sp.wait_ge(*vec.when(("shift", name, gi)))
                    if gi == 0:
                        sp.wait_ge(*pool_done.when(("m_zero" if a.layer else "shift_ones", name)))
                    for r in range(3):
                        rows = m_rows(b) if a.layer else q_stack(a, b)
                        at = r if a.layer else 96 + r
                        sp.dma_start(rows[at:at + 1, g * a.G:(g + 1) * a.G, :], shiftb[0:a.G, r, :])\
                          .then_inc(*shift_in[gi % 2].next((name, gi), 16))

            def own_stacks(name):
                for u in range(B):
                    for which in "kq":
                        for c in range(DC):
                            store_parts(name, which, u, c)
                        stack(name, which, u)

            own_stacks("sa0")
            shifts("sa0")
            for b in range(B):
                sp.wait_ge(*last_unit(ATTENTIONS["sa0"], b))
            stack("ca0", "k", 2)
            stack("ca0", "k", 3)
            for u in range(B):
                for c in range(DC):
                    store_parts("ca0", "q", u, c)
                stack("ca0", "q", u)
            sp.wait_ge(*a_free.when(("proj", B - 1, "sa0")))
            loads("wsa1", weights("sa1"))
            shifts("ca0")
            sp.wait_ge(*a_free.when(("proj", B - 1, "ca0")))
            loads("wca1", weights("ca1"))
            for u in range(2):
                for c in range(DC):
                    store_parts("ca1", "k", u, c)
            sp.wait_ge(*vec.when("slot_e"))

            def store_results(s):
                sp.wait_ge(*a_free.when(("eo", s)))
                sp.dma_start(computed[s * SLOT:(s + 1) * SLOT, :].rearrange("(t p) d -> p t d", p=P), yS[s % 2])\
                  .then_inc(*slot_out[s % 2].next(s, 16))

            def first_weights(s):
                if s >= 2:
                    sp.wait_ge(*b_full.when(("h", s - 2, FC - 1)))
                    sp.wait_ge(*b_free.when(("h", s - 2, FC - 1)))
                experts[s] = sp.value_load(slot_e[0:1, s:s + 1], min_val=0, max_val=E - 1)
                e = experts[s]
                sp.dma_start(w1[s % 2], io[L0 + "e_w1"][DynSlice(e, 1)].rearrange("e (c p) f -> p (e c) f", p=P))\
                  .then_inc(*w1_load[s % 2].next(s, 16))
                sp.dma_start(b1S[s % 2], b1T[:, DynSlice(e, 1), :].rearrange("p e f -> p (e f)"))\
                  .then_inc(*b1_load[s % 2].next(s, 16))

            def second_weights(s):
                if s >= 2:
                    sp.wait_ge(*a_full.when(("eo", s - 2)))
                sp.dma_start(w2[s % 2], io[L0 + "e_w2"][DynSlice(experts[s], 1)]
                             .rearrange("e (f p) n -> p (e f) n", p=P)).then_inc(*w2_load[s % 2].next(s, 16))

            def slot_tokens(s):
                if s >= 2:
                    sp.wait_ge(*a_full.when(("xs", s - 2)))
                sp.dma_start(xS[s % 2], sent[s * SLOT:(s + 1) * SLOT, :].rearrange("(t p) d -> p t d", p=P))\
                  .then_inc(*slot_in[s % 2].next(s, 16))

            experts = {}
            first_weights(0)
            first_weights(1)
            second_weights(0)
            for u in range(2, 4):
                for c in range(DC):
                    store_parts("ca1", "k", u, c)
            sp.wait_ge(*sent_out.when("all"))
            slot_tokens(0)
            slot_tokens(1)
            for s in range(1, SLOTS):
                if s + 1 < SLOTS:
                    slot_tokens(s + 1) if s + 1 >= 2 else None
                    first_weights(s + 1)
                second_weights(s)
                if s >= 2:
                    store_results(s - 2)
            store_results(SLOTS - 2)
            store_results(SLOTS - 1)

            def mlp_weights(name):
                pre = "L1_xattn_" + name[:2] + "mlp_w"
                loads("mlp_" + name, [
                    (mlp_w[0].rearrange("p (c f) -> p c f", c=DC), io[pre + "g"].rearrange("(c p) f -> p c f", p=P)),
                    (mlp_w[1].rearrange("p (c f) -> p c f", c=DC), io[pre + "u"].rearrange("(c p) f -> p c f", p=P)),
                    (mlp_w[2].rearrange("p (c n) -> p c n", c=FC), io[pre + "d"].rearrange("(f p) n -> p f n", p=P))])

            sp.wait_ge(*a_full.when(("eo", SLOTS - 1)))
            own_stacks("sa1")
            shifts("sa1")
            sp.wait_ge(*a_free.when(("heads", B - 1, "sa1")))
            mlp_weights("sa1")
            sp.wait_ge(*a_full.when(("down", "sa1", B - 1)))
            stack("ca1", "k", 0)
            stack("ca1", "k", 1)
            for u in range(B):
                for c in range(DC):
                    store_parts("ca1", "q", u, c)
                stack("ca1", "q", u)
                if u == 0:
                    stack("ca1", "k", 2)
                    stack("ca1", "k", 3)
            shifts("ca1")
            sp.wait_ge(*a_free.when(("down", "sa1", B - 1)))
            mlp_weights("ca1")
            for b in range(B):
                sp.wait_ge(*a_free.when(("out", b)))
                sp.dma_start(io["out"][b].rearrange("(t p) d -> p t d", p=P), xtok[:, b * TB:(b + 1) * TB, :])\
                  .then_inc(*stored.next("out", 16))
            sp.wait_ge(*stored.now())

    seen = {n: s.seen for n, s in signals.items()}
    seen["_a_turn"] = {k: i % 2 for i, k in enumerate(a_keys)}
    seen["_b_turn"] = {k: i % 2 for i, k in enumerate(b_keys)}
    return seen


def kernel(**inputs):
    import numpy as _np
    import concourse.bacc as _bacc
    from concourse import mybir as _mybir
    from concourse.bass_utils import run_bass_kernel_spmd as _run

    arrays = {f"in_{name}": _np.ascontiguousarray(a) for name, a in inputs.items()}

    def build(known):
        nc = _bacc.Bacc("TRN2", target_bir_lowering=False, num_devices=1)
        io = {name[3:]: nc.dram_tensor(name, a.shape, _mybir.dt.from_np(a.dtype), kind="ExternalInput").ap()
              for name, a in arrays.items()}
        io["out"] = nc.dram_tensor("out", (B, S, D), F32, kind="ExternalOutput").ap()
        return nc, program(nc, io, known)

    _, known = build(None)
    nc, _ = build(known)
    r = _run(nc, [arrays], core_ids=[0])
    return r.results[0]["out"]
```

```python
from contextlib import ExitStack

import numpy as np
from concourse import mybir
from concourse.bass import DynSlice, IndirectOffsetOnAxis

F32 = mybir.dt.float32
F32R = mybir.dt.float32r
BF16 = mybir.dt.bfloat16
U32 = mybir.dt.uint32
ALU = mybir.AluOpType
ACT = mybir.ActivationFunctionType
AX = mybir.AxisListType

P = 128
B, S, D = 2, 512, 256
SE = 1024
T = B * S
DC = D // P
TB = S // P
NT = T // P
FF = 1024
FC = FF // P
PASSES = ((0, 0), (0, 1), (1, 0))
PREPARED = 2
PIECE = 2
E = 8
NEG = -1.0e30
EPS = 1e-5
TOP = 2
SLOT = 256
SLOTS = (TOP * T + E * (SLOT - 1)) // SLOT
ST = SLOT // P


class Signal:

    def __init__(self, sem, known):
        self.sem, self.known, self.count, self.seen = sem, known, 0, {}

    def next(self, label=None, by=1):
        self.count += by
        if label is not None:
            self.seen[label] = self.count
        return self.sem, by

    def mark(self, label):
        self.seen[label] = self.count

    def when(self, label):
        return self.sem, (self.known[label] if self.known is not None else 1)

    def now(self):
        return self.sem, self.count


class Attention:

    def __init__(self, name, heads, nk, causal, group, layer):
        self.name, self.H, self.nk, self.causal, self.G = name, heads, nk, causal, group
        self.HD = D // heads
        self.scale = 1.0 / float(np.sqrt(self.HD))
        self.KT = nk // P
        self.layer = layer
        self.per_job = 2 if nk == S else 1

    def queries_from(self, kt):
        return kt * P if self.causal else 0

    def together(self, kt):
        return S // (S - self.queries_from(kt))

    def keys_to(self, qt):
        return (qt + 1) * P if self.causal else self.nk


ATTENTIONS = {
    "sa0": Attention("sa0", 16, S, True, 4, 0),
    "ca0": Attention("ca0", 16, SE, False, 4, 0),
    "sa1": Attention("sa1", 4, S, False, 2, 1),
    "ca1": Attention("ca1", 4, SE, False, 2, 1),
}
LN_OF = {"sa0": "ln1", "ca0": "ln2", "moe": "ln3"}
GAIN_BY_POOL = (("sa0", 0), ("sa0", 1), ("ca0", 0))
ATT_NO = {n: i for i, n in enumerate(ATTENTIONS)}
QUERY_PARTS = (0, 0, 1, 1, 0, 2)
KEY_PARTS = (0, 1, 0, 1, 2, 0)
KEY_PARTS_R = ((0, 0, 0), (0, 0, 64), (1, 1, 0))
RING = (4, 6)
LAG = 2


def segment(names, inserts, lead):
    groups = [(n, b, g) for n in names for b in range(B) for g in range(ATTENTIONS[n].H // ATTENTIONS[n].G)]
    first, first_at, units, unit_at = [], [0], [], [0]
    for n, b, g in groups:
        a = ATTENTIONS[n]
        hs = range(g * a.G, (g + 1) * a.G, a.per_job)
        jobs = [("max", n, b, h, qt) for h in hs for qt in range(TB)] + [("parts", n, b, g)]
        if first:
            jobs.insert(2, ("shift",) + groups[len(first_at) - 2])
        if (n, b, g) == groups[-1]:
            jobs.append(("shift", n, b, g))
        first += jobs
        units += [(n, b, g, kt, j) for kt in range(a.KT) for j in range(0, a.G, a.together(kt))]
        first_at.append(len(first))
        unit_at.append(len(units))
    first_at += [len(first)] * 2
    units = [u + (i,) for i, u in enumerate(units)]
    out, at, held = [], 0, []
    for gi, (n, b, g) in enumerate(groups):
        a = ATTENTIONS[n]
        size = unit_at[gi + 1] - unit_at[gi]
        for i in range(unit_at[gi], unit_at[gi + 1]):
            part = (i + 1 - unit_at[gi]) / size
            want = first_at[gi + 1] + int(np.ceil(part * (first_at[gi + 2] - first_at[gi + 1]))) + lead
            while at < min(want, len(first)):
                out.append(first[at])
                at += 1
            out.append(("unit",) + units[i])
            held.append((i + LAG, 0, ("pv",) + units[i]))
            if a.layer and units[i][3] > 0:
                held.append((i + LAG, 1, ("sum",) + units[i]))
            if i + 1 == unit_at[gi + 1]:
                held.append((i + LAG, 2, ("evict", n, b, g)))
                held.append((i + 4, 3, ("norm", n, b, g)))
                if g == a.H // a.G - 1:
                    held.append((i + 8, 3, ("heads", n, b)))
                    held.append((i + 11, 3, ("proj", n, b)))
                    if a.layer == 0:
                        held.append((i + 12, 3, ("stats", n, b)))
                        held.append((i + 14, 3, ("centre", n, b)))
                        held.append((i + 17, 3, ("turn", n, b)))
                        held.append((i + 18, 4, ("gain", n, b)))
            for x in sorted(x for x in held if x[0] <= i):
                out.append(x[2])
            held = [x for x in held if x[0] > i]
            out += inserts.get(i, [])
    out += first[at:]
    out += [x[2] for x in sorted(held)]
    return groups, {u[-1]: u for u in units}, out


def split_steps(name, which, u):
    return [("split", name, which, u, c) for c in range(DC)]


def stack_steps(name, which, u):
    return [("stack", name, which, u, c) for c in range(DC)]


def schedule():
    inserts = {}

    def insert(at, *steps):
        inserts.setdefault(at, []).extend(steps)

    start = [("turn_x", 0)]
    for c in range(DC):
        start += [("split", "sa0", "k", 0, c), ("split", "sa0", "q", 0, c)]
        start += [("stack", "sa0", "k", 0, c), ("stack", "sa0", "q", 0, c)]
    start += [("turn_x", 1), ("v", "sa0", 0)]
    insert(0, ("load", "ctx0"))
    insert(3, ("load", "ctx1"))
    insert(10, ("load", "rows"))
    for u in range(B * SE // S):
        insert((9, 13, 18, 21)[u], ("turn_ctx", u))
    for c in range(DC):
        insert(11 + 3 * c, ("split", "sa0", "k", 1, c))
        insert(12 + 3 * c, ("split", "sa0", "q", 1, c), ("stack", "sa0", "k", 1, c), ("stack", "sa0", "q", 1, c))
    insert(16, ("load", "wca0"))
    insert(18, ("v", "sa0", 1))
    for i in range(8):
        u, c = i // DC, i % DC
        insert(27 + 4 * i, ("split", "ca0", "k", u, c))
        if u < 2:
            insert(29 + 4 * i, ("stack", "ca0", "k", u, c))
    for t in range(SLOTS):
        insert(92 + 4 * t, ("fill", t))
    insert(65, ("v", "ca0", 0))
    insert(70, ("v", "ca0", 1))
    insert(62, ("split", "ca0", "q", 0, 0), ("stack", "ca0", "q", 0, 0))
    insert(64, ("split", "ca0", "q", 0, 1), ("stack", "ca0", "q", 0, 1))
    insert(94, ("v", "ca0", 2), *stack_steps("ca0", "k", 2))
    insert(106, ("v", "ca0", 3), *stack_steps("ca0", "k", 3))
    insert(118, ("split", "ca0", "q", 1, 0), ("stack", "ca0", "q", 1, 0))
    insert(122, ("split", "ca0", "q", 1, 1), ("stack", "ca0", "q", 1, 1))
    insert(120, ("load", "wsa1"))
    insert(242, ("route", 0))
    parts = {"A": segment(["sa0", "ca0"], inserts, 7)}
    inserts = {}
    insert(3, ("split", "sa1", "k", 1, 1), ("split", "sa1", "q", 1, 1))
    insert(6, ("v", "sa1", 1))
    insert(8, ("load", "mlp_sa1"))
    insert(29, ("prepare", "sa1"))
    parts["B"] = segment(["sa1"], inserts, 4)
    parts["C"] = segment(["ca1"], {36: [("load", "mlp_ca1")], 56: [("prepare", "ca1")]}, 6)
    steps = start + parts["A"][2] + [("load", "wca1"), ("route", 1), ("moe",)]
    steps += [("combine", 0), ("stats", "moe", 0), ("centre", "moe", 0), ("combine", 1)]
    steps += [("turn", "moe", 0), ("stats", "moe", 1)] + split_steps("sa1", "k", 0)
    steps += [("centre", "moe", 1)] + split_steps("sa1", "q", 0) + [("turn", "moe", 1), ("v", "sa1", 0)]
    steps += [("split", "sa1", "k", 1, 0), ("split", "sa1", "q", 1, 0)]
    steps += parts["B"][2] + [("mlp", "sa1")]
    for u in range(B * SE // S):
        steps += stack_steps("ca1", "k", u)
    for u in range(B):
        steps += split_steps("ca1", "q", u)
    steps += [("v", "ca1", u) for u in range(B * SE // S)]
    steps += parts["C"][2] + [("mlp", "ca1"), ("out",)]
    return steps, parts


STEPS, PARTS = schedule()
GROUP_NO = {g: i for groups, _, _ in PARTS.values() for i, g in enumerate(groups)}
SEGMENT = {g[0]: part for part, (groups, _, _) in PARTS.items() for g in groups}
UNITS = {part: units for part, (_, units, _) in PARTS.items()}
LAST_UNIT = {u[0:3]: u for units in UNITS.values() for u in units.values()}
SPLITS = []
for _s in STEPS:
    if _s[0] == "split" and not (ATTENTIONS[_s[1]].layer):
        SPLITS.append(_s[1:])
    if _s[0] == "moe":
        SPLITS += [("ca1", "k", _v, _c) for _v in range(B * SE // S) for _c in range(DC)]
SPLIT_NO = {j: i for i, j in enumerate(SPLITS)}


def program(nc, io, known):
    ctx = ExitStack()
    signals = {}

    with ctx:
        place_of = {}

        def sb(name, shape, dt=F32):
            place_of[name] = -(-nc.sbuf_base // 32) * 32
            return ctx.enter_context(nc.sbuf_tensor(name, shape, dt))

        def signal(name):
            s = Signal(ctx.enter_context(nc.semaphore(name)), None if known is None else known[name])
            signals[name] = s
            return s

        ident = sb("ident", [P, P])
        identb = sb("identb", [P, P], BF16)
        mask_q = sb("mask_q", [P, P], BF16)
        mask_k = sb("mask_k", [P, P], BF16)
        onesb = sb("onesb", [P, P], BF16)
        onesf = sb("onesf", [P, 32])
        minus_half = sb("minus_half", [P, TB])
        expert_no = sb("expert_no", [P, E])
        xT = sb("xT", [P, DC, T])
        xtok = sb("xtok", [P, NT, D])
        ctxT = sb("ctxT", [P, DC, B * SE])
        wset = [sb(f"wset{i}", [P, 4, DC, D]) for i in range(2)]
        arena = sb("arena", [P, 49152], BF16)
        vx = sb("vx", [P, 16 * 272 + 16])
        oT = sb("oT", [P, DC, S])
        parts_f = sb("parts_f", [P, 2, 2, S])
        probs = sb("probs", [P, 4, S])
        sums = sb("sums", [P, S])
        rest = sb("rest", [P, S])
        
        otok = sb("otok", [P, TB, D])
        negmax = sb("negmax", [P, 2, TB, 4])
        shift_parts = sb("shift_parts", [12, S], BF16)
        shift_r = sb("shift_r", [4, S], F32R)
        maxb = sb("maxb", [P, TB, 3, 4], BF16)
        maxr = sb("maxr", [P, TB, 2, 2], F32R)
        maxrest = sb("maxrest", [P, TB, 4])
        rden = sb("rden", [P, TB, 4])
        biasT = {n: sb(f"biasT_{n}", [P, DC]) for n in ("sa_bq", "sa_bk", "ca_bq", "ca_bk")}
        gainT = {ln: sb(f"gainT_{ln}", [P, 2, DC]) for ln in LN_OF.values()}
        row_names = ("sa_bv", "sa_bo", "ca_bv", "ca_bo", "ln1_g", "ln1_b", "ln2_g", "ln2_b", "ln3_g", "ln3_b")
        rows = sb("rows", [P, len(row_names) * D])
        row = {n: rows[:, i * D:(i + 1) * D] for i, n in enumerate(row_names)}
        den_sum = rows[:, 0:2 * S].rearrange("p (j t) -> p j t", j=2)
        prob_bufs = [probs[:, i, :] for i in range(4)] + [rows[:, (2 + i) * S:(3 + i) * S] for i in range(2)]
        stats = sb("stats", [P, TB, 6])
        mv = sb("mv", [P, TB, 2])
        var = sb("var", [P, TB])
        negmean = sb("negmean", [P, TB])
        offset = sb("offset", [P, TB])
        rstd = sb("rstd", [P, TB])
        rw = sb("rw", [P, DC, E])
        rb = sb("rb", [P, E])
        b1T = sb("b1T", [P, E, FC])
        b1_slot = sb("b1_slot", [P, 2, FC])
        small = sb("small", [P, 6, NT])
        below = sb("below", [P, P], BF16)
        placed = sb("placed", [P, TOP, NT])
        place_no = sb("place_no", [P, TOP, NT], U32)
        slot_no = sb("slot_no", [1, SLOTS])
        slot_ef = sb("slot_ef", [1, SLOTS])
        slot_e = sb("slot_e", [1, SLOTS], U32)
        def table(n, *shape, at=[0]):
            view = vx[:, at[0]:at[0] + n]
            at[0] += n
            if len(shape) == 1:
                return view
            names = "abc"[:len(shape)]
            return view.rearrange("p (%s) -> p %s" % (" ".join(names), " ".join(names)), **dict(zip(names, shape)))

        lg = rest[:, 0:NT * E].rearrange("p (t e) -> p t e", e=E)
        best = table(NT * 8, NT, 8)
        besti = table(NT * 8, NT, 8).bitcast(U32)
        bestf = table(NT * 8, NT, 8)
        comb = table(NT * E, NT, E)
        chosen = table(TOP * NT * E, TOP, NT, E)
        chosenb = table(NT * E // 2, NT * E // 2).bitcast(BF16).rearrange("p (t e) -> p t e", e=E)
        rank = table((NT + 1) * E, NT + 1, E)
        ends = table(4 * (4 + E), 4, 4 + E)
        place = table(NT * E, NT, E)
        past = table(SLOTS * E, SLOTS, E)[0:1]
        b2 = table(D, D)[0:E]
        combT = otok[0:E, :, :].rearrange("e t d -> e (t d)")

        a_bank = [ctx.enter_context(nc.psum_tensor(f"a_bank{i}", [P, 2 * 512], F32)) for i in range(2)]
        b_bank = [ctx.enter_context(nc.psum_tensor(f"b_bank{i}", [P, 512], F32)) for i in range(2)]
        o_bank = [ctx.enter_context(nc.psum_tensor(f"o_bank{i}", [P, 512], F32)) for i in range(2)]

        arena_f = arena[:, :].bitcast(F32)
        ctx_in = arena_f[:, 8192:8192 + 16 * D].rearrange("p (t d) -> p t d", t=16)

        def w1_part(i, part=None):
            room, at = (arena_f, 0) if part is None else (arena_r, 8192 if part == 0 else 0)
            return room[:, at + 2048 * i:at + 2048 * (i + 1)]

        def w2_part(i, part=None):
            room, at = (arena_f, 4096) if part is None else (arena_r, 12288 if part == 0 else 4096)
            return room[:, at + 2048 * i:at + 2048 * (i + 1)]

        def slot_hid(i, part):
            at = 16384 + 4096 * i + 2048 * part
            return arena_r[:, at:at + 2048].rearrange("p (c t) -> p c t", c=FC)

        def slot_x(i, part):
            return parts_r[:, i, part, :].rearrange("p (c t) -> p c t", c=DC)

        slot_gelu = probs[:, :, :].rearrange("p i t -> p (i t)").rearrange("p (c t) -> p c t", c=FC)
        xS = [oT[:, i, :].rearrange("p (t d) -> p t d", t=ST) for i in range(2)]
        yS = [x[:, :].rearrange("p (t d) -> p t d", t=ST) for x in (sums, rest)]
        back = arena_f[:, 8192:8192 + TOP * NT * D].rearrange("p (k t d) -> p k t d", k=TOP, t=NT)
        b1S = [b1_slot[:, i, :] for i in range(2)]

        def mlp_low(name, i, loaded=False):
            at = (8192 if name == "sa1" else 16384) + 2048 * i
            return (arena_f if loaded else arena_r)[:, at:at + 2048]

        def mlp_high(i):
            return arena_r[:, 2048 * i:2048 * (i + 1)]

        def mlp_x(name, hf, part):
            at = {"sa1": (14336, 16384), "ca1": (22528, 8192)}[name][hf] + part * DC * S
            return arena_r[:, at:at + DC * S].rearrange("p (c t) -> p c t", c=DC)

        def mlp_h(name, f, part):
            i = 2 * f + part
            if i < 4:
                at = 6144 + i * S
            else:
                at = (18432 if name == "sa1" else 10240) + (i - 4) * S
            return arena_r[:, at:at + S]

        gate, hidden = probs[:, 0:2, :], probs[:, 2:4, :]

        def q_stack(a, b, i=0):
            if a.layer:
                at = (b * 2 + i) * a.H * S
                return arena_r[:, at:at + a.H * S].rearrange("p (h t) -> p h t", h=a.H)
            at = b * a.H * S
            return arena[:, at:at + a.H * S].rearrange("p (h t) -> p h t", h=a.H)

        def k_stack(a, b, i=0):
            n = a.H * a.nk
            if a.layer:
                at = (16384 + b * 2 * n if a.nk == S else 16384 - b * 8192) + i * n
                return arena_r[:, at:at + n].rearrange("p (h t) -> p h t", h=a.H)
            at = (32768 if a.causal else 16384) + b * n
            return arena[:, at:at + n].rearrange("p (h t) -> p h t", h=a.H)

        def v_tile(a, b, kt):
            if a.name == "sa0":
                return 8 + b * TB + kt
            return b * a.KT + kt

        def v_head(a, tile, h):
            if a.layer:
                return vx[:, tile * D + h * 64:tile * D + h * 64 + 64]
            return vx[:, tile * 272 + h * 17:tile * 272 + h * 17 + 32]

        scratch_q = nc.dram_tensor("scratch_q", (2, 3, D, T), BF16, kind="Internal").ap()
        sent = nc.dram_tensor("sent", (SLOTS * SLOT, D), F32, kind="Internal").ap()
        computed = nc.dram_tensor("computed", (SLOTS * SLOT, D), F32, kind="Internal").ap()
        scratch_k = nc.dram_tensor("scratch_k", (2, 3, D, B * SE), BF16, kind="Internal").ap()
        scratch_kr = nc.dram_tensor("scratch_kr", (2, D, B * SE), F32, kind="Internal").ap()

        arena_r = nc.alloc_sbuf_tensor_at("arena_r", [P, 24576], F32R, offset=place_of["arena"])
        parts = nc.alloc_sbuf_tensor_at("parts_b", [P, 2, 3, S], BF16, offset=place_of["parts_f"])
        parts_r = nc.alloc_sbuf_tensor_at("parts_r", [P, 2, 2, S], F32R, offset=place_of["parts_f"])

        a_full = signal("a_full")
        b_full = signal("b_full")
        pv_done = signal("pv_done")
        a_free = signal("a_free")
        vec = signal("vec")
        b_free = signal("b_free")
        act_done = signal("act_done")
        pool_done = signal("pool_done")
        load = {n: signal("load_" + n) for n in
                ("x0", "x1", "bias", "ctx0", "ctx1", "wsa0", "wca0", "wsa1", "wca1", "rows", "b2", "mlp_sa1", "mlp_ca1")}
        w1_load = [signal(f"load_w1_{i}") for i in range(2)]
        w2_load = [signal(f"load_w2_{i}") for i in range(2)]
        part_out = [signal(f"part_out{i}") for i in range(2)]
        stack_in = {(n, b, c): signal(f"stack_in_{n}_{b}_{c}") for n in ATTENTIONS if n != "sa1"
                    for b in range(B) for c in range(DC)}
        shift_in = [signal(f"shift_in{i}") for i in range(2)]
        stored = signal("stored")
        filled = signal("filled")
        sent_out = signal("sent_out")
        b1_load = [signal(f"b1_load{i}") for i in range(2)]
        slot_in = [signal(f"slot_in{i}") for i in range(2)]
        slot_out = [signal(f"slot_out{i}") for i in range(2)]
        back_in = [signal(f"back_in{t}") for t in range(NT)]
        a_keys, b_keys = [], []
        a_turn = {} if known is None else known["_a_turn"]
        b_turn = {} if known is None else known["_b_turn"]

        def a_slot(key):
            return a_bank[a_turn.get(key, 0)]

        def b_slot(key):
            return b_bank[b_turn.get(key, 0)]

        def before(name, b, g, k=1):
            groups = PARTS[SEGMENT[name]][0]
            i = GROUP_NO[name, b, g] - k
            return groups[i] if i >= 0 else None

        def last_max(a, b, g):
            return ("max", a.name, b, (g + 1) * a.G - a.per_job, TB - 1)

        block = ctx.enter_context(nc.Block())

        @block.tensor
        def _(pe):
            def take_a(key):
                if len(a_keys) >= 2:
                    pe.wait_ge(*a_free.when(a_keys[-2]))
                a_keys.append(key)
                return a_bank[(len(a_keys) - 1) % 2]

            def take_b(key):
                if len(b_keys) >= 2:
                    pe.wait_ge(*b_free.when(b_keys[-2]))
                b_keys.append(key)
                return b_bank[(len(b_keys) - 1) % 2]

            waited = set()

            def once(signal_name, sig, label):
                if (signal_name, label) not in waited:
                    waited.add((signal_name, label))
                    pe.wait_ge(*sig.when(label))

            def turn(key, tiles):
                pair = take_a(key)
                for t, tile in enumerate(tiles):
                    for c in range(DC):
                        mm = pe.transpose(pair[:, c * S + t * P:c * S + (t + 1) * P],
                                          tile[:, c * P:(c + 1) * P], ident[:, :])
                mm.then_inc(*a_full.next(key))

            def tokens_of(b):
                return [xtok[:, b * TB + t, :] for t in range(TB)]

            def turn_ctx(u):
                once(("ctx", u * S // SE), load["ctx%d" % (u * S // SE)], "all")
                for c in range(DC):
                    bank = take_b(("ctx", u, c))
                    for t in range(TB):
                        mm = pe.transpose(bank[:, t * P:(t + 1) * P], ctx_in[:, u * TB + t, c * P:(c + 1) * P],
                                          ident[:, :])
                    mm.then_inc(*b_full.next(("ctx", u, c)))

            def source(name, of_context, u):
                once("w" + name, load["w" + name], "all")
                if of_context:
                    once("b_free", b_free, ("ctx", B * SE // S - 1, DC - 1))
                    return ctxT
                once("a_free", a_free, {"sa0": ("turn_x", u), "ca0": ("turn", "sa0", u),
                                        "sa1": ("turn", "moe", u), "ca1": ("down", "sa1", u)}[name])
                return xT

            def project_chunk(name, which, u, c):
                a = ATTENTIONS[name]
                w = wset[ATT_NO[name] % 2][:, "qk".index(which)]
                src = source(name, which == "k" and a.nk != S, u)
                key = ("split", name, which, u, c)
                pair = take_a(key)
                for k in range(DC):
                    mm = pe.matmul(pair[:, 0:S], w[:, k, c * P:(c + 1) * P], src[:, k, u * S:(u + 1) * S],
                                   start=(k == 0), stop=(k == DC - 1))
                mm.then_inc(*a_full.next(key))

            def project_T(key, w, src, at):
                pair = take_a(key)
                for dc in range(DC):
                    for c in range(DC):
                        mm = pe.matmul(pair[:, dc * S:(dc + 1) * S], w[:, c, dc * P:(dc + 1) * P],
                                       src[:, c, at:at + S], start=(c == 0), stop=(c == DC - 1))
                mm.then_inc(*a_full.next(key))

            def project_tok(key, w, src, at):
                pair = take_a(key)
                for t in range(TB):
                    for c in range(DC):
                        mm = pe.matmul(pair[:, t * D:(t + 1) * D], src[:, c, at + t * P:at + (t + 1) * P],
                                       w[:, c, :], start=(c == 0), stop=(c == DC - 1))
                mm.then_inc(*a_full.next(key))

            def score_passes(a, b, h, queries, keys, with_shift):
                if a.layer:
                    return [(q_stack(a, b, i)[0:rows, h, queries], k_stack(a, b, i)[0:rows, h, keys])
                            for i, rows in enumerate((P, 66))]
                rows = 99 if with_shift else 96
                return [(q_stack(a, b)[0:rows, h, queries], k_stack(a, b)[0:rows, h, keys])]

            def maxima(step):
                _, name, b, h, qt = step
                a = ATTENTIONS[name]
                if name != "sa1":
                    c = h * a.HD // P
                    once(("stack_in", name, b, c), stack_in[name, b, c], "all")
                if a.layer:
                    once("a_free", a_free, ("split", name, "q", b, h * a.HD // P))
                    if name == "sa1":
                        once("a_free", a_free, ("split", name, "k", b, h * a.HD // P))
                    once("pool_done", pool_done, ("rows", name, b))
                pair = take_a(step)
                nk = a.keys_to(qt)
                for hh in range(a.per_job):
                    for k0 in range(0, nk, 512):
                        n = min(512, nk - k0)
                        at = hh * S + k0
                        ps = score_passes(a, b, h + hh, slice(qt * P, (qt + 1) * P), slice(k0, k0 + n), False)
                        for i, (q, k) in enumerate(ps):
                            mm = pe.matmul(pair[:, at:at + n], q, k, start=(i == 0),
                                           stop=(i == len(ps) - 1 and not a.causal))
                    if a.causal:
                        at = hh * S + qt * P
                        mm = pe.matmul(pair[:, at:at + P], identb[:, :], mask_q[:, :],
                                       start=False, stop=True)
                mm.then_inc(*a_full.next(step))

            def shift_turn(step):
                _, name, b, g = step
                bank = take_b(step)
                pe.wait_ge(*vec.when(("parts",) + step[1:]))
                for qt in range(TB):
                    out = bank[0:4 if ATTENTIONS[name].layer else 12, qt * P:(qt + 1) * P]
                    if ATTENTIONS[name].layer:
                        mm = pe.transpose(out, maxr[:, qt, :, :].rearrange("p r h -> p (r h)").bitcast(F32), ident[:, :])
                    else:
                        mm = pe.matmul(out, maxb[:, qt, :, :].rearrange("p r h -> p (r h)"), identb[:, :],
                                       start=True, stop=True)
                mm.then_inc(*b_full.next(step))

            def unit(step):
                _, name, b, g, kt, j, n = step
                a = ATTENTIONS[name]
                h = g * a.G + j
                q0 = a.queries_from(kt)
                once("shift_in" + name, shift_in[GROUP_NO[name, b, g] % 2], (name, b, g))
                if not a.layer:
                    once("pool_done", pool_done, ("shift_ones", name))
                key = ("unit", SEGMENT[name], n)
                bank = take_b(key)
                w = S - q0
                for hh in range(a.together(kt)):
                    at = hh * w
                    ps = score_passes(a, b, h + hh, slice(q0, S), slice(kt * P, (kt + 1) * P), True)
                    for i, (q, k) in enumerate(ps):
                        mm = pe.matmul(bank[:, at:at + w], k, q, start=(i == 0),
                                       stop=(i == len(ps) - 1 and not a.causal))
                    if a.causal:
                        mm = pe.matmul(bank[:, at:at + P], identb[:, :], mask_k[:, :], start=False, stop=True)
                mm.then_inc(*b_full.next(key))

            def product(step):
                _, name, b, g, kt, j, n = step
                a = ATTENTIONS[name]
                q0 = a.queries_from(kt)
                gi = GROUP_NO[name, b, g]
                if kt == 0 and j == 0:
                    if before(name, b, g, 2):
                        pe.wait_ge(*act_done.when(("evict",) + before(name, b, g, 2)))
                    once("a_free", a_free, ("v", name, (b + 1) * a.nk // S - 1))
                pe.wait_ge(*b_free.when(("unit", SEGMENT[name], n)))
                w = P // a.G
                for hh in range(a.together(kt)):
                    p = prob_bufs[n % RING[a.layer]][:, hh * (S - q0):(hh + 1) * (S - q0)]
                    at = w * (j + hh)
                    mm = pe.matmul(o_bank[gi % 2][at:at + w, q0:S], v_head(a, v_tile(a, b, kt), g * a.G + j + hh), p,
                                   start=(kt == 0), stop=(kt == a.KT - 1), tile_position=(0, at))
                mm.then_inc(*pv_done.next((SEGMENT[name], n)))

            def norm_turn(step):
                _, name, b, g = step
                a = ATTENTIONS[name]
                pair = take_a(step)
                pe.wait_ge(*act_done.when(("evict",) + step[1:]))
                if a.layer:
                    pe.wait_ge(*vec.when(("sums", name, b, g)))
                    for j in range(a.G):
                        for qt in range(TB):
                            at = S + j * TB + qt
                            pe.matmul(pair[:, at:at + 1], den_sum[:, j, qt * P:(qt + 1) * P], onesf[:, 0:1],
                                      start=True, stop=True)
                for qt in range(TB):
                    mm = pe.transpose(pair[:, qt * P:(qt + 1) * P], sums[:, qt * P:(qt + 1) * P], ident[:, :])
                mm.then_inc(*a_full.next(step))

            def heads_turn(step):
                _, name, b = step
                a = ATTENTIONS[name]
                pe.wait_ge(*a_free.when(("norm", name, b, a.H // a.G - 1)))
                turn(step, [otok[:, t, :] for t in range(TB)])

            def output_projection(step):
                _, name, b = step
                pe.wait_ge(*a_free.when(("heads", name, b)))
                w = wset[ATT_NO[name] % 2][:, 3]
                (project_T if ATTENTIONS[name].layer else project_tok)(step, w, oT, 0)

            def turn_normalised(step):
                _, name, b = step
                pe.wait_ge(*act_done.when(("centre", name, b)))
                turn(step, tokens_of(b))

            def route(step):
                b = step[1]
                once("a_free", a_free, ("turn", "ca0", b))
                pair = take_a(step)
                for t in range(TB):
                    for c in range(DC):
                        at = b * S + t * P
                        mm = pe.matmul(pair[:, t * E:(t + 1) * E], xT[:, c, at:at + P], rw[:, c, :],
                                       start=(c == 0), stop=(c == DC - 1))
                mm.then_inc(*a_full.next(step))

            def experts_step():
                def slot_turn(s):
                    pair = take_a(("xs", s))
                    pe.wait_ge(*slot_in[s % 2].when(s))
                    for t in range(ST):
                        for c in range(DC):
                            mm = pe.transpose(pair[:, c * SLOT + t * P:c * SLOT + (t + 1) * P],
                                              xS[s % 2][:, t, c * P:(c + 1) * P], ident[:, :])
                    mm.then_inc(*a_full.next(("xs", s)))

                def slot_hidden(s):
                    pe.wait_ge(*vec.when(("w1", s)))
                    pe.wait_ge(*a_free.when(("xs", s)))
                    w = [w1_part(s % 2, part).rearrange("p (c f) -> p c f", c=DC) for part in range(2)]
                    for f in range(FC):
                        bank = take_b(("h", s, f))
                        for i, (c, (m, n)) in enumerate(((c, p) for c in range(DC) for p in PASSES)):
                            mm = pe.matmul(bank[:, 0:SLOT], w[m][:, c, f * P:(f + 1) * P],
                                           slot_x(s % 2, n)[:, c, :], start=(i == 0), stop=(i == 3 * DC - 1))
                        mm.then_inc(*b_full.next(("h", s, f)))

                def slot_result(s):
                    pair = take_a(("eo", s))
                    pe.wait_ge(*vec.when(("w2", s)))
                    w = [w2_part(s % 2, part).rearrange("p (c n) -> p c n", c=FC) for part in range(2)]
                    for t in range(ST):
                        for i, (f, (m, n)) in enumerate(((f, p) for f in range(FC) for p in PASSES)):
                            if t == 0 and i % (3 * PIECE) == 0:
                                pe.wait_ge(*vec.when(("h", s, f // PIECE)))
                            mm = pe.matmul(pair[:, t * D:(t + 1) * D], slot_hid(s % 2, m)[:, f, t * P:(t + 1) * P],
                                           w[n][:, f, :], start=(i == 0), stop=(i == 3 * FC - 1))
                    mm.then_inc(*a_full.next(("eo", s)))

                def ranks():
                    pair = take_a(("rank",))
                    pe.wait_ge(*vec.when("chosen"))
                    for t in range(NT):
                        pe.matmul(pair[:, (t + 1) * E:(NT + 1) * E], onesb[:, :],
                                  chosenb[:, t, :].unsqueeze(1).to_broadcast([P, NT - t, E]),
                                  start=(t == 0), stop=False, skip_group_check=True)
                    pe.matmul(pair[:, 0:NT * E], below[:, :], chosenb[:, :, :].rearrange("p t e -> p (t e)"),
                              start=False, stop=True, skip_group_check=True).then_inc(*a_full.next(("rank",)))

                def share_of_b2():
                    pair = take_a(("combT",))
                    pe.wait_ge(*vec.when("comb"))
                    for t in range(NT):
                        mm = pe.transpose(pair[0:E, t * P:(t + 1) * P], comb[:, t, :], ident[:, :])
                    mm.then_inc(*a_full.next(("combT",)))
                    pe.wait_ge(*a_free.when(("combT",)))
                    for b in range(B):
                        pair = take_a(("b2", b))
                        for t in range(TB):
                            at = (b * TB + t) * P
                            mm = pe.matmul(pair[:, t * D:(t + 1) * D], combT[:, at:at + P], b2[:, :],
                                           start=True, stop=True)
                        mm.then_inc(*a_full.next(("b2", b)))

                ranks()
                for u in range(B * SE // S):
                    for c in range(DC):
                        project_chunk("ca1", "k", u, c)
                once("b2", load["b2"], "all")
                share_of_b2()
                slot_turn(0)
                slot_turn(1)
                slot_hidden(0)
                for s in range(SLOTS):
                    if s + 1 < SLOTS:
                        slot_hidden(s + 1)
                    if s + 2 < SLOTS:
                        slot_turn(s + 2)
                    slot_result(s)

            def mlp(name):
                def halves(i, c):
                    return [w.rearrange("p (c f) -> p c f", c=c) for w in (mlp_high(i), mlp_low(name, i))]

                (wg, wu), wd = (halves(0, DC), halves(1, DC)), halves(2, FC)
                for hf in range(B):
                    pe.wait_ge(*vec.when(("x", name, hf)))
                    x = [mlp_x(name, hf, part) for part in range(2)]
                    for f in range(FC):
                        bank = take_b(("g", name, hf, f))
                        if hf == 0:
                            pe.wait_ge(*vec.when(("w", name, f)))
                        for i, (c, (m, n)) in enumerate(((c, p) for c in range(DC) for p in PASSES)):
                            mm = pe.matmul(bank[:, :], wg[m][:, c, f * P:(f + 1) * P], x[n][:, c, :],
                                           start=(i == 0), stop=(i == 3 * DC - 1))
                        mm.then_inc(*b_full.next(("g", name, hf, f)))
                        pair = take_a(("u", name, hf, f))
                        for i, (c, (m, n)) in enumerate(((c, p) for c in range(DC) for p in PASSES)):
                            mm = pe.matmul(pair[:, 0:S], wu[m][:, c, f * P:(f + 1) * P], x[n][:, c, :],
                                           start=(i == 0), stop=(i == 3 * DC - 1))
                        mm.then_inc(*a_full.next(("u", name, hf, f)))
                    pair = take_a(("down", name, hf))
                    if hf == 0:
                        pe.wait_ge(*pool_done.when(("wd", name)))
                    for dc in range(DC):
                        for i, (f, (m, n)) in enumerate(((f, p) for f in range(FC) for p in PASSES)):
                            if dc == 0 and i % 3 == 0:
                                pe.wait_ge(*vec.when(("h", name, hf, f)))
                            mm = pe.matmul(pair[:, dc * S:(dc + 1) * S], wd[m][:, f, dc * P:(dc + 1) * P],
                                           mlp_h(name, f, n), start=(i == 0), stop=(i == 3 * FC - 1))
                    mm.then_inc(*a_full.next(("down", name, hf)))

            def out_turn():
                for b in range(B):
                    pe.wait_ge(*a_free.when(("down", "ca1", b)))
                    pair = take_a(("out", b))
                    for t in range(TB):
                        for c in range(DC):
                            at = (b * TB + t) * P
                            mm = pe.transpose(pair[:, t * D + c * P:t * D + (c + 1) * P], xT[:, c, at:at + P],
                                              ident[:, :])
                    mm.then_inc(*a_full.next(("out", b)))

            pe.wait_ge(*pool_done.when("constants"))
            for step in STEPS:
                kind = step[0]
                if kind == "turn_x":
                    pe.wait_ge(*load["x%d" % step[1]].when("all"))
                    turn(step, tokens_of(step[1]))
                elif kind == "turn_ctx":
                    turn_ctx(step[1])
                elif kind == "split":
                    project_chunk(*step[1:])
                elif kind == "v":
                    _, name, u = step
                    src = source(name, ATTENTIONS[name].nk != S, u)
                    project_tok(step, wset[ATT_NO[name] % 2][:, 2], src, u * S)
                elif kind == "max":
                    maxima(step)
                elif kind == "shift":
                    shift_turn(step)
                elif kind == "unit":
                    unit(step)
                elif kind == "pv":
                    product(step)
                elif kind == "norm":
                    norm_turn(step)
                elif kind == "heads":
                    heads_turn(step)
                elif kind == "proj":
                    output_projection(step)
                elif kind == "turn":
                    turn_normalised(step)
                elif kind == "route":
                    route(step)
                elif kind == "moe":
                    experts_step()
                elif kind == "mlp":
                    mlp(step[1])
                elif kind == "out":
                    out_turn()

        @block.vector
        def _(dve):
            def copy_T(key, dst):
                dve.wait_ge(*a_full.when(key))
                dve.tensor_copy(dst, a_slot(key)[:, :].rearrange("p (c t) -> p c t", c=DC))\
                   .then_inc(*a_free.next(key))

            def split_in_place(name, which, u, c):
                a = ATTENTIONS[name]
                key = ("split", name, which, u, c)
                dve.wait_ge(*act_done.when(key))
                for h in range(DC * c, DC * c + 2):
                    at = h % 2 * 64
                    if which == "q":
                        high = q_stack(a, u)[at:at + 64, h, :]
                        low = q_stack(a, u)[64 - at:128 - at, h, :]
                    else:
                        high, low = k_stack(a, u)[at:at + 64, h, :], k_stack(a, u, 1)[0:64, h, :]
                    dve.tensor_tensor(low, a_slot(key)[at:at + 64, 0:S], high.bitcast(F32), ALU.subtract)\
                       .then_inc(*a_free.next(key) if h % 2 else vec.next())

            def split(name, which, u, c):
                a = ATTENTIONS[name]
                key = ("split", name, which, u, c)
                i = SPLIT_NO[name, which, u, c]
                dve.wait_ge(*act_done.when(("high", i)))
                if a.layer:
                    dve.tensor_tensor(parts_r[:, i % 2, 1, :], a_slot(key)[:, 0:S], parts_r[:, i % 2, 0, :].bitcast(F32),
                                      ALU.subtract).then_inc(*a_free.next(key))
                else:
                    bias = biasT[name[:2] + "_b" + which]
                    part = parts[:, i % 2]
                    dve.wait_ge(*vec.now())
                    if name == "ca0" and SPLITS[i - 1][0] == "ca0":
                        dve.wait_ge(*pool_done.when(("split", i - 1)))
                    dve.scalar_tensor_tensor(out=rest[:, :], in0=a_slot(key)[:, 0:S], scalar=bias[:, c:c + 1],
                                             in1=part[:, 0, :], op0=ALU.add, op1=ALU.subtract)\
                       .then_inc(*a_free.next(key))
                    if name == "ca0":
                        return
                    dve.wait_ge(*a_free.now())
                    dve.tensor_copy(part[:, 1, :], rest[:, :]).then_inc(*vec.next())
                    dve.wait_ge(*vec.now())
                    dve.tensor_tensor(part[:, 2, :], rest[:, :], part[:, 1, :], ALU.subtract)\
                       .then_inc(*vec.next(("split", i)))

            def values(name, u):
                a = ATTENTIONS[name]
                key = ("v", name, u)
                dve.wait_ge(*a_full.when(key))
                pair = a_slot(key)
                if a.layer == 0:
                    dve.wait_ge(*load["bias" if name == "sa0" else "rows"].when("all"))
                    for t in range(TB):
                        tile = v_tile(a, u * S // a.nk, u % (a.nk // S) * TB + t)
                        dst = vx[:, tile * 272:tile * 272 + 272].rearrange("p (h d) -> p h d", d=17)[:, :, 0:16]
                        ins = dve.tensor_tensor(dst, pair[:, t * D:(t + 1) * D].rearrange("p (h d) -> p h d", d=16),
                                                row[name[:2] + "_bv"].rearrange("p (h d) -> p h d", d=16),
                                                ALU.add)
                        ins.then_inc(*(a_free.next(key) if t == TB - 1 else vec.next()))
                else:
                    at = u * TB * D
                    dve.tensor_copy(vx[:, at:at + TB * D], pair[:, :]).then_inc(*a_free.next(key))

            def maxima(step):
                _, name, b, h, qt = step
                a = ATTENTIONS[name]
                gi, j = GROUP_NO[name, b, h // a.G], h % a.G
                dve.wait_ge(*a_full.when(step))
                if a.per_job == 1:
                    scores = a_slot(step)[:, 0:a.keys_to(qt)]
                else:
                    scores = a_slot(step)[:, :].rearrange("p (h k) -> p h k", h=2)[:, :, 0:a.keys_to(qt)]
                dve.tensor_reduce(negmax[:, gi % 2, qt, j:j + a.per_job], scores,
                                  AX.X, ALU.max, negate=True).then_inc(*a_free.next(step))

            def max_parts(step):
                _, name, b, g = step
                a = ATTENTIONS[name]
                m = negmax[:, GROUP_NO[name, b, g] % 2, :, 0:a.G]
                dve.wait_ge(*a_free.when(last_max(a, b, g)))
                if before(name, b, g):
                    dve.wait_ge(*b_full.when(("shift",) + before(name, b, g)))
                if a.layer:
                    dve.tensor_copy(maxr[:, :, 0, :], m).then_inc(*vec.next())
                    dve.wait_ge(*vec.now())
                    dve.tensor_tensor(maxr[:, :, 1, :], m, maxr[:, :, 0, :].bitcast(F32), ALU.subtract)\
                       .then_inc(*vec.next(step))
                    return
                dve.tensor_copy(maxb[:, :, 0, :], m).then_inc(*vec.next())
                dve.wait_ge(*vec.now())
                dve.tensor_tensor(maxrest[:, :, :], m, maxb[:, :, 0, :], ALU.subtract).then_inc(*vec.next())
                dve.wait_ge(*vec.now())
                dve.tensor_copy(maxb[:, :, 1, :], maxrest[:, :, :]).then_inc(*vec.next())
                dve.wait_ge(*vec.now())
                dve.tensor_tensor(maxb[:, :, 2, :], maxrest[:, :, :], maxb[:, :, 1, :], ALU.subtract)\
                   .then_inc(*vec.next(step))

            def denominators(step):
                _, name, b, g, kt, j, n = step
                a = ATTENTIONS[name]
                dve.wait_ge(*b_free.when(("unit", SEGMENT[name], n)))
                if kt == 1:
                    if before(name, b, g):
                        dve.wait_ge(*a_full.when(("norm",) + before(name, b, g)))
                    so_far = prob_bufs[(n - a.G) % RING[1]]
                else:
                    dve.wait_ge(*vec.when(("sum", SEGMENT[name], n - a.G)))
                    so_far = den_sum[:, j, :]
                dve.tensor_tensor(den_sum[:, j, :], so_far, prob_bufs[n % RING[1]], ALU.add)\
                   .then_inc(*vec.next(("sum", SEGMENT[name], n)))
                if kt == a.KT - 1 and j == a.G - 1:
                    vec.mark(("sums", name, b, g))

            stats_done = []

            def normalise(step):
                _, name, b, g = step
                a = ATTENTIONS[name]
                dve.wait_ge(*a_full.when(step))
                pair = a_slot(step)
                if a.layer:
                    o = pair[:, 0:S].rearrange("p (t h d) -> p t h d", t=TB, h=a.G)
                    den = pair[:, S:S + TB * a.G].rearrange("p (h t) -> p t h", t=TB)
                else:
                    o = pair[:, 0:S].rearrange("p (t h d) -> p t h d", t=TB, h=a.G)
                    den = o[:, :, :, 16]
                    o = o[:, :, :, 0:16]
                if before(name, b, g):
                    dve.wait_ge(*a_free.when(("norm",) + before(name, b, g)))
                dve.reciprocal(rden[:, :, 0:a.G], den).then_inc(*vec.next())
                dve.wait_ge(*vec.now())
                w = a.G * a.HD
                dst = otok[:, :, g * w:(g + 1) * w].rearrange("p t (h d) -> p t h d", d=a.HD)
                for t in range(TB):
                    r = rden[:, t, 0:a.G].unsqueeze(2).to_broadcast([P, a.G, a.HD])
                    ins = dve.tensor_tensor(dst[:, t], o[:, t], r, ALU.mult)
                    ins.then_inc(*(a_free.next(step) if t == TB - 1 else vec.next()))

            def residual(step):
                _, name, b = step
                dve.wait_ge(*a_full.when(step))
                pair = a_slot(step)
                if ATTENTIONS[name].layer:
                    x = xT[:, :, b * S:(b + 1) * S]
                    y = pair[:, :].rearrange("p (c t) -> p c t", c=DC)
                else:
                    dve.wait_ge(*pool_done.when(("bo", name, b)))
                    x = xtok[:, b * TB:(b + 1) * TB, :]
                    y = pair[:, :].rearrange("p (t d) -> p t d", t=TB)
                dve.tensor_tensor(x, y, x, ALU.add).then_inc(*a_free.next(step))

            def statistics(name, b):
                for t in range(TB):
                    dve.bn_stats(stats[:, t, :], xtok[:, b * TB + t, :]).then_inc(*vec.next())
                dve.wait_ge(*vec.now())
                for t in range(TB):
                    dve.bn_aggr(mv[:, t, :], stats[:, t, :]).then_inc(*vec.next())
                dve.wait_ge(*vec.now())
                if stats_done:
                    dve.wait_ge(*pool_done.when(("rstd",) + stats_done[-1]))
                stats_done.append((name, b))
                dve.tensor_scalar(var[:, :], mv[:, :, 1], EPS, None, ALU.add).then_inc(*vec.next())
                dve.tensor_scalar(negmean[:, :], mv[:, :, 0], -1.0, None, ALU.mult)\
                   .then_inc(*vec.next(("stats", name, b)))

            def turned(step):
                _, name, b = step
                dve.wait_ge(*a_full.when(step))
                for c in range(DC):
                    dve.tensor_scalar(xT[:, c, b * S:(b + 1) * S], a_slot(step)[:, c * S:(c + 1) * S],
                                      gainT[LN_OF[name]][:, 0, c:c + 1], gainT[LN_OF[name]][:, 1, c:c + 1],
                                      ALU.mult, ALU.add).then_inc(*(a_free.next(step) if c == DC - 1 else vec.next()))

            def gain_and_bias(name, b):
                x = xtok[:, b * TB:(b + 1) * TB, :]
                for kind, op in (("_g", ALU.mult), ("_b", ALU.add)):
                    dve.wait_ge(*vec.now())
                    dve.tensor_tensor(x, x, row[LN_OF[name] + kind].unsqueeze(1).to_broadcast([P, TB, D]), op)\
                       .then_inc(*vec.next(("gain", name, b)))

            def logits(step):
                dve.wait_ge(*a_full.when(step))
                dve.tensor_tensor(lg[:, step[1] * TB:(step[1] + 1) * TB, :],
                                  a_slot(step)[:, 0:TB * E].rearrange("p (t e) -> p t e", e=E),
                                  rb[:, :].unsqueeze(1).to_broadcast([P, TB, E]), ALU.add)\
                   .then_inc(*a_free.next(step))

            def experts_step():
                def link(ins):
                    ins.then_inc(*vec.next())
                    dve.wait_ge(*vec.now())

                dve.wait_ge(*a_free.when(("route", B - 1)))
                dve.wait_ge(*pool_done.when("router_constants"))
                link(dve.tensor_reduce(small[:, 0, :], lg[:, :, :], AX.X, ALU.max))
                dve.tensor_tensor(lg[:, :, :], lg[:, :, :], small[:, 0, :].unsqueeze(2).to_broadcast([P, NT, E]),
                                  ALU.subtract).then_inc(*vec.next("logits"))
                dve.wait_ge(*act_done.when("router_exp"))
                link(dve.tensor_reduce(small[:, 1, :], lg[:, :, :], AX.X, ALU.add))
                link(dve.reciprocal(small[:, 2, :], small[:, 1, :]))
                link(dve.tensor_tensor(lg[:, :, :], lg[:, :, :], small[:, 2, :].unsqueeze(2).to_broadcast([P, NT, E]),
                                       ALU.mult))
                for t in range(NT):
                    dve.max(best[:, t, :], lg[:, t, :]).then_inc(*vec.next())
                dve.wait_ge(*vec.now())
                dve.tensor_tensor(small[:, 3, :], best[:, :, 1], best[:, :, 0], ALU.subtract)\
                   .then_inc(*vec.next("gap"))
                for t in range(NT):
                    dve.max_index(besti[:, t, :], best[:, t, :], lg[:, t, :]).then_inc(*vec.next())
                dve.wait_ge(*vec.now())
                link(dve.tensor_copy(bestf[:, :, :], besti[:, :, :]))
                dve.wait_ge(*act_done.when("gap_exp"))
                link(dve.tensor_scalar(small[:, 4, :], small[:, 3, :], 1.0, None, ALU.add))
                link(dve.reciprocal(small[:, 4, :], small[:, 4, :]))
                link(dve.tensor_tensor(small[:, 5, :], small[:, 3, :], small[:, 4, :], ALU.mult))
                for k in range(TOP):
                    dve.tensor_tensor(chosen[:, k], expert_no[:, :].unsqueeze(1).to_broadcast([P, NT, E]),
                                      bestf[:, :, k].unsqueeze(2).to_broadcast([P, NT, E]), ALU.is_equal)\
                       .then_inc(*vec.next())
                dve.wait_ge(*vec.now())
                dve.tensor_tensor(chosenb[:, :, :], chosen[:, 0], chosen[:, 1], ALU.add).then_inc(*vec.next("chosen"))
                link(dve.tensor_tensor(comb[:, :, :], chosen[:, 0], small[:, 4, :].unsqueeze(2).to_broadcast([P, NT, E]),
                                       ALU.mult))
                link(dve.tensor_tensor(place[:, :, :], chosen[:, 1], small[:, 5, :].unsqueeze(2).to_broadcast([P, NT, E]),
                                       ALU.mult))
                dve.tensor_tensor(comb[:, :, :], comb[:, :, :], place[:, :, :], ALU.add).then_inc(*vec.next("comb"))
                dve.memset(ends[:, :, :], 0.0).then_inc(*vec.next())
                dve.wait_ge(*a_full.when(("rank",)))
                dve.tensor_copy(rank[:, :, :], a_slot(("rank",))[:, 0:(NT + 1) * E].rearrange("p (t e) -> p t e", e=E))\
                   .then_inc(*a_free.next(("rank",)))
                dve.wait_ge(*a_free.now())
                dve.wait_ge(*vec.now())
                need = ends[:, 0, 4:4 + E]
                link(dve.tensor_scalar(need, rank[:, NT, :], 0.0, None, ALU.is_gt))
                for k in range(1, T // SLOT):
                    link(dve.scalar_tensor_tensor(out=need, in0=rank[:, NT, :], scalar=float(k * SLOT), in1=need,
                                                  op0=ALU.is_gt, op1=ALU.add))
                for i, by in enumerate((1, 2, 4)):
                    link(dve.tensor_tensor(ends[:, i + 1, 4:4 + E], ends[:, i, 4:4 + E],
                                           ends[:, i, 4 - by:4 - by + E], ALU.add))
                link(dve.tensor_tensor(past[:, :, :], ends[0:1, 3, 4:4 + E].unsqueeze(1).to_broadcast([1, SLOTS, E]),
                                       slot_no[:, :].unsqueeze(2).to_broadcast([1, SLOTS, E]), ALU.is_le))
                link(dve.tensor_reduce(slot_ef[:, :], past[:, :, :], AX.X, ALU.add))
                link(dve.tensor_scalar(slot_ef[:, :], slot_ef[:, :], float(E - 1), None, ALU.min))
                dve.tensor_copy(slot_e[:, :], slot_ef[:, :]).then_inc(*vec.next("slot_e"))
                dve.wait_ge(*vec.now())
                link(dve.scalar_tensor_tensor(out=rank[:, 0:NT, :], in0=ends[:, 3, 3:3 + E].unsqueeze(1).to_broadcast([P, NT, E]),
                                              scalar=float(SLOT), in1=rank[:, 0:NT, :], op0=ALU.mult, op1=ALU.add))
                for k in range(TOP):
                    link(dve.tensor_tensor(place[:, :, :], chosen[:, k], rank[:, 0:NT, :], ALU.mult))
                    link(dve.tensor_reduce(placed[:, k, :], place[:, :, :], AX.X, ALU.add))
                dve.tensor_copy(place_no[:, :, :], placed[:, :, :]).then_inc(*vec.next("places"))
                for u in range(B * SE // S):
                    for c in range(DC):
                        split("ca1", "k", u, c)
                def low_x(s):
                    dve.wait_ge(*act_done.when(("slot x", s)))
                    dve.tensor_tensor(slot_x(s % 2, 1), a_slot(("xs", s))[:, 0:DC * SLOT]
                                      .rearrange("p (c t) -> p c t", c=DC), slot_x(s % 2, 0).bitcast(F32),
                                      ALU.subtract).then_inc(*a_free.next(("xs", s)))

                def low_w(kind, s):
                    dve.wait_ge(*act_done.when((kind, s)))
                    w = w1_part if kind == "w1" else w2_part
                    dve.tensor_tensor(w(s % 2, 1), w(s % 2), w(s % 2, 0).bitcast(F32), ALU.subtract)\
                       .then_inc(*vec.next((kind, s)))

                def low_hidden(s):
                    for i in range(FC // PIECE):
                        fs = slice(i * PIECE, (i + 1) * PIECE)
                        dve.wait_ge(*act_done.when(("h", s, i)))
                        dve.tensor_tensor(slot_hid(s % 2, 1)[:, fs, :], slot_gelu[:, fs, :],
                                          slot_hid(s % 2, 0)[:, fs, :].bitcast(F32), ALU.subtract)\
                           .then_inc(*vec.next(("h", s, i)))

                dve.wait_ge(*a_full.when(("combT",)))
                dve.tensor_copy(combT[:, :], a_slot(("combT",))[0:E, :]).then_inc(*a_free.next(("combT",)))
                low_w("w1", 0)
                for b in range(B):
                    key = ("b2", b)
                    dve.wait_ge(*a_full.when(key))
                    if b == 0:
                        dve.wait_ge(*sent_out.when("all"))
                    x = xtok[:, b * TB:(b + 1) * TB, :]
                    dve.tensor_tensor(x, a_slot(key)[:, :].rearrange("p (t d) -> p t d", t=TB), x, ALU.add)\
                       .then_inc(*a_free.next(key))

                low_x(0)
                low_x(1)
                low_w("w1", 1)
                low_hidden(0)
                low_w("w2", 0)
                for s in range(SLOTS):
                    if s + 1 < SLOTS:
                        low_hidden(s + 1)
                    if s + 2 < SLOTS:
                        low_x(s + 2)
                        low_w("w1", s + 2)
                    if s + 1 < SLOTS:
                        low_w("w2", s + 1)
                    key = ("eo", s)
                    dve.wait_ge(*a_full.when(key))
                    if s >= 2:
                        dve.wait_ge(*slot_out[s % 2].when(s - 2))
                    dve.tensor_copy(yS[s % 2], a_slot(key)[:, 0:ST * D].rearrange("p (t d) -> p t d", t=ST))\
                       .then_inc(*a_free.next(key))

            def combine(b):
                for t in range(b * TB, (b + 1) * TB):
                    x = xtok[:, t, :]
                    dve.wait_ge(*back_in[t].when("all"))
                    for k in range(TOP):
                        dve.scalar_tensor_tensor(out=x, in0=back[:, k, t, :], scalar=small[:, 4 + k, t:t + 1], in1=x,
                                                 op0=ALU.mult, op1=ALU.add).then_inc(*vec.next(("combined", b)))
                        dve.wait_ge(*vec.now())

            def low(out, x, high, label):
                dve.tensor_tensor(out, x, high.bitcast(F32), ALU.subtract).then_inc(*vec.next(label))

            def mlp_low_x(name, hf):
                dve.wait_ge(*act_done.when(("x", name, hf)))
                for c in range(DC):
                    low(mlp_x(name, hf, 1)[:, c, :], xT[:, c, hf * S:(hf + 1) * S], mlp_x(name, hf, 0)[:, c, :],
                        ("x", name, hf))

            def mlp_low_w(name, f):
                dve.wait_ge(*act_done.when(("w", name, f)))
                for i in range(2):
                    for c in range(DC):
                        cols = slice(c * FF + f * P, c * FF + (f + 1) * P)
                        low(mlp_low(name, i)[:, cols], mlp_low(name, i, loaded=True)[:, cols],
                            mlp_high(i)[:, cols], ("w", name, f))

            def mlp_low_h(name, hf, f):
                dve.wait_ge(*act_done.when(("h", name, hf, f)))
                low(mlp_h(name, f, 1), hidden[:, f % 2, :], mlp_h(name, f, 0), ("h", name, hf, f))

            def mlp(name):
                for hf in range(B):
                    for f in range(FC):
                        if hf == 0 and f + PREPARED < FC:
                            mlp_low_w(name, f + PREPARED)
                        if hf == 0 and f == 4:
                            mlp_low_x(name, 1)
                        key = ("u", name, hf, f)
                        dve.wait_ge(*a_full.when(key))
                        dve.wait_ge(*b_free.when(("g", name, hf, f)))
                        if f >= 2:
                            dve.wait_ge(*vec.when(("h", name, hf, f - 2)))
                        dve.tensor_tensor(hidden[:, f % 2, :], a_slot(key)[:, 0:S], gate[:, f % 2, :], ALU.mult)\
                           .then_inc(*a_free.next(key))
                        if f:
                            mlp_low_h(name, hf, f - 1)
                    mlp_low_h(name, hf, FC - 1)
                    key = ("down", name, hf)
                    dve.wait_ge(*a_full.when(key))
                    x = xT[:, :, hf * S:(hf + 1) * S]
                    dve.tensor_tensor(x, a_slot(key)[:, :].rearrange("p (c t) -> p c t", c=DC), x, ALU.add)\
                       .then_inc(*a_free.next(key))

            dve.wait_ge(*pool_done.when("constants"))
            for step in STEPS:
                kind = step[0]
                if kind == "turn_x":
                    copy_T(step, xT[:, :, step[1] * S:(step[1] + 1) * S])
                elif kind == "split":
                    (split_in_place if ATTENTIONS[step[1]].layer else split)(*step[1:])
                elif kind == "v":
                    values(*step[1:])
                elif kind == "max":
                    maxima(step)
                elif kind == "parts":
                    max_parts(step)
                elif kind == "sum":
                    denominators(step)
                elif kind == "norm":
                    normalise(step)
                elif kind == "heads":
                    copy_T(step, oT[:, :, :])
                elif kind == "proj":
                    residual(step)
                elif kind == "stats":
                    if step[1] != "moe":
                        dve.wait_ge(*a_free.when(("proj",) + step[1:]))
                    statistics(*step[1:])
                elif kind == "gain" and step[1:] not in GAIN_BY_POOL:
                    gain_and_bias(*step[1:])
                elif kind == "turn":
                    turned(step)
                elif kind == "route":
                    logits(step)
                elif kind == "moe":
                    experts_step()
                elif kind == "combine":
                    combine(step[1])
                elif kind == "prepare":
                    mlp_low_x(step[1], 0)
                    for f in range(PREPARED):
                        mlp_low_w(step[1], f)
                elif kind == "mlp":
                    dve.wait_ge(*a_free.now())
                    mlp(step[1])
                    dve.wait_ge(*a_free.now())
                elif kind == "out":
                    for b in range(B):
                        key = ("out", b)
                        dve.wait_ge(*a_full.when(key))
                        dve.tensor_copy(xtok[:, b * TB:(b + 1) * TB, :],
                                        a_slot(key)[:, :].rearrange("p (t d) -> p t d", t=TB))\
                           .then_inc(*a_free.next(key))

        @block.scalar
        def _(act):
            def high_part(name, which, u, c):
                key = ("split", name, which, u, c)
                i = SPLIT_NO[name, which, u, c]
                act.wait_ge(*a_full.when(key))
                if i >= 2:
                    act.wait_ge(*part_out[i % 2].when(i - 2))
                if ATTENTIONS[name].layer:
                    act.activation(parts_r[:, i % 2, 0, :], a_slot(key)[:, 0:S], ACT.Identity)\
                       .then_inc(*act_done.next(("high", i)))
                else:
                    if i == 0:
                        act.wait_ge(*load["bias"].when("all"))
                    act.activation(parts[:, i % 2, 0, :], a_slot(key)[:, 0:S], ACT.Identity,
                                   bias=biasT[name[:2] + "_b" + which][:, c:c + 1])\
                       .then_inc(*act_done.next(("high", i)))

            def high_in_place(name, which, u, c):
                a = ATTENTIONS[name]
                key = ("split", name, which, u, c)
                act.wait_ge(*a_full.when(key))
                for h in range(DC * c, DC * c + 2):
                    at = h % 2 * 64
                    if which == "q":
                        places = q_stack(a, u)[at:at + 64, h, :], q_stack(a, u, 1)[0:64, h, :]
                    else:
                        places = k_stack(a, u)[at:at + 64, h, :], k_stack(a, u)[64 - at:128 - at, h, :]
                    for place in places:
                        act.activation(place, a_slot(key)[at:at + 64, 0:S], ACT.Identity)\
                           .then_inc(*act_done.next(key))

            def shift_rows(step):
                _, name, b, g = step
                act.wait_ge(*b_full.when(step))
                if before(name, b, g):
                    act.wait_ge(*shift_in[(GROUP_NO[name, b, g] - 1) % 2].when(before(name, b, g)))
                rows = shift_r if ATTENTIONS[name].layer else shift_parts
                act.activation(rows[:, :], b_slot(step)[0:4 if ATTENTIONS[name].layer else 12, :], ACT.Identity)\
                   .then_inc(*b_free.next(step))

            def exp(step):
                _, name, b, g, kt, j, n = step
                a = ATTENTIONS[name]
                seg, ring = SEGMENT[name], RING[a.layer]
                key = ("unit", seg, n)
                w = (S - a.queries_from(kt)) * a.together(kt)
                act.wait_ge(*b_full.when(key))
                if n >= ring:
                    act.wait_ge(*pv_done.when((seg, n - ring)))
                    if a.layer:
                        m = n - ring + (a.G if UNITS[seg][n - ring][3] == 0 else 0)
                        act.wait_ge(*vec.when(("sum", seg, m)))
                act.activation(prob_bufs[n % ring][:, 0:w], b_slot(key)[:, 0:w], ACT.Exp, scale=a.scale)\
                   .then_inc(*b_free.next(key))

            def centre(step):
                _, name, b = step
                act.wait_ge(*pool_done.when(("rstd", name, b)))
                for t in range(TB):
                    x = xtok[:, b * TB + t, :]
                    act.activation(x, x, ACT.Identity, scale=rstd[:, t:t + 1], bias=offset[:, t:t + 1])\
                       .then_inc(*act_done.next(step))

            def evict(step):
                _, name, b, g = step
                a = ATTENTIONS[name]
                act.wait_ge(*pv_done.when((SEGMENT[name], LAST_UNIT[name, b, g][-1])))
                if before(name, b, g):
                    act.wait_ge(*a_full.when(("norm",) + before(name, b, g)))
                act.activation(sums[:, :], o_bank[GROUP_NO[name, b, g] % 2][:, :], ACT.Identity)\
                   .then_inc(*act_done.next(step))

            def experts_step():
                act.wait_ge(*vec.when("logits"))
                act.activation(lg[:, :, :], lg[:, :, :], ACT.Exp).then_inc(*act_done.next("router_exp"))
                act.wait_ge(*vec.when("gap"))
                act.activation(small[:, 3, :], small[:, 3, :], ACT.Exp).then_inc(*act_done.next("gap_exp"))
                for u in range(B * SE // S):
                    for c in range(DC):
                        high_part("ca1", "k", u, c)

                def high_x(s):
                    act.wait_ge(*a_full.when(("xs", s)))
                    if s == 0:
                        for i in range(2):
                            act.wait_ge(*part_out[i].when(len(SPLITS) - 2 + i))
                    act.activation(slot_x(s % 2, 0), a_slot(("xs", s))[:, 0:DC * SLOT]
                                   .rearrange("p (c t) -> p c t", c=DC), ACT.Identity)\
                       .then_inc(*act_done.next(("slot x", s)))

                def high_w(kind, s):
                    if kind == "w1":
                        w, loaded = w1_part, w1_load
                    else:
                        w, loaded = w2_part, w2_load
                        if s >= 2:
                            act.wait_ge(*a_full.when(("eo", s - 2)))
                    act.wait_ge(*loaded[s % 2].when(s))
                    act.activation(w(s % 2, 0), w(s % 2), ACT.Identity).then_inc(*act_done.next((kind, s)))

                def gelus(s):
                    act.wait_ge(*b1_load[s % 2].when(s))
                    for f in range(FC):
                        key = ("h", s, f)
                        act.wait_ge(*b_full.when(key))
                        if s >= 1 and f % PIECE == 0:
                            act.wait_ge(*vec.when(("h", s - 1, f // PIECE)))
                        act.activation(slot_gelu[:, f, :], b_slot(key)[:, 0:SLOT], ACT.Gelu,
                                       bias=b1S[s % 2][:, f:f + 1]).then_inc(*b_free.next(key))
                        if f % PIECE == PIECE - 1:
                            if f == PIECE - 1 and s >= 2:
                                act.wait_ge(*a_full.when(("eo", s - 2)))
                            fs = slice(f + 1 - PIECE, f + 1)
                            act.wait_ge(*b_free.now())
                            act.activation(slot_hid(s % 2, 0)[:, fs, :], slot_gelu[:, fs, :], ACT.Identity)\
                               .then_inc(*act_done.next(("h", s, f // PIECE)))

                high_w("w1", 0)
                high_x(0)
                high_x(1)
                high_w("w1", 1)
                gelus(0)
                high_w("w2", 0)
                for s in range(SLOTS):
                    if s + 1 < SLOTS:
                        gelus(s + 1)
                    if s + 2 < SLOTS:
                        high_x(s + 2)
                        high_w("w1", s + 2)
                    if s + 1 < SLOTS:
                        high_w("w2", s + 1)

            def mlp_high_x(name, hf):
                act.wait_ge(*a_free.when(("proj", name, hf)))
                for c in range(DC):
                    act.activation(mlp_x(name, hf, 0)[:, c, :], xT[:, c, hf * S:(hf + 1) * S], ACT.Identity)\
                       .then_inc(*act_done.next(("x", name, hf)))

            def mlp_high_w(name, f):
                for i in range(2):
                    for c in range(DC):
                        cols = slice(c * FF + f * P, c * FF + (f + 1) * P)
                        act.activation(mlp_high(i)[:, cols], mlp_low(name, i, loaded=True)[:, cols], ACT.Identity)\
                           .then_inc(*act_done.next(("w", name, f)))

            def mlp_high_h(name, hf, f):
                act.wait_ge(*a_free.when(("u", name, hf, f)))
                act.activation(mlp_h(name, f, 0), hidden[:, f % 2, :], ACT.Identity)\
                   .then_inc(*act_done.next(("h", name, hf, f)))

            def prepare(name):
                a = ATTENTIONS[name]
                act.wait_ge(*b_full.when(("unit", SEGMENT[name], LAST_UNIT[name, 0, a.H // a.G - 1][-1])))
                act.wait_ge(*load["mlp_" + name].when("all"))
                mlp_high_x(name, 0)
                for f in range(PREPARED):
                    mlp_high_w(name, f)

            def mlp(name):
                act.wait_ge(*a_full.when(("proj", name, B - 1)))
                for hf in range(B):
                    for f in range(FC):
                        if hf == 0 and f + PREPARED < FC:
                            mlp_high_w(name, f + PREPARED)
                        if hf == 0 and f == 4:
                            mlp_high_x(name, 1)
                        key = ("g", name, hf, f)
                        act.wait_ge(*b_full.when(key))
                        n = hf * FC + f
                        if n >= 2:
                            act.wait_ge(*a_free.when(("u", name, (n - 2) // FC, (n - 2) % FC)))
                        act.activation(gate[:, f % 2, :], b_slot(key)[:, :], ACT.Silu).then_inc(*b_free.next(key))
                        if f:
                            mlp_high_h(name, hf, f - 1)
                    mlp_high_h(name, hf, FC - 1)

            for step in STEPS:
                kind = step[0]
                if kind == "turn_ctx":
                    for c in range(DC):
                        key = ("ctx", step[1], c)
                        act.wait_ge(*b_full.when(key))
                        act.activation(ctxT[:, c, step[1] * S:(step[1] + 1) * S], b_slot(key)[:, :], ACT.Identity)\
                           .then_inc(*b_free.next(key))
                elif kind == "split":
                    (high_in_place if ATTENTIONS[step[1]].layer else high_part)(*step[1:])
                elif kind == "unit":
                    exp(step)
                elif kind == "shift":
                    shift_rows(step)
                elif kind == "evict":
                    evict(step)
                elif kind == "centre":
                    centre(step)
                elif kind == "moe":
                    experts_step()
                elif kind == "prepare":
                    prepare(step[1])
                elif kind == "mlp":
                    mlp(step[1])

        @block.gpsimd
        def _(pool):
            for t, v in ((ident, 0.0), (identb, 0.0), (mask_q, 0.0), (mask_k, 0.0)):
                pool.memset(t[:, :], v).then_inc(*pool_done.next())
            pool.memset(onesb[:, :], 1.0).then_inc(*pool_done.next())
            pool.memset(onesf[:, :], 1.0).then_inc(*pool_done.next())
            pool.memset(minus_half[:, :], -0.5).then_inc(*pool_done.next())
            pool.iota(expert_no[:, :], pattern=[[1, E]], base=0, channel_multiplier=0,
                      allow_small_or_imprecise_dtypes=True).then_inc(*pool_done.next())
            pool.wait_ge(*pool_done.now())
            for m in (ident, identb):
                pool.affine_select(out=m[:, :], in_=m[:, :], compare_op=ALU.not_equal, fill=1.0, base=0,
                                   pattern=[[-1, P]], channel_multiplier=1).then_inc(*pool_done.next())
            pool.affine_select(out=mask_q[:, :], in_=mask_q[:, :], compare_op=ALU.is_ge, fill=NEG, base=0,
                               pattern=[[-1, P]], channel_multiplier=1).then_inc(*pool_done.next())
            pool.affine_select(out=mask_k[:, :], in_=mask_k[:, :], compare_op=ALU.is_ge, fill=NEG, base=0,
                               pattern=[[1, P]], channel_multiplier=-1).then_inc(*pool_done.next())
            pool.memset(vx[:, :], 1.0).then_inc(*pool_done.next("constants"))
            pool.memset(below[:, :], 1.0).then_inc(*pool_done.next())
            pool.wait_ge(*pool_done.now())
            pool.affine_select(out=below[:, :], in_=below[:, :], compare_op=ALU.is_ge, fill=0.0, base=-1,
                               pattern=[[1, P]], channel_multiplier=-1).then_inc(*pool_done.next())
            pool.iota(slot_no[:, :], pattern=[[1, SLOTS]], base=0, channel_multiplier=0,
                      allow_small_or_imprecise_dtypes=True).then_inc(*pool_done.next("router_constants"))
            def add_bo(name, b):
                pool.wait_ge(*pool_done.now())
                x = xtok[:, b * TB:(b + 1) * TB, :]
                pool.tensor_tensor(x, x, row[name[:2] + "_bo"].unsqueeze(1).to_broadcast([P, TB, D]), ALU.add)\
                    .then_inc(*pool_done.next(("bo", name, b)))

            pool.wait_ge(*pool_done.now())
            pool.memset(arena[96:99, 32768:49152], 1.0).then_inc(*pool_done.next(("shift_ones", "sa0")))
            pool.wait_ge(*load["bias"].when("all"))
            for b in range(B):
                pool.wait_ge(*a_full.when(("turn_x", b)))
                add_bo("sa0", b)
            pool.wait_ge(*b_full.when(("ctx", B * SE // S - 1, DC - 1)))
            pool.wait_ge(*pool_done.now())
            pool.memset(arena[96:99, 16384:32768], 1.0).then_inc(*pool_done.next(("shift_ones", "ca0")))

            def power(name, b):
                pool.wait_ge(*pool_done.now())
                pool.wait_ge(*vec.when(("stats", name, b)))
                if centred:
                    pool.wait_ge(*act_done.when(("centre",) + centred[-1]))
                centred.append((name, b))
                pool.tensor_tensor(rstd[:, :], var[:, :], minus_half[:, :], ALU.pow).then_inc(*pool_done.next())
                pool.wait_ge(*pool_done.now())
                pool.tensor_tensor(offset[:, :], negmean[:, :], rstd[:, :], ALU.mult)\
                    .then_inc(*pool_done.next(("rstd", name, b)))

            centred = []

            def gain_and_bias(name, b):
                pool.wait_ge(*a_full.when(("turn", name, b)))
                x = xtok[:, b * TB:(b + 1) * TB, :]
                for kind, op in (("_g", ALU.mult), ("_b", ALU.add)):
                    pool.wait_ge(*pool_done.now())
                    pool.tensor_tensor(x, x, row[LN_OF[name] + kind].unsqueeze(1).to_broadcast([P, TB, D]), op)\
                        .then_inc(*pool_done.next(("ln", name, b)))

            def lower_parts(name, which, u, c):
                i = SPLIT_NO[name, which, u, c]
                part = parts[:, i % 2]
                pool.wait_ge(*pool_done.now())
                pool.wait_ge(*a_free.when(("split", name, which, u, c)))
                pool.tensor_copy(part[:, 1, :], rest[:, :]).then_inc(*pool_done.next())
                pool.wait_ge(*pool_done.now())
                pool.tensor_tensor(part[:, 2, :], rest[:, :], part[:, 1, :], ALU.subtract)\
                    .then_inc(*pool_done.next(("split", i)))

            def shift_rows(name, b):
                a = ATTENTIONS[name]
                for value, at, n in ((1.0, {"sa1": 18432 + b * 4096, "ca1": 20480 - b * 8192}[name], a.H * a.nk),
                                     (0.0, 2048 + b * 4096, a.H * S)):
                    pool.wait_ge(*pool_done.now())
                    pool.memset(arena_r[64:66, at:at + n].bitcast(F32), value)\
                        .then_inc(*pool_done.next(("rows", name, b)))

            def down_parts(name):
                high, w = mlp_high(2), mlp_low(name, 2, loaded=True)
                pool.wait_ge(*a_full.when(("proj", name, B - 1)))
                pool.wait_ge(*load["mlp_" + name].when("all"))
                pool.wait_ge(*pool_done.now())
                pool.tensor_copy(high, w).then_inc(*pool_done.next())
                pool.wait_ge(*pool_done.now())
                pool.tensor_tensor(mlp_low(name, 2), w, high.bitcast(F32), ALU.subtract)\
                    .then_inc(*pool_done.next(("wd", name)))

            def experts_step():
                pool.wait_ge(*vec.when("places"))
                pool.wait_ge(*filled.when("all"))
                for t in range(NT):
                    for k in range(TOP):
                        pool.indirect_dma_start(sent, IndirectOffsetOnAxis(ap=place_no[:, k, t:t + 1], axis=0),
                                                xtok[:, t, :], None).then_inc(*sent_out.next("all", 16))
                for s in range(SLOTS - 2, SLOTS):
                    pool.wait_ge(*slot_out[s % 2].when(s))
                for t in range(NT):
                    for k in range(TOP):
                        pool.indirect_dma_start(back[:, k, t, :], None, computed,
                                                IndirectOffsetOnAxis(ap=place_no[:, k, t:t + 1], axis=0))\
                            .then_inc(*back_in[t].next("all", 16))

            for step in STEPS:
                kind = step[0]
                if kind == "stats":
                    power(*step[1:])
                    if step[1] == "moe":
                        shift_rows("sa1", step[2])
                elif kind == "gain" and step[1:] in GAIN_BY_POOL:
                    gain_and_bias(*step[1:])
                    if step[1] == "sa0":
                        add_bo("ca0", step[2])
                elif kind == "split" and step[1] == "ca0":
                    lower_parts(*step[1:])
                elif kind == "moe":
                    experts_step()
                elif kind == "mlp":
                    down_parts(step[1])
                    if step[1] == "sa1":
                        pool.wait_ge(*a_full.when(("down", "sa1", B - 1)))
                        for b in range(B):
                            shift_rows("ca1", b)

        @block.sync
        def _(sp):
            L0 = "L0_xattn_"

            def as_words(x):
                return x[:, :, :].bitcast(F32) if x.dtype == F32R else x

            def loads(name, pairs):
                for dst, src in pairs:
                    sp.dma_start(dst, src).then_inc(*load[name].next("all", 16))

            def weights(name):
                pre = "L%s_xattn_%s_w" % (name[2], name[:2])
                i = ATT_NO[name]
                loads("w" + name, [(wset[i % 2][:, n], io[pre + c].rearrange("(c p) n -> p c n", p=P))
                                   for n, c in enumerate("qkvo")])

            def mlp_weights(name):
                pre = "L1_xattn_" + name[:2] + "mlp_w"
                loads("mlp_" + name, [
                    (mlp_low(name, i, loaded=True).rearrange("p (c f) -> p c f", c=c),
                     io[pre + x].rearrange("(c p) f -> p c f", p=P)) for i, (x, c) in enumerate((("g", DC), ("u", DC), ("d", FC)))])

            def store_parts(name, which, u, c):
                i = SPLIT_NO[name, which, u, c]
                cols = (slice(None), slice(c * P, (c + 1) * P), slice(u * S, (u + 1) * S))
                if ATTENTIONS[name].layer:
                    sp.wait_ge(*a_free.when(("split", name, which, u, c)))
                    scr, src = scratch_kr, as_words(parts_r[:, i % 2])
                else:
                    sp.wait_ge(*(pool_done if name == "ca0" else vec).when(("split", i)))
                    scr, src = (scratch_q if which == "q" else scratch_k)[ATT_NO[name]], parts[:, i % 2]
                sp.dma_start(scr[cols].rearrange("r p t -> p r t"), src).then_inc(*part_out[i % 2].next(i, 16))

            def last_unit(name, b):
                a = ATTENTIONS[name]
                return b_full.when(("unit", SEGMENT[name], LAST_UNIT[name, b, a.H // a.G - 1][-1]))

            def stack(name, which, u, c):
                a = ATTENTIONS[name]
                if name == "ca0" and which == "q":
                    sp.wait_ge(*last_unit("sa0", u))
                elif name == "ca0" and u == 0:
                    sp.wait_ge(*pool_done.when(("shift_ones", "ca0")))
                elif name == "ca0" and u == 2:
                    sp.wait_ge(*last_unit("sa0", B - 1))
                elif name == "ca1" and which == "k" and u == 0:
                    sp.wait_ge(*a_full.when(("down", "sa1", B - 1)))
                i = SPLIT_NO[name, which, u, c]
                sp.wait_ge(*part_out[i % 2].when(i))
                per = a.nk // S if which == "k" else 1
                b, t0 = u // per, (u % per) * S
                at = (q_stack if which == "q" else k_stack)
                if a.layer:
                    scr, places = scratch_kr, KEY_PARTS_R
                else:
                    scr = (scratch_q if which == "q" else scratch_k)[ATT_NO[name]]
                    places = [(part, 0, r * 16) for r, part in enumerate(QUERY_PARTS if which == "q" else KEY_PARTS)]
                for part, i, r in places:
                    src = scr[part, c * P:(c + 1) * P, u * S:(u + 1) * S].rearrange("(h d) t -> d h t", d=a.HD)
                    dst = at(a, b, i)[r:r + a.HD, c * P // a.HD:(c + 1) * P // a.HD, t0:t0 + S]
                    sp.dma_start(as_words(dst), src).then_inc(*stack_in[name, b, c].next("all", 16))

            def shift_store(step):
                _, name, b, g = step
                a = ATTENTIONS[name]
                sp.wait_ge(*b_free.when(step))
                if a.layer:
                    rows, first, src = as_words(q_stack(a, b, 1)), 64, shift_r[:, :].bitcast(F32)
                else:
                    rows, first, src = q_stack(a, b), 96, shift_parts[:, :]
                for r in range(2 if a.layer else 3):
                    sp.dma_start(rows[first + r:first + r + 1, g * a.G:(g + 1) * a.G, :], src[r * a.G:(r + 1) * a.G, :])\
                      .then_inc(*shift_in[GROUP_NO[name, b, g] % 2].next((name, b, g), 16))

            def experts_step():

                def store_results(s):
                    sp.wait_ge(*a_free.when(("eo", s)))
                    sp.dma_start(computed[s * SLOT:(s + 1) * SLOT, :].rearrange("(t p) d -> p t d", p=P), yS[s % 2])\
                      .then_inc(*slot_out[s % 2].next(s, 16))

                def first_weights(s):
                    if s >= 2:
                        sp.wait_ge(*b_full.when(("h", s - 2, FC - 1)))
                        sp.wait_ge(*b_free.when(("h", s - 2, FC - 1)))
                    experts[s] = sp.value_load(slot_e[0:1, s:s + 1], min_val=0, max_val=E - 1)
                    e = experts[s]
                    sp.dma_start(w1_part(s % 2).rearrange("p (c f) -> p c f", c=DC),
                                 io[L0 + "e_w1"][DynSlice(e, 1)].rearrange("e (c p) f -> p (e c) f", p=P))\
                      .then_inc(*w1_load[s % 2].next(s, 16))
                    sp.dma_start(b1S[s % 2], b1T[:, DynSlice(e, 1), :].rearrange("p e f -> p (e f)"))\
                      .then_inc(*b1_load[s % 2].next(s, 16))

                def second_weights(s):
                    if s >= 2:
                        sp.wait_ge(*a_full.when(("eo", s - 2)))
                    sp.dma_start(w2_part(s % 2).rearrange("p (c n) -> p c n", c=FC), io[L0 + "e_w2"][DynSlice(experts[s], 1)]
                                 .rearrange("e (f p) n -> p (e f) n", p=P)).then_inc(*w2_load[s % 2].next(s, 16))

                def slot_tokens(s):
                    if s >= 2:
                        sp.wait_ge(*a_full.when(("xs", s - 2)))
                    sp.dma_start(xS[s % 2], sent[s * SLOT:(s + 1) * SLOT, :].rearrange("(t p) d -> p t d", p=P))\
                      .then_inc(*slot_in[s % 2].next(s, 16))

                experts = {}
                sp.wait_ge(*vec.when("slot_e"))
                first_weights(0)
                for u in range(B * SE // S):
                    for c in range(DC):
                        store_parts("ca1", "k", u, c)
                first_weights(1)
                second_weights(0)
                sp.wait_ge(*sent_out.when("all"))
                slot_tokens(0)
                slot_tokens(1)
                for s in range(1, SLOTS):
                    if s + 1 < SLOTS:
                        slot_tokens(s + 1) if s + 1 >= 2 else None
                        first_weights(s + 1)
                    second_weights(s)
                    if s >= 2:
                        store_results(s - 2)
                store_results(SLOTS - 2)
                store_results(SLOTS - 1)

            loads("x0", [(xtok[:, 0:TB, :], io["x"][0].rearrange("(t p) d -> p t d", p=P))])
            weights("sa0")
            with nc.allow_non_contiguous_dma(reason="biases onto the partitions, a few kilobytes"):
                loads("bias", [(biasT[n][:, :], io[L0 + n].rearrange("(c p) -> p c", p=P)) for n in biasT])
            loads("bias", [(row[n], io[L0 + n].partition_broadcast(P)) for n in ("sa_bv", "sa_bo")])
            loads("x1", [(xtok[:, TB:NT, :], io["x"][1].rearrange("(t p) d -> p t d", p=P))])
            for step in STEPS:
                kind = step[0]
                if kind == "split":
                    if not ATTENTIONS[step[1]].layer:
                        store_parts(*step[1:])
                elif kind == "fill":
                    rows = slice(step[1] * SLOT, (step[1] + 1) * SLOT)
                    tokens = io["ctx_1024"].rearrange("b s d -> (b s) d")
                    sp.dma_start(sent[rows, :], tokens[0:SLOT, :]).then_inc(*filled.next("all", 16))
                elif step in (("load", "ctx0"), ("load", "ctx1")):
                    b = int(step[1][-1])
                    loads(step[1], [(ctx_in[:, b * 8:(b + 1) * 8, :],
                                     io["ctx_1024"][b].rearrange("(t p) d -> p t d", p=P))])
                elif step == ("load", "rows"):
                    loads("rows", [(row[n], io[L0 + n].partition_broadcast(P)) for n in row_names[2:]]
                          + [(rb[:, :], io[L0 + "router_b"].partition_broadcast(P)),
                             (rw[:, :, :], io[L0 + "router_w"].rearrange("(c p) n -> p c n", p=P))])
                    with nc.allow_non_contiguous_dma(reason="biases onto the partitions, a few kilobytes"):
                        loads("rows", [(gainT[ln][:, i, :], io[L0 + ln + x].rearrange("(c p) -> p c", p=P))
                                       for ln in gainT for i, x in enumerate(("_g", "_b"))])
                        loads("rows", [(b1T[:, :, :], io[L0 + "e_b1"].rearrange("e (f p) -> p e f", p=P))])
                elif step == ("load", "wca0"):
                    weights("ca0")
                elif kind == "stack":
                    stack(*step[1:])
                elif kind == "shift":
                    shift_store(step)
                elif step == ("load", "wsa1"):
                    sp.wait_ge(*a_free.when(("proj", "sa0", B - 1)))
                    weights("sa1")
                elif step == ("load", "wca1"):
                    sp.wait_ge(*a_free.when(("proj", "ca0", B - 1)))
                    weights("ca1")
                    loads("b2", [(b2[:, :], io[L0 + "e_b2"])])
                elif step == ("load", "mlp_sa1"):
                    mlp_weights("sa1")
                elif step == ("load", "mlp_ca1"):
                    sp.wait_ge(*last_unit("ca1", 0))
                    mlp_weights("ca1")
                elif kind == "moe":
                    experts_step()
                elif kind == "out":
                    for b in range(B):
                        sp.wait_ge(*a_free.when(("out", b)))
                        sp.dma_start(io["out"][b].rearrange("(t p) d -> p t d", p=P),
                                     xtok[:, b * TB:(b + 1) * TB, :]).then_inc(*stored.next("out", 16))
            sp.wait_ge(*stored.now())

    seen = {n: s.seen for n, s in signals.items()}
    seen["_a_turn"] = {k: i % 2 for i, k in enumerate(a_keys)}
    seen["_b_turn"] = {k: i % 2 for i, k in enumerate(b_keys)}
    return seen


def kernel(**inputs):
    import numpy as _np
    import concourse.bacc as _bacc
    from concourse import mybir as _mybir
    from concourse.bass_utils import run_bass_kernel_spmd as _run

    arrays = {f"in_{name}": _np.ascontiguousarray(a) for name, a in inputs.items()}

    def build(known):
        nc = _bacc.Bacc("TRN2", target_bir_lowering=False, num_devices=1)
        io = {name[3:]: nc.dram_tensor(name, a.shape, _mybir.dt.from_np(a.dtype), kind="ExternalInput").ap()
              for name, a in arrays.items()}
        io["out"] = nc.dram_tensor("out", (B, S, D), F32, kind="ExternalOutput").ap()
        return nc, program(nc, io, known)

    _, known = build(None)
    nc, _ = build(known)
    r = _run(nc, [arrays], core_ids=[0])
    return r.results[0]["out"]
```
